# Optimizing a Trainium2 kernel written in Bass

```python
import numpy as np
import jax
import jax.numpy as jnp

def _softmax(x, axis=-1):
    return jax.nn.softmax(x, axis=axis)

def _gelu(x):
    return jax.nn.gelu(x, approximate=True)

def _silu(x):
    return jax.nn.silu(x)

def _sigmoid(x):
    return jax.nn.sigmoid(x)

def _layernorm(x, axis=-1, eps=1e-05):
    m = jnp.mean(x, axis=axis, keepdims=True)
    v = jnp.var(x, axis=axis, keepdims=True)
    return (x - m) / jnp.sqrt(v + eps)

def _scatter_add(tgt, idx, src, axis=0):
    return tgt.at[idx].add(src)

def _segment_sum(src, seg, n):
    return jax.ops.segment_sum(src, seg, n)
kernel_name = 'mk_adaln_attn_ffn_d4_seqx_r8_b33b12'

def setup_inputs(seed: int=0):
    np.random.seed(seed)
    _w = jnp.asarray

    def _rec_inputs():
        import jax
        import jax.numpy as jnp
        _rk = jax.random.key(seed)
        x = -0.000125 + 0.9999 * jax.random.normal(jax.random.fold_in(_rk, 1), (4, 256, 256), jnp.float32)
        _lenS = 256 - jax.random.randint(jax.random.fold_in(_rk, 7), (4,), 0, max(1, 256 // 4) + 1, jnp.int32)
        _lenS2 = 256 - jax.random.randint(jax.random.fold_in(_rk, 8), (4,), 0, max(1, 256 // 4) + 1, jnp.int32)
        fside_BxSxS_0 = -1.52775e-05 + 0.999936 * jax.random.normal(jax.random.fold_in(_rk, 11), (4, 256, 256), jnp.float32)
        cond_512 = -5.03954e-05 + 1.00559 * jax.random.normal(jax.random.fold_in(_rk, 12), (4, 64), jnp.float32)
        return (x, fside_BxSxS_0, cond_512)
    x, fside_BxSxS_0, cond_512 = _rec_inputs()

    def _L0_cond_setup():
        import jax, jax.numpy as jnp
        from jax import lax
        import numpy as np
        B, T, C, TD = (8, 256, 256, 64)

        def _bi_wkv(r, k, v, w, u, time_emb):
            tf = jax.nn.sigmoid(jnp.sum(time_emb, axis=-1))[:, None, None]
            decay = jnp.exp(-jnp.exp(w.astype(jnp.float32)))[None, :] * (0.5 + 0.5 * tf[:, :, 0])
            kf = k.astype(jnp.float32)
            vf = v.astype(jnp.float32)
            ek = jnp.exp(jnp.minimum(kf, 30.0))
            ekv = ek * vf

            def step(carry, x):
                a, b = carry
                ekv_t, ek_t = x
                a = a * decay + ekv_t
                b = b * decay + ek_t
                return ((a, b), (a, b))
            ekv_t = jnp.swapaxes(ekv, 0, 1)
            ek_t = jnp.swapaxes(ek, 0, 1)
            init = (jnp.zeros_like(decay), jnp.zeros_like(decay))
            _, (nf, df) = lax.scan(step, init, (ekv_t, ek_t))
            _, (nb, db) = lax.scan(step, init, (ekv_t, ek_t), reverse=True)
            nf = jnp.swapaxes(nf, 0, 1)
            df = jnp.swapaxes(df, 0, 1)
            nb = jnp.swapaxes(nb, 0, 1)
            db = jnp.swapaxes(db, 0, 1)
            euk = jnp.exp(jnp.minimum(u.astype(jnp.float32)[None, None, :] + kf, 30.0))
            num = nf + nb - ekv + euk * vf
            den = df + db - ek + euk
            base = jax.nn.sigmoid(r.astype(jnp.float32)) * (num / jnp.maximum(den, 1e-08))
            out = base * (0.8 + 0.2 * tf)
            return out.astype(r.dtype)
        key = jax.random.key(seed)
        ks = jax.random.split(key, 6)
        return {'r': jax.random.normal(ks[0], (B, T, C), dtype=jnp.float32), 'k': jax.random.normal(ks[1], (B, T, C), dtype=jnp.float32), 'v': jax.random.normal(ks[2], (B, T, C), dtype=jnp.float32), 'w': jax.random.normal(ks[3], (C,), dtype=jnp.float32), 'u': jax.random.normal(ks[4], (C,), dtype=jnp.float32), 'time_emb': jax.random.normal(ks[5], (B, TD), dtype=jnp.float32)}
    _L0_cond_all = _L0_cond_setup()
    _L0_cond_in = {k: v for k, v in _L0_cond_all.items() if k in ('w', 'u')}
    del _L0_cond_all

    def _L0_attn_setup():
        import jax, jax.numpy as jnp
        import numpy as np
        DIM = 256
        HEADS = 16
        HEAD_DIM = DIM // HEADS
        CHUNK = 128
        B, N = (4, 256)

        def _rmsnorm(x, w, eps):
            return x * jax.lax.rsqrt(jnp.mean(x * x, axis=-1, keepdims=True) + eps) * w

        def _weight_quant(w):
            scale = 1.0 / jnp.clip(jnp.mean(jnp.abs(w)), 1e-05, None)
            q = jnp.clip(jnp.round(w * scale), -1.0, 1.0) / scale
            return w + jax.lax.stop_gradient(q - w)

        def _forward(x, qkv_w, qkv_norm_w, proj_w, proj_norm_w, norm_w, s):
            Bb, Nn, C = x.shape
            H, D, T = (HEADS, HEAD_DIM, CHUNK)
            nc = Nn // T
            eps = jnp.finfo(x.dtype).eps
            scale = D ** (-0.5)
            h = _rmsnorm(x, qkv_norm_w, eps)
            qkv = h @ _weight_quant(qkv_w).T
            qkv = qkv.reshape(Bb, Nn, 3, H, D)
            q, k, v = (qkv[:, :, 0], qkv[:, :, 1], qkv[:, :, 2])

            def chunks(t):
                return t.reshape(Bb, nc, T, H, D).transpose(1, 0, 3, 2, 4)
            qc, kc, vc = (chunks(q), chunks(k), chunks(v))
            tt = jnp.arange(T, dtype=x.dtype)
            lam_t = jnp.exp(-s[:, None] * tt)
            lam_rev = jnp.exp(-s[:, None] * (T - tt))
            diff = tt[:, None] - tt[None, :]
            mask = jnp.where(diff >= 0, jnp.exp(-s[:, None, None] * diff), 0.0)
            lam_T = jnp.exp(-s * T)[:, None, None]

            def step(S, qkv_c):
                qi, ki, vi = qkv_c
                scores = jnp.einsum('bhtd,bhsd,hts->bhts', qi, ki, mask)
                intra = jnp.einsum('bhts,bhsd->bhtd', scores, vi)
                cross = jnp.einsum('bhtd,ht,bhde->bhte', qi, lam_t, S)
                o = scale * (intra + cross)
                kv = jnp.einsum('bhtd,ht,bhte->bhde', ki, lam_rev, vi)
                return (lam_T * S + kv, o)
            S0 = jnp.zeros((Bb, H, D, D), x.dtype)
            _, outs = jax.lax.scan(step, S0, (qc, kc, vc))
            out = outs.transpose(1, 0, 3, 2, 4).reshape(Bb, Nn, C)
            out = _rmsnorm(out, norm_w, 1e-06)
            out = _rmsnorm(out, proj_norm_w, eps) @ _weight_quant(proj_w).T
            return out
        key = jax.random.key(seed)
        ks = jax.random.split(key, 3)
        x = jax.random.normal(ks[0], (B, N, DIM), jnp.float32)
        bound = float(1.0 / np.sqrt(DIM))
        qkv_w = jax.random.uniform(ks[1], (3 * DIM, DIM), jnp.float32, -bound, bound)
        proj_w = jax.random.uniform(ks[2], (DIM, DIM), jnp.float32, -bound, bound)
        return {'x': x, 'qkv_w': qkv_w, 'qkv_norm_w': jnp.ones((DIM,), jnp.float32), 'proj_w': proj_w, 'proj_norm_w': jnp.ones((DIM,), jnp.float32), 'norm_w': jnp.ones((DIM,), jnp.float32), 's': jnp.full((HEADS,), 0.02, jnp.float32)}
    _L0_attn_all = _L0_attn_setup()
    _L0_attn_in = {k: v for k, v in _L0_attn_all.items() if k in ('qkv_w', 'qkv_norm_w', 'proj_w', 'proj_norm_w', 'norm_w', 's')}
    del _L0_attn_all

    def _L0_cond2_setup():
        import jax, jax.numpy as jnp
        from jax import lax
        import numpy as np
        B, T, C, TD = (8, 256, 256, 64)

        def _bi_wkv(r, k, v, w, u, time_emb):
            tf = jax.nn.sigmoid(jnp.sum(time_emb, axis=-1))[:, None, None]
            decay = jnp.exp(-jnp.exp(w.astype(jnp.float32)))[None, :] * (0.5 + 0.5 * tf[:, :, 0])
            kf = k.astype(jnp.float32)
            vf = v.astype(jnp.float32)
            ek = jnp.exp(jnp.minimum(kf, 30.0))
            ekv = ek * vf

            def step(carry, x):
                a, b = carry
                ekv_t, ek_t = x
                a = a * decay + ekv_t
                b = b * decay + ek_t
                return ((a, b), (a, b))
            ekv_t = jnp.swapaxes(ekv, 0, 1)
            ek_t = jnp.swapaxes(ek, 0, 1)
            init = (jnp.zeros_like(decay), jnp.zeros_like(decay))
            _, (nf, df) = lax.scan(step, init, (ekv_t, ek_t))
            _, (nb, db) = lax.scan(step, init, (ekv_t, ek_t), reverse=True)
            nf = jnp.swapaxes(nf, 0, 1)
            df = jnp.swapaxes(df, 0, 1)
            nb = jnp.swapaxes(nb, 0, 1)
            db = jnp.swapaxes(db, 0, 1)
            euk = jnp.exp(jnp.minimum(u.astype(jnp.float32)[None, None, :] + kf, 30.0))
            num = nf + nb - ekv + euk * vf
            den = df + db - ek + euk
            base = jax.nn.sigmoid(r.astype(jnp.float32)) * (num / jnp.maximum(den, 1e-08))
            out = base * (0.8 + 0.2 * tf)
            return out.astype(r.dtype)
        key = jax.random.key(seed)
        ks = jax.random.split(key, 6)
        return {'r': jax.random.normal(ks[0], (B, T, C), dtype=jnp.float32), 'k': jax.random.normal(ks[1], (B, T, C), dtype=jnp.float32), 'v': jax.random.normal(ks[2], (B, T, C), dtype=jnp.float32), 'w': jax.random.normal(ks[3], (C,), dtype=jnp.float32), 'u': jax.random.normal(ks[4], (C,), dtype=jnp.float32), 'time_emb': jax.random.normal(ks[5], (B, TD), dtype=jnp.float32)}
    _L0_cond2_all = _L0_cond2_setup()
    _L0_cond2_in = {k: v for k, v in _L0_cond2_all.items() if k in ('w', 'u')}
    del _L0_cond2_all

    def _L0_ffn_setup():
        import jax, jax.numpy as jnp
        import numpy as np
        B, S, D, F, E, K = (2, 256, 256, 512, 8, 1)

        def _silu_mul(gu):
            g, u = jnp.split(gu, 2, axis=-1)
            return jax.nn.silu(g) * u

        def _moe_forward(hidden_states, router_w, w_gate_up, w_down, shared_gate_up, shared_down, top_k=K):
            b, s, d = hidden_states.shape
            x = hidden_states.reshape(-1, d)
            router_logits = x @ router_w.T
            topk_vals, topk_ids = jax.lax.top_k(router_logits, top_k)
            gate = jax.nn.sigmoid(topk_vals.astype(jnp.float32)).astype(x.dtype)
            xs = (x[:, None, :] * gate[:, :, None]).reshape(-1, d)
            ids_flat = topk_ids.reshape(-1)
            n_experts = w_gate_up.shape[0]

            def body(acc, inp):
                wg, wd, e = inp
                h = _silu_mul(xs @ wg)
                o = h @ wd
                mask = (ids_flat == e)[:, None]
                return (acc + jnp.where(mask, o, jnp.zeros((), o.dtype)), None)
            acc0 = jnp.zeros_like(xs)
            routed, _ = jax.lax.scan(body, acc0, (w_gate_up, w_down, jnp.arange(n_experts)))
            routed = routed.reshape(-1, top_k, d).sum(1)
            shared = _silu_mul(x @ shared_gate_up) @ shared_down
            return (routed + shared).reshape(b, s, d)
        key = jax.random.key(seed)
        ks = jax.random.split(key, 6)
        scale = 0.02
        return {'hidden_states': jax.random.normal(ks[0], (B, S, D), jnp.float32), 'router_w': jax.random.normal(ks[1], (E, D), jnp.float32) * scale, 'w_gate_up': jax.random.normal(ks[2], (E, D, 2 * F), jnp.float32) * scale, 'w_down': jax.random.normal(ks[3], (E, F, D), jnp.float32) * scale, 'shared_gate_up': jax.random.normal(ks[4], (D, 2 * F), jnp.float32) * scale, 'shared_down': jax.random.normal(ks[5], (F, D), jnp.float32) * scale}
    _L0_ffn_all = _L0_ffn_setup()
    _L0_ffn_in = {k: v for k, v in _L0_ffn_all.items() if k in ('router_w', 'w_gate_up', 'w_down', 'shared_gate_up', 'shared_down')}
    del _L0_ffn_all

    def _L1_cond_setup():
        import jax, jax.numpy as jnp
        from jax import lax
        import numpy as np
        B, T, C, TD = (8, 256, 256, 64)

        def _bi_wkv(r, k, v, w, u, time_emb):
            tf = jax.nn.sigmoid(jnp.sum(time_emb, axis=-1))[:, None, None]
            decay = jnp.exp(-jnp.exp(w.astype(jnp.float32)))[None, :] * (0.5 + 0.5 * tf[:, :, 0])
            kf = k.astype(jnp.float32)
            vf = v.astype(jnp.float32)
            ek = jnp.exp(jnp.minimum(kf, 30.0))
            ekv = ek * vf

            def step(carry, x):
                a, b = carry
                ekv_t, ek_t = x
                a = a * decay + ekv_t
                b = b * decay + ek_t
                return ((a, b), (a, b))
            ekv_t = jnp.swapaxes(ekv, 0, 1)
            ek_t = jnp.swapaxes(ek, 0, 1)
            init = (jnp.zeros_like(decay), jnp.zeros_like(decay))
            _, (nf, df) = lax.scan(step, init, (ekv_t, ek_t))
            _, (nb, db) = lax.scan(step, init, (ekv_t, ek_t), reverse=True)
            nf = jnp.swapaxes(nf, 0, 1)
            df = jnp.swapaxes(df, 0, 1)
            nb = jnp.swapaxes(nb, 0, 1)
            db = jnp.swapaxes(db, 0, 1)
            euk = jnp.exp(jnp.minimum(u.astype(jnp.float32)[None, None, :] + kf, 30.0))
            num = nf + nb - ekv + euk * vf
            den = df + db - ek + euk
            base = jax.nn.sigmoid(r.astype(jnp.float32)) * (num / jnp.maximum(den, 1e-08))
            out = base * (0.8 + 0.2 * tf)
            return out.astype(r.dtype)
        key = jax.random.key(seed)
        ks = jax.random.split(key, 6)
        return {'r': jax.random.normal(ks[0], (B, T, C), dtype=jnp.float32), 'k': jax.random.normal(ks[1], (B, T, C), dtype=jnp.float32), 'v': jax.random.normal(ks[2], (B, T, C), dtype=jnp.float32), 'w': jax.random.normal(ks[3], (C,), dtype=jnp.float32), 'u': jax.random.normal(ks[4], (C,), dtype=jnp.float32), 'time_emb': jax.random.normal(ks[5], (B, TD), dtype=jnp.float32)}
    _L1_cond_all = _L1_cond_setup()
    _L1_cond_in = {k: v for k, v in _L1_cond_all.items() if k in ('w', 'u')}
    del _L1_cond_all

    def _L1_attn_setup():
        import jax, jax.numpy as jnp
        import numpy as np
        D_MODEL = 256
        N_HEADS = 16
        HEAD_DIM = D_MODEL // N_HEADS
        WINDOW = 32
        G = 16
        LN_EPS = 1e-05

        def _sparse_mask(T, dtype=jnp.float32):
            i = jnp.arange(T)[:, None]
            j = jnp.arange(T)[None, :]
            band = (j <= i) & (j >= i - WINDOW + 1)
            neg = jnp.array(-jnp.inf, dtype)
            mask = jnp.full((G + T, G + T), neg, dtype)
            mask = mask.at[:G, :].set(0.0)
            mask = mask.at[:, :G].set(0.0)
            mask = mask.at[G:, G:].set(jnp.where(band, jnp.array(0.0, dtype), neg))
            return mask
        key = jax.random.key(seed)
        ks = jax.random.split(key, 6)
        B, T, D = (2, 256, D_MODEL)
        s = 1.0 / np.sqrt(D)
        return {'x': jax.random.normal(ks[0], (B, T, D), jnp.float32), 'global_tokens': jax.random.normal(ks[1], (1, G, D), jnp.float32) * 0.02, 'ln_scale': jnp.ones((D,), jnp.float32), 'ln_bias': jnp.zeros((D,), jnp.float32), 'Wq': jax.random.normal(ks[2], (D, D), jnp.float32) * s, 'Wk': jax.random.normal(ks[3], (D, D), jnp.float32) * s, 'Wv': jax.random.normal(ks[4], (D, D), jnp.float32) * s, 'Wo': jax.random.normal(ks[5], (D, D), jnp.float32) * s}
    _L1_attn_all = _L1_attn_setup()
    _L1_attn_in = {k: v for k, v in _L1_attn_all.items() if k in ('global_tokens', 'ln_scale', 'ln_bias', 'Wq', 'Wk', 'Wv', 'Wo')}
    del _L1_attn_all

    def _L1_cond2_setup():
        import jax, jax.numpy as jnp
        from jax import lax
        import numpy as np
        B, T, C, TD = (8, 256, 256, 64)

        def _bi_wkv(r, k, v, w, u, time_emb):
            tf = jax.nn.sigmoid(jnp.sum(time_emb, axis=-1))[:, None, None]
            decay = jnp.exp(-jnp.exp(w.astype(jnp.float32)))[None, :] * (0.5 + 0.5 * tf[:, :, 0])
            kf = k.astype(jnp.float32)
            vf = v.astype(jnp.float32)
            ek = jnp.exp(jnp.minimum(kf, 30.0))
            ekv = ek * vf

            def step(carry, x):
                a, b = carry
                ekv_t, ek_t = x
                a = a * decay + ekv_t
                b = b * decay + ek_t
                return ((a, b), (a, b))
            ekv_t = jnp.swapaxes(ekv, 0, 1)
            ek_t = jnp.swapaxes(ek, 0, 1)
            init = (jnp.zeros_like(decay), jnp.zeros_like(decay))
            _, (nf, df) = lax.scan(step, init, (ekv_t, ek_t))
            _, (nb, db) = lax.scan(step, init, (ekv_t, ek_t), reverse=True)
            nf = jnp.swapaxes(nf, 0, 1)
            df = jnp.swapaxes(df, 0, 1)
            nb = jnp.swapaxes(nb, 0, 1)
            db = jnp.swapaxes(db, 0, 1)
            euk = jnp.exp(jnp.minimum(u.astype(jnp.float32)[None, None, :] + kf, 30.0))
            num = nf + nb - ekv + euk * vf
            den = df + db - ek + euk
            base = jax.nn.sigmoid(r.astype(jnp.float32)) * (num / jnp.maximum(den, 1e-08))
            out = base * (0.8 + 0.2 * tf)
            return out.astype(r.dtype)
        key = jax.random.key(seed)
        ks = jax.random.split(key, 6)
        return {'r': jax.random.normal(ks[0], (B, T, C), dtype=jnp.float32), 'k': jax.random.normal(ks[1], (B, T, C), dtype=jnp.float32), 'v': jax.random.normal(ks[2], (B, T, C), dtype=jnp.float32), 'w': jax.random.normal(ks[3], (C,), dtype=jnp.float32), 'u': jax.random.normal(ks[4], (C,), dtype=jnp.float32), 'time_emb': jax.random.normal(ks[5], (B, TD), dtype=jnp.float32)}
    _L1_cond2_all = _L1_cond2_setup()
    _L1_cond2_in = {k: v for k, v in _L1_cond2_all.items() if k in ('w', 'u')}
    del _L1_cond2_all

    def _L1_ffn_setup():
        import jax, jax.numpy as jnp
        import numpy as np
        B, S, H, F, E, R, K = (2, 128, 256, 896, 8, 32, 2)

        def _gather_slot(a_all, e):
            return jnp.take_along_axis(a_all, e[:, None, None], axis=1)[:, 0]
        key = jax.random.key(seed)
        ks = jax.random.split(key, 12)
        sc = 0.02
        n = lambda k, shape, s: jax.random.normal(k, shape, dtype=jnp.float32) * s
        return {'hidden_states': n(ks[0], (B, S, H), 1.0), 'Wg': n(ks[1], (E, H), sc), 'W1': n(ks[2], (F, H), sc), 'W2': n(ks[3], (H, F), sc), 'W3': n(ks[4], (F, H), sc), 'A1': n(ks[5], (E, R, H), sc), 'B1': n(ks[6], (E, F, R), sc), 'A2': n(ks[7], (E, R, F), sc), 'B2': n(ks[8], (E, H, R), sc), 'A3': n(ks[9], (E, R, H), sc), 'B3': n(ks[10], (E, F, R), sc)}
    _L1_ffn_all = _L1_ffn_setup()
    _L1_ffn_in = {k: v for k, v in _L1_ffn_all.items() if k in ('Wg', 'W1', 'W2', 'W3', 'A1', 'B1', 'A2', 'B2', 'A3', 'B3')}
    del _L1_ffn_all

    def _L2_cond_setup():
        import jax, jax.numpy as jnp
        from jax import lax
        import numpy as np
        B, T, C, TD = (8, 256, 256, 64)

        def _bi_wkv(r, k, v, w, u, time_emb):
            tf = jax.nn.sigmoid(jnp.sum(time_emb, axis=-1))[:, None, None]
            decay = jnp.exp(-jnp.exp(w.astype(jnp.float32)))[None, :] * (0.5 + 0.5 * tf[:, :, 0])
            kf = k.astype(jnp.float32)
            vf = v.astype(jnp.float32)
            ek = jnp.exp(jnp.minimum(kf, 30.0))
            ekv = ek * vf

            def step(carry, x):
                a, b = carry
                ekv_t, ek_t = x
                a = a * decay + ekv_t
                b = b * decay + ek_t
                return ((a, b), (a, b))
            ekv_t = jnp.swapaxes(ekv, 0, 1)
            ek_t = jnp.swapaxes(ek, 0, 1)
            init = (jnp.zeros_like(decay), jnp.zeros_like(decay))
            _, (nf, df) = lax.scan(step, init, (ekv_t, ek_t))
            _, (nb, db) = lax.scan(step, init, (ekv_t, ek_t), reverse=True)
            nf = jnp.swapaxes(nf, 0, 1)
            df = jnp.swapaxes(df, 0, 1)
            nb = jnp.swapaxes(nb, 0, 1)
            db = jnp.swapaxes(db, 0, 1)
            euk = jnp.exp(jnp.minimum(u.astype(jnp.float32)[None, None, :] + kf, 30.0))
            num = nf + nb - ekv + euk * vf
            den = df + db - ek + euk
            base = jax.nn.sigmoid(r.astype(jnp.float32)) * (num / jnp.maximum(den, 1e-08))
            out = base * (0.8 + 0.2 * tf)
            return out.astype(r.dtype)
        key = jax.random.key(seed)
        ks = jax.random.split(key, 6)
        return {'r': jax.random.normal(ks[0], (B, T, C), dtype=jnp.float32), 'k': jax.random.normal(ks[1], (B, T, C), dtype=jnp.float32), 'v': jax.random.normal(ks[2], (B, T, C), dtype=jnp.float32), 'w': jax.random.normal(ks[3], (C,), dtype=jnp.float32), 'u': jax.random.normal(ks[4], (C,), dtype=jnp.float32), 'time_emb': jax.random.normal(ks[5], (B, TD), dtype=jnp.float32)}
    _L2_cond_all = _L2_cond_setup()
    _L2_cond_in = {k: v for k, v in _L2_cond_all.items() if k in ('w', 'u')}
    del _L2_cond_all

    def _L2_attn_setup():
        import math
        import jax, jax.numpy as jnp
        import numpy as np
        H, KV, D = (16, 4, 128)
        HID = 256
        ROPE_BASE = 1000000.0
        EPS = 1e-06

        def _layernorm(x, w, b):
            mu = jnp.mean(x, axis=-1, keepdims=True)
            xc = x - mu
            var = jnp.mean(xc * xc, axis=-1, keepdims=True)
            return xc * jax.lax.rsqrt(var + EPS) * w + b

        def _rope(x, cos, sin):
            xr, xi = (x[..., 0::2], x[..., 1::2])
            c, s = (cos[None, None], sin[None, None])
            out = jnp.stack([xr * c - xi * s, xr * s + xi * c], axis=-1)
            return out.reshape(x.shape)
        key = jax.random.key(seed)
        ks = jax.random.split(key, 3)
        B, S = (2, 256)
        s = 0.02
        return {'x': jax.random.normal(ks[0], (B, S, HID), jnp.float32), 'w_qkv': jax.random.normal(ks[1], (2 * H * D + 2 * KV * D, HID), jnp.float32) * s, 'w_o': jax.random.normal(ks[2], (HID, H * D), jnp.float32) * s, 'q_norm_w': jnp.ones((D,), jnp.float32), 'q_norm_b': jnp.zeros((D,), jnp.float32), 'k_norm_w': jnp.ones((D,), jnp.float32), 'k_norm_b': jnp.zeros((D,), jnp.float32)}
    _L2_attn_all = _L2_attn_setup()
    _L2_attn_in = {k: v for k, v in _L2_attn_all.items() if k in ('w_qkv', 'w_o', 'q_norm_w', 'q_norm_b', 'k_norm_w', 'k_norm_b')}
    del _L2_attn_all

    def _L2_cond2_setup():
        import jax, jax.numpy as jnp
        from jax import lax
        import numpy as np
        B, T, C, TD = (8, 256, 256, 64)

        def _bi_wkv(r, k, v, w, u, time_emb):
            tf = jax.nn.sigmoid(jnp.sum(time_emb, axis=-1))[:, None, None]
            decay = jnp.exp(-jnp.exp(w.astype(jnp.float32)))[None, :] * (0.5 + 0.5 * tf[:, :, 0])
            kf = k.astype(jnp.float32)
            vf = v.astype(jnp.float32)
            ek = jnp.exp(jnp.minimum(kf, 30.0))
            ekv = ek * vf

            def step(carry, x):
                a, b = carry
                ekv_t, ek_t = x
                a = a * decay + ekv_t
                b = b * decay + ek_t
                return ((a, b), (a, b))
            ekv_t = jnp.swapaxes(ekv, 0, 1)
            ek_t = jnp.swapaxes(ek, 0, 1)
            init = (jnp.zeros_like(decay), jnp.zeros_like(decay))
            _, (nf, df) = lax.scan(step, init, (ekv_t, ek_t))
            _, (nb, db) = lax.scan(step, init, (ekv_t, ek_t), reverse=True)
            nf = jnp.swapaxes(nf, 0, 1)
            df = jnp.swapaxes(df, 0, 1)
            nb = jnp.swapaxes(nb, 0, 1)
            db = jnp.swapaxes(db, 0, 1)
            euk = jnp.exp(jnp.minimum(u.astype(jnp.float32)[None, None, :] + kf, 30.0))
            num = nf + nb - ekv + euk * vf
            den = df + db - ek + euk
            base = jax.nn.sigmoid(r.astype(jnp.float32)) * (num / jnp.maximum(den, 1e-08))
            out = base * (0.8 + 0.2 * tf)
            return out.astype(r.dtype)
        key = jax.random.key(seed)
        ks = jax.random.split(key, 6)
        return {'r': jax.random.normal(ks[0], (B, T, C), dtype=jnp.float32), 'k': jax.random.normal(ks[1], (B, T, C), dtype=jnp.float32), 'v': jax.random.normal(ks[2], (B, T, C), dtype=jnp.float32), 'w': jax.random.normal(ks[3], (C,), dtype=jnp.float32), 'u': jax.random.normal(ks[4], (C,), dtype=jnp.float32), 'time_emb': jax.random.normal(ks[5], (B, TD), dtype=jnp.float32)}
    _L2_cond2_all = _L2_cond2_setup()
    _L2_cond2_in = {k: v for k, v in _L2_cond2_all.items() if k in ('w', 'u')}
    del _L2_cond2_all

    def _L2_ffn_setup():
        import jax, jax.numpy as jnp
        import numpy as np
        QMAX = 127.0
        EPS = 1e-08

        def _quant_dequant(v, axis):
            scale = jnp.max(jnp.abs(v), axis=axis, keepdims=True) / QMAX
            scale = jnp.maximum(scale, EPS)
            q = jnp.clip(jnp.round(v / scale), -QMAX, QMAX)
            return q * scale

        def _ste(v, axis):
            return v + jax.lax.stop_gradient(_quant_dequant(v, axis) - v)
        key = jax.random.key(seed)
        k1, k2, k3 = jax.random.split(key, 3)
        H, I = (256, 704)
        x = jax.random.normal(k1, (4, 256, H), dtype=jnp.float32)
        w_gate_up = jax.random.normal(k2, (2 * I, H), dtype=jnp.float32) * H ** (-0.5)
        w_down = jax.random.normal(k3, (H, I), dtype=jnp.float32) * I ** (-0.5)
        return {'x': x, 'w_gate_up': w_gate_up, 'w_down': w_down}
    _L2_ffn_all = _L2_ffn_setup()
    _L2_ffn_in = {k: v for k, v in _L2_ffn_all.items() if k in ('w_gate_up', 'w_down')}
    del _L2_ffn_all

    def _L3_cond_setup():
        import jax, jax.numpy as jnp
        from jax import lax
        import numpy as np
        B, T, C, TD = (8, 256, 256, 64)

        def _bi_wkv(r, k, v, w, u, time_emb):
            tf = jax.nn.sigmoid(jnp.sum(time_emb, axis=-1))[:, None, None]
            decay = jnp.exp(-jnp.exp(w.astype(jnp.float32)))[None, :] * (0.5 + 0.5 * tf[:, :, 0])
            kf = k.astype(jnp.float32)
            vf = v.astype(jnp.float32)
            ek = jnp.exp(jnp.minimum(kf, 30.0))
            ekv = ek * vf

            def step(carry, x):
                a, b = carry
                ekv_t, ek_t = x
                a = a * decay + ekv_t
                b = b * decay + ek_t
                return ((a, b), (a, b))
            ekv_t = jnp.swapaxes(ekv, 0, 1)
            ek_t = jnp.swapaxes(ek, 0, 1)
            init = (jnp.zeros_like(decay), jnp.zeros_like(decay))
            _, (nf, df) = lax.scan(step, init, (ekv_t, ek_t))
            _, (nb, db) = lax.scan(step, init, (ekv_t, ek_t), reverse=True)
            nf = jnp.swapaxes(nf, 0, 1)
            df = jnp.swapaxes(df, 0, 1)
            nb = jnp.swapaxes(nb, 0, 1)
            db = jnp.swapaxes(db, 0, 1)
            euk = jnp.exp(jnp.minimum(u.astype(jnp.float32)[None, None, :] + kf, 30.0))
            num = nf + nb - ekv + euk * vf
            den = df + db - ek + euk
            base = jax.nn.sigmoid(r.astype(jnp.float32)) * (num / jnp.maximum(den, 1e-08))
            out = base * (0.8 + 0.2 * tf)
            return out.astype(r.dtype)
        key = jax.random.key(seed)
        ks = jax.random.split(key, 6)
        return {'r': jax.random.normal(ks[0], (B, T, C), dtype=jnp.float32), 'k': jax.random.normal(ks[1], (B, T, C), dtype=jnp.float32), 'v': jax.random.normal(ks[2], (B, T, C), dtype=jnp.float32), 'w': jax.random.normal(ks[3], (C,), dtype=jnp.float32), 'u': jax.random.normal(ks[4], (C,), dtype=jnp.float32), 'time_emb': jax.random.normal(ks[5], (B, TD), dtype=jnp.float32)}
    _L3_cond_all = _L3_cond_setup()
    _L3_cond_in = {k: v for k, v in _L3_cond_all.items() if k in ('w', 'u')}
    del _L3_cond_all

    def _L3_attn_setup():
        import jax, jax.numpy as jnp
        import numpy as np
        B, L, D = (4, 256, 256)
        E, N, DT, DC = (512, 16, 128, 4)
        EPS = 1e-05
        key = jax.random.key(seed)
        ks = jax.random.split(key, 12)
        s = lambda k, shape, scale: jax.random.normal(k, shape, jnp.float32) * scale
        return {'x': jax.random.normal(ks[0], (B, L, D), jnp.float32), 'norm_w': jnp.ones((D,), jnp.float32), 'W_skip': s(ks[1], (E, D), 0.02), 'W_in': s(ks[2], (E, D), 0.02), 'conv_w': s(ks[3], (E, 1, DC), 0.1), 'conv_b': jnp.zeros((E,), jnp.float32), 'Wd1': s(ks[4], (DT, E), 0.02), 'Wd2': s(ks[5], (E, DT), 0.02), 'bd2': jnp.zeros((E,), jnp.float32), 'WB': s(ks[6], (N, E), 0.02), 'WC': s(ks[7], (N, E), 0.02), 'A_log': s(ks[8], (E, N), 0.5), 'W_D': jnp.ones((E,), jnp.float32), 'W_out': s(ks[9], (D, E), 0.02)}
    _L3_attn_all = _L3_attn_setup()
    _L3_attn_in = {k: v for k, v in _L3_attn_all.items() if k in ('norm_w', 'W_skip', 'W_in', 'conv_w', 'conv_b', 'Wd1', 'Wd2', 'bd2', 'WB', 'WC', 'A_log', 'W_D', 'W_out')}
    del _L3_attn_all

    def _L3_cond2_setup():
        import jax, jax.numpy as jnp
        from jax import lax
        import numpy as np
        B, T, C, TD = (8, 256, 256, 64)

        def _bi_wkv(r, k, v, w, u, time_emb):
            tf = jax.nn.sigmoid(jnp.sum(time_emb, axis=-1))[:, None, None]
            decay = jnp.exp(-jnp.exp(w.astype(jnp.float32)))[None, :] * (0.5 + 0.5 * tf[:, :, 0])
            kf = k.astype(jnp.float32)
            vf = v.astype(jnp.float32)
            ek = jnp.exp(jnp.minimum(kf, 30.0))
            ekv = ek * vf

            def step(carry, x):
                a, b = carry
                ekv_t, ek_t = x
                a = a * decay + ekv_t
                b = b * decay + ek_t
                return ((a, b), (a, b))
            ekv_t = jnp.swapaxes(ekv, 0, 1)
            ek_t = jnp.swapaxes(ek, 0, 1)
            init = (jnp.zeros_like(decay), jnp.zeros_like(decay))
            _, (nf, df) = lax.scan(step, init, (ekv_t, ek_t))
            _, (nb, db) = lax.scan(step, init, (ekv_t, ek_t), reverse=True)
            nf = jnp.swapaxes(nf, 0, 1)
            df = jnp.swapaxes(df, 0, 1)
            nb = jnp.swapaxes(nb, 0, 1)
            db = jnp.swapaxes(db, 0, 1)
            euk = jnp.exp(jnp.minimum(u.astype(jnp.float32)[None, None, :] + kf, 30.0))
            num = nf + nb - ekv + euk * vf
            den = df + db - ek + euk
            base = jax.nn.sigmoid(r.astype(jnp.float32)) * (num / jnp.maximum(den, 1e-08))
            out = base * (0.8 + 0.2 * tf)
            return out.astype(r.dtype)
        key = jax.random.key(seed)
        ks = jax.random.split(key, 6)
        return {'r': jax.random.normal(ks[0], (B, T, C), dtype=jnp.float32), 'k': jax.random.normal(ks[1], (B, T, C), dtype=jnp.float32), 'v': jax.random.normal(ks[2], (B, T, C), dtype=jnp.float32), 'w': jax.random.normal(ks[3], (C,), dtype=jnp.float32), 'u': jax.random.normal(ks[4], (C,), dtype=jnp.float32), 'time_emb': jax.random.normal(ks[5], (B, TD), dtype=jnp.float32)}
    _L3_cond2_all = _L3_cond2_setup()
    _L3_cond2_in = {k: v for k, v in _L3_cond2_all.items() if k in ('w', 'u')}
    del _L3_cond2_all

    def _L3_ffn_setup():
        import jax, jax.numpy as jnp
        import numpy as np
        from jax import lax
        H = 256
        I = 176
        E = 16
        K = 4
        ISH = 2 * I
        B, S = (4, 256)

        def _router(xf, rg_w, ru_w, extra_scale, extra_bias):
            g = xf @ rg_w.T
            u = xf @ ru_w.T
            scores = jnp.abs(u * jax.nn.silu(g))
            probs = jax.nn.softmax(scores.astype(jnp.float32), axis=-1)
            biased = probs + extra_bias[None, :]
            _, idx = lax.top_k(biased, K)
            orig = 1.0 + probs * extra_scale[None, :]
            w = jnp.take_along_axis(orig, idx, axis=1).astype(xf.dtype)
            return (w, idx)
        key = jax.random.key(seed)
        ks = jax.random.split(key, 12)
        sc = 0.02
        return {'x': jax.random.normal(ks[0], (B, S, H), dtype=jnp.float32), 'rg_w': jax.random.normal(ks[1], (E, H), dtype=jnp.float32) * sc, 'ru_w': jax.random.normal(ks[2], (E, H), dtype=jnp.float32) * sc, 'extra_scale': jnp.zeros((E,), dtype=jnp.float32), 'extra_bias': jnp.zeros((E,), dtype=jnp.float32), 'Wg': jax.random.normal(ks[3], (E, I, H), dtype=jnp.float32) * sc, 'Wu': jax.random.normal(ks[4], (E, I, H), dtype=jnp.float32) * sc, 'Wd': jax.random.normal(ks[5], (E, H, I), dtype=jnp.float32) * sc, 'Sg': jax.random.normal(ks[6], (ISH, H), dtype=jnp.float32) * sc, 'Su': jax.random.normal(ks[7], (ISH, H), dtype=jnp.float32) * sc, 'Sd': jax.random.normal(ks[8], (H, ISH), dtype=jnp.float32) * sc}
    _L3_ffn_all = _L3_ffn_setup()
    _L3_ffn_in = {k: v for k, v in _L3_ffn_all.items() if k in ('rg_w', 'ru_w', 'extra_scale', 'extra_bias', 'Wg', 'Wu', 'Wd', 'Sg', 'Su', 'Sd')}
    del _L3_ffn_all
    return {'x': x, 'fside_BxSxS_0': fside_BxSxS_0, 'cond_512': cond_512, 'L0_cond_w': _L0_cond_in['w'], 'L0_cond_u': _L0_cond_in['u'], 'L0_attn_qkv_w': _L0_attn_in['qkv_w'], 'L0_attn_qkv_norm_w': _L0_attn_in['qkv_norm_w'], 'L0_attn_proj_w': _L0_attn_in['proj_w'], 'L0_attn_proj_norm_w': _L0_attn_in['proj_norm_w'], 'L0_attn_norm_w': _L0_attn_in['norm_w'], 'L0_attn_s': _L0_attn_in['s'], 'L0_cond2_w': _L0_cond2_in['w'], 'L0_cond2_u': _L0_cond2_in['u'], 'L0_ffn_router_w': _L0_ffn_in['router_w'], 'L0_ffn_w_gate_up': _L0_ffn_in['w_gate_up'], 'L0_ffn_w_down': _L0_ffn_in['w_down'], 'L0_ffn_shared_gate_up': _L0_ffn_in['shared_gate_up'], 'L0_ffn_shared_down': _L0_ffn_in['shared_down'], 'L1_cond_w': _L1_cond_in['w'], 'L1_cond_u': _L1_cond_in['u'], 'L1_attn_global_tokens': _L1_attn_in['global_tokens'], 'L1_attn_ln_scale': _L1_attn_in['ln_scale'], 'L1_attn_ln_bias': _L1_attn_in['ln_bias'], 'L1_attn_Wq': _L1_attn_in['Wq'], 'L1_attn_Wk': _L1_attn_in['Wk'], 'L1_attn_Wv': _L1_attn_in['Wv'], 'L1_attn_Wo': _L1_attn_in['Wo'], 'L1_cond2_w': _L1_cond2_in['w'], 'L1_cond2_u': _L1_cond2_in['u'], 'L1_ffn_Wg': _L1_ffn_in['Wg'], 'L1_ffn_W1': _L1_ffn_in['W1'], 'L1_ffn_W2': _L1_ffn_in['W2'], 'L1_ffn_W3': _L1_ffn_in['W3'], 'L1_ffn_A1': _L1_ffn_in['A1'], 'L1_ffn_B1': _L1_ffn_in['B1'], 'L1_ffn_A2': _L1_ffn_in['A2'], 'L1_ffn_B2': _L1_ffn_in['B2'], 'L1_ffn_A3': _L1_ffn_in['A3'], 'L1_ffn_B3': _L1_ffn_in['B3'], 'L2_cond_w': _L2_cond_in['w'], 'L2_cond_u': _L2_cond_in['u'], 'L2_attn_w_qkv': _L2_attn_in['w_qkv'], 'L2_attn_w_o': _L2_attn_in['w_o'], 'L2_attn_q_norm_w': _L2_attn_in['q_norm_w'], 'L2_attn_q_norm_b': _L2_attn_in['q_norm_b'], 'L2_attn_k_norm_w': _L2_attn_in['k_norm_w'], 'L2_attn_k_norm_b': _L2_attn_in['k_norm_b'], 'L2_cond2_w': _L2_cond2_in['w'], 'L2_cond2_u': _L2_cond2_in['u'], 'L2_ffn_w_gate_up': _L2_ffn_in['w_gate_up'], 'L2_ffn_w_down': _L2_ffn_in['w_down'], 'L3_cond_w': _L3_cond_in['w'], 'L3_cond_u': _L3_cond_in['u'], 'L3_attn_norm_w': _L3_attn_in['norm_w'], 'L3_attn_W_skip': _L3_attn_in['W_skip'], 'L3_attn_W_in': _L3_attn_in['W_in'], 'L3_attn_conv_w': _L3_attn_in['conv_w'], 'L3_attn_conv_b': _L3_attn_in['conv_b'], 'L3_attn_Wd1': _L3_attn_in['Wd1'], 'L3_attn_Wd2': _L3_attn_in['Wd2'], 'L3_attn_bd2': _L3_attn_in['bd2'], 'L3_attn_WB': _L3_attn_in['WB'], 'L3_attn_WC': _L3_attn_in['WC'], 'L3_attn_A_log': _L3_attn_in['A_log'], 'L3_attn_W_D': _L3_attn_in['W_D'], 'L3_attn_W_out': _L3_attn_in['W_out'], 'L3_cond2_w': _L3_cond2_in['w'], 'L3_cond2_u': _L3_cond2_in['u'], 'L3_ffn_rg_w': _L3_ffn_in['rg_w'], 'L3_ffn_ru_w': _L3_ffn_in['ru_w'], 'L3_ffn_extra_scale': _L3_ffn_in['extra_scale'], 'L3_ffn_extra_bias': _L3_ffn_in['extra_bias'], 'L3_ffn_Wg': _L3_ffn_in['Wg'], 'L3_ffn_Wu': _L3_ffn_in['Wu'], 'L3_ffn_Wd': _L3_ffn_in['Wd'], 'L3_ffn_Sg': _L3_ffn_in['Sg'], 'L3_ffn_Su': _L3_ffn_in['Su'], 'L3_ffn_Sd': _L3_ffn_in['Sd']}

def reference(x, fside_BxSxS_0, cond_512, L0_cond_w, L0_cond_u, L0_attn_qkv_w, L0_attn_qkv_norm_w, L0_attn_proj_w, L0_attn_proj_norm_w, L0_attn_norm_w, L0_attn_s, L0_cond2_w, L0_cond2_u, L0_ffn_router_w, L0_ffn_w_gate_up, L0_ffn_w_down, L0_ffn_shared_gate_up, L0_ffn_shared_down, L1_cond_w, L1_cond_u, L1_attn_global_tokens, L1_attn_ln_scale, L1_attn_ln_bias, L1_attn_Wq, L1_attn_Wk, L1_attn_Wv, L1_attn_Wo, L1_cond2_w, L1_cond2_u, L1_ffn_Wg, L1_ffn_W1, L1_ffn_W2, L1_ffn_W3, L1_ffn_A1, L1_ffn_B1, L1_ffn_A2, L1_ffn_B2, L1_ffn_A3, L1_ffn_B3, L2_cond_w, L2_cond_u, L2_attn_w_qkv, L2_attn_w_o, L2_attn_q_norm_w, L2_attn_q_norm_b, L2_attn_k_norm_w, L2_attn_k_norm_b, L2_cond2_w, L2_cond2_u, L2_ffn_w_gate_up, L2_ffn_w_down, L3_cond_w, L3_cond_u, L3_attn_norm_w, L3_attn_W_skip, L3_attn_W_in, L3_attn_conv_w, L3_attn_conv_b, L3_attn_Wd1, L3_attn_Wd2, L3_attn_bd2, L3_attn_WB, L3_attn_WC, L3_attn_A_log, L3_attn_W_D, L3_attn_W_out, L3_cond2_w, L3_cond2_u, L3_ffn_rg_w, L3_ffn_ru_w, L3_ffn_extra_scale, L3_ffn_extra_bias, L3_ffn_Wg, L3_ffn_Wu, L3_ffn_Wd, L3_ffn_Sg, L3_ffn_Su, L3_ffn_Sd):
    import jax
    import jax.numpy as jnp

    def _L0_cond_ref(r, k, v, w, u, time_emb):
        import jax, jax.numpy as jnp
        from jax import lax
        import numpy as np
        B, T, C, TD = (8, 256, 256, 64)

        def _bi_wkv(r, k, v, w, u, time_emb):
            tf = jax.nn.sigmoid(jnp.sum(time_emb, axis=-1))[:, None, None]
            decay = jnp.exp(-jnp.exp(w.astype(jnp.float32)))[None, :] * (0.5 + 0.5 * tf[:, :, 0])
            kf = k.astype(jnp.float32)
            vf = v.astype(jnp.float32)
            ek = jnp.exp(jnp.minimum(kf, 30.0))
            ekv = ek * vf

            def step(carry, x):
                a, b = carry
                ekv_t, ek_t = x
                a = a * decay + ekv_t
                b = b * decay + ek_t
                return ((a, b), (a, b))
            ekv_t = jnp.swapaxes(ekv, 0, 1)
            ek_t = jnp.swapaxes(ek, 0, 1)
            init = (jnp.zeros_like(decay), jnp.zeros_like(decay))
            _, (nf, df) = lax.scan(step, init, (ekv_t, ek_t))
            _, (nb, db) = lax.scan(step, init, (ekv_t, ek_t), reverse=True)
            nf = jnp.swapaxes(nf, 0, 1)
            df = jnp.swapaxes(df, 0, 1)
            nb = jnp.swapaxes(nb, 0, 1)
            db = jnp.swapaxes(db, 0, 1)
            euk = jnp.exp(jnp.minimum(u.astype(jnp.float32)[None, None, :] + kf, 30.0))
            num = nf + nb - ekv + euk * vf
            den = df + db - ek + euk
            base = jax.nn.sigmoid(r.astype(jnp.float32)) * (num / jnp.maximum(den, 1e-08))
            out = base * (0.8 + 0.2 * tf)
            return out.astype(r.dtype)
        return _bi_wkv(r, k, v, w, u, time_emb)

    def _L0_attn_ref(x, qkv_w, qkv_norm_w, proj_w, proj_norm_w, norm_w, s):
        import jax, jax.numpy as jnp
        import numpy as np
        DIM = 256
        HEADS = 16
        HEAD_DIM = DIM // HEADS
        CHUNK = 128
        B, N = (4, 256)

        def _rmsnorm(x, w, eps):
            return x * jax.lax.rsqrt(jnp.mean(x * x, axis=-1, keepdims=True) + eps) * w

        def _weight_quant(w):
            scale = 1.0 / jnp.clip(jnp.mean(jnp.abs(w)), 1e-05, None)
            q = jnp.clip(jnp.round(w * scale), -1.0, 1.0) / scale
            return w + jax.lax.stop_gradient(q - w)

        def _forward(x, qkv_w, qkv_norm_w, proj_w, proj_norm_w, norm_w, s):
            Bb, Nn, C = x.shape
            H, D, T = (HEADS, HEAD_DIM, CHUNK)
            nc = Nn // T
            eps = jnp.finfo(x.dtype).eps
            scale = D ** (-0.5)
            h = _rmsnorm(x, qkv_norm_w, eps)
            qkv = h @ _weight_quant(qkv_w).T
            qkv = qkv.reshape(Bb, Nn, 3, H, D)
            q, k, v = (qkv[:, :, 0], qkv[:, :, 1], qkv[:, :, 2])

            def chunks(t):
                return t.reshape(Bb, nc, T, H, D).transpose(1, 0, 3, 2, 4)
            qc, kc, vc = (chunks(q), chunks(k), chunks(v))
            tt = jnp.arange(T, dtype=x.dtype)
            lam_t = jnp.exp(-s[:, None] * tt)
            lam_rev = jnp.exp(-s[:, None] * (T - tt))
            diff = tt[:, None] - tt[None, :]
            mask = jnp.where(diff >= 0, jnp.exp(-s[:, None, None] * diff), 0.0)
            lam_T = jnp.exp(-s * T)[:, None, None]

            def step(S, qkv_c):
                qi, ki, vi = qkv_c
                scores = jnp.einsum('bhtd,bhsd,hts->bhts', qi, ki, mask)
                intra = jnp.einsum('bhts,bhsd->bhtd', scores, vi)
                cross = jnp.einsum('bhtd,ht,bhde->bhte', qi, lam_t, S)
                o = scale * (intra + cross)
                kv = jnp.einsum('bhtd,ht,bhte->bhde', ki, lam_rev, vi)
                return (lam_T * S + kv, o)
            S0 = jnp.zeros((Bb, H, D, D), x.dtype)
            _, outs = jax.lax.scan(step, S0, (qc, kc, vc))
            out = outs.transpose(1, 0, 3, 2, 4).reshape(Bb, Nn, C)
            out = _rmsnorm(out, norm_w, 1e-06)
            out = _rmsnorm(out, proj_norm_w, eps) @ _weight_quant(proj_w).T
            return out
        return _forward(x, qkv_w, qkv_norm_w, proj_w, proj_norm_w, norm_w, s)

    def _L0_cond2_ref(r, k, v, w, u, time_emb):
        import jax, jax.numpy as jnp
        from jax import lax
        import numpy as np
        B, T, C, TD = (8, 256, 256, 64)

        def _bi_wkv(r, k, v, w, u, time_emb):
            tf = jax.nn.sigmoid(jnp.sum(time_emb, axis=-1))[:, None, None]
            decay = jnp.exp(-jnp.exp(w.astype(jnp.float32)))[None, :] * (0.5 + 0.5 * tf[:, :, 0])
            kf = k.astype(jnp.float32)
            vf = v.astype(jnp.float32)
            ek = jnp.exp(jnp.minimum(kf, 30.0))
            ekv = ek * vf

            def step(carry, x):
                a, b = carry
                ekv_t, ek_t = x
                a = a * decay + ekv_t
                b = b * decay + ek_t
                return ((a, b), (a, b))
            ekv_t = jnp.swapaxes(ekv, 0, 1)
            ek_t = jnp.swapaxes(ek, 0, 1)
            init = (jnp.zeros_like(decay), jnp.zeros_like(decay))
            _, (nf, df) = lax.scan(step, init, (ekv_t, ek_t))
            _, (nb, db) = lax.scan(step, init, (ekv_t, ek_t), reverse=True)
            nf = jnp.swapaxes(nf, 0, 1)
            df = jnp.swapaxes(df, 0, 1)
            nb = jnp.swapaxes(nb, 0, 1)
            db = jnp.swapaxes(db, 0, 1)
            euk = jnp.exp(jnp.minimum(u.astype(jnp.float32)[None, None, :] + kf, 30.0))
            num = nf + nb - ekv + euk * vf
            den = df + db - ek + euk
            base = jax.nn.sigmoid(r.astype(jnp.float32)) * (num / jnp.maximum(den, 1e-08))
            out = base * (0.8 + 0.2 * tf)
            return out.astype(r.dtype)
        return _bi_wkv(r, k, v, w, u, time_emb)

    def _L0_ffn_ref(hidden_states, router_w, w_gate_up, w_down, shared_gate_up, shared_down):
        import jax, jax.numpy as jnp
        import numpy as np
        B, S, D, F, E, K = (2, 256, 256, 512, 8, 1)

        def _silu_mul(gu):
            g, u = jnp.split(gu, 2, axis=-1)
            return jax.nn.silu(g) * u

        def _moe_forward(hidden_states, router_w, w_gate_up, w_down, shared_gate_up, shared_down, top_k=K):
            b, s, d = hidden_states.shape
            x = hidden_states.reshape(-1, d)
            router_logits = x @ router_w.T
            topk_vals, topk_ids = jax.lax.top_k(router_logits, top_k)
            gate = jax.nn.sigmoid(topk_vals.astype(jnp.float32)).astype(x.dtype)
            xs = (x[:, None, :] * gate[:, :, None]).reshape(-1, d)
            ids_flat = topk_ids.reshape(-1)
            n_experts = w_gate_up.shape[0]

            def body(acc, inp):
                wg, wd, e = inp
                h = _silu_mul(xs @ wg)
                o = h @ wd
                mask = (ids_flat == e)[:, None]
                return (acc + jnp.where(mask, o, jnp.zeros((), o.dtype)), None)
            acc0 = jnp.zeros_like(xs)
            routed, _ = jax.lax.scan(body, acc0, (w_gate_up, w_down, jnp.arange(n_experts)))
            routed = routed.reshape(-1, top_k, d).sum(1)
            shared = _silu_mul(x @ shared_gate_up) @ shared_down
            return (routed + shared).reshape(b, s, d)
        return _moe_forward(hidden_states, router_w, w_gate_up, w_down, shared_gate_up, shared_down)

    def _L1_cond_ref(r, k, v, w, u, time_emb):
        import jax, jax.numpy as jnp
        from jax import lax
        import numpy as np
        B, T, C, TD = (8, 256, 256, 64)

        def _bi_wkv(r, k, v, w, u, time_emb):
            tf = jax.nn.sigmoid(jnp.sum(time_emb, axis=-1))[:, None, None]
            decay = jnp.exp(-jnp.exp(w.astype(jnp.float32)))[None, :] * (0.5 + 0.5 * tf[:, :, 0])
            kf = k.astype(jnp.float32)
            vf = v.astype(jnp.float32)
            ek = jnp.exp(jnp.minimum(kf, 30.0))
            ekv = ek * vf

            def step(carry, x):
                a, b = carry
                ekv_t, ek_t = x
                a = a * decay + ekv_t
                b = b * decay + ek_t
                return ((a, b), (a, b))
            ekv_t = jnp.swapaxes(ekv, 0, 1)
            ek_t = jnp.swapaxes(ek, 0, 1)
            init = (jnp.zeros_like(decay), jnp.zeros_like(decay))
            _, (nf, df) = lax.scan(step, init, (ekv_t, ek_t))
            _, (nb, db) = lax.scan(step, init, (ekv_t, ek_t), reverse=True)
            nf = jnp.swapaxes(nf, 0, 1)
            df = jnp.swapaxes(df, 0, 1)
            nb = jnp.swapaxes(nb, 0, 1)
            db = jnp.swapaxes(db, 0, 1)
            euk = jnp.exp(jnp.minimum(u.astype(jnp.float32)[None, None, :] + kf, 30.0))
            num = nf + nb - ekv + euk * vf
            den = df + db - ek + euk
            base = jax.nn.sigmoid(r.astype(jnp.float32)) * (num / jnp.maximum(den, 1e-08))
            out = base * (0.8 + 0.2 * tf)
            return out.astype(r.dtype)
        return _bi_wkv(r, k, v, w, u, time_emb)

    def _L1_attn_ref(x, global_tokens, ln_scale, ln_bias, Wq, Wk, Wv, Wo):
        import jax, jax.numpy as jnp
        import numpy as np
        D_MODEL = 256
        N_HEADS = 16
        HEAD_DIM = D_MODEL // N_HEADS
        WINDOW = 32
        G = 16
        LN_EPS = 1e-05

        def _sparse_mask(T, dtype=jnp.float32):
            i = jnp.arange(T)[:, None]
            j = jnp.arange(T)[None, :]
            band = (j <= i) & (j >= i - WINDOW + 1)
            neg = jnp.array(-jnp.inf, dtype)
            mask = jnp.full((G + T, G + T), neg, dtype)
            mask = mask.at[:G, :].set(0.0)
            mask = mask.at[:, :G].set(0.0)
            mask = mask.at[G:, G:].set(jnp.where(band, jnp.array(0.0, dtype), neg))
            return mask
        B, T, D = x.shape
        residual = x
        mu = jnp.mean(x, axis=-1, keepdims=True)
        var = jnp.mean(jnp.square(x - mu), axis=-1, keepdims=True)
        xn = (x - mu) * jax.lax.rsqrt(var + LN_EPS) * ln_scale + ln_bias
        g = jnp.broadcast_to(global_tokens, (B, G, D))
        xg = jnp.concatenate([g, xn], axis=1)

        def proj(W):
            return (xg @ W.T).reshape(B, G + T, N_HEADS, HEAD_DIM)
        Q, K, V = (proj(Wq), proj(Wk), proj(Wv))
        scale = HEAD_DIM ** (-0.5)
        scores = jnp.einsum('bqhd,bkhd->bhqk', Q, K) * scale
        scores = scores + _sparse_mask(T, scores.dtype)[None, None]
        attn = jax.nn.softmax(scores, axis=-1)
        out = jnp.einsum('bhqk,bkhd->bqhd', attn, V).reshape(B, G + T, D)
        out = out[:, G:] @ Wo.T
        return out + residual

    def _L1_cond2_ref(r, k, v, w, u, time_emb):
        import jax, jax.numpy as jnp
        from jax import lax
        import numpy as np
        B, T, C, TD = (8, 256, 256, 64)

        def _bi_wkv(r, k, v, w, u, time_emb):
            tf = jax.nn.sigmoid(jnp.sum(time_emb, axis=-1))[:, None, None]
            decay = jnp.exp(-jnp.exp(w.astype(jnp.float32)))[None, :] * (0.5 + 0.5 * tf[:, :, 0])
            kf = k.astype(jnp.float32)
            vf = v.astype(jnp.float32)
            ek = jnp.exp(jnp.minimum(kf, 30.0))
            ekv = ek * vf

            def step(carry, x):
                a, b = carry
                ekv_t, ek_t = x
                a = a * decay + ekv_t
                b = b * decay + ek_t
                return ((a, b), (a, b))
            ekv_t = jnp.swapaxes(ekv, 0, 1)
            ek_t = jnp.swapaxes(ek, 0, 1)
            init = (jnp.zeros_like(decay), jnp.zeros_like(decay))
            _, (nf, df) = lax.scan(step, init, (ekv_t, ek_t))
            _, (nb, db) = lax.scan(step, init, (ekv_t, ek_t), reverse=True)
            nf = jnp.swapaxes(nf, 0, 1)
            df = jnp.swapaxes(df, 0, 1)
            nb = jnp.swapaxes(nb, 0, 1)
            db = jnp.swapaxes(db, 0, 1)
            euk = jnp.exp(jnp.minimum(u.astype(jnp.float32)[None, None, :] + kf, 30.0))
            num = nf + nb - ekv + euk * vf
            den = df + db - ek + euk
            base = jax.nn.sigmoid(r.astype(jnp.float32)) * (num / jnp.maximum(den, 1e-08))
            out = base * (0.8 + 0.2 * tf)
            return out.astype(r.dtype)
        return _bi_wkv(r, k, v, w, u, time_emb)

    def _L1_ffn_ref(hidden_states, Wg, W1, W2, W3, A1, B1, A2, B2, A3, B3):
        import jax, jax.numpy as jnp
        import numpy as np
        B, S, H, F, E, R, K = (2, 128, 256, 896, 8, 32, 2)

        def _gather_slot(a_all, e):
            return jnp.take_along_axis(a_all, e[:, None, None], axis=1)[:, 0]
        b, s, h = hidden_states.shape
        x = hidden_states.reshape(-1, h)
        nE = Wg.shape[0]
        logits = x @ Wg.T
        probs = jax.nn.softmax(logits.astype(jnp.float32), axis=-1)
        rw, sel = jax.lax.top_k(probs, K)
        rw = (rw / rw.sum(axis=-1, keepdims=True)).astype(x.dtype)
        base1 = x @ W1.T
        base3 = x @ W3.T
        a1_all = jnp.einsum('th,erh->ter', x, A1)
        a3_all = jnp.einsum('th,erh->ter', x, A3)
        out = jnp.zeros_like(x)
        for k in range(K):
            e = sel[:, k]
            mask = jax.nn.one_hot(e, nE, dtype=x.dtype)
            a1 = _gather_slot(a1_all, e)
            a3 = _gather_slot(a3_all, e)
            lora1 = jnp.einsum('ter,efr->tf', mask[:, :, None] * a1[:, None, :], B1)
            lora3 = jnp.einsum('ter,efr->tf', mask[:, :, None] * a3[:, None, :], B3)
            x1 = base1 + lora1
            x3 = base3 + lora3
            x2 = jax.nn.silu(x1) * x3
            down = x2 @ W2.T
            a2_all = jnp.einsum('tf,erf->ter', x2, A2)
            a2 = _gather_slot(a2_all, e)
            lora2 = jnp.einsum('ter,ehr->th', mask[:, :, None] * a2[:, None, :], B2)
            out = out + (down + lora2) * rw[:, k:k + 1]
        return out.reshape(b, s, h)

    def _L2_cond_ref(r, k, v, w, u, time_emb):
        import jax, jax.numpy as jnp
        from jax import lax
        import numpy as np
        B, T, C, TD = (8, 256, 256, 64)

        def _bi_wkv(r, k, v, w, u, time_emb):
            tf = jax.nn.sigmoid(jnp.sum(time_emb, axis=-1))[:, None, None]
            decay = jnp.exp(-jnp.exp(w.astype(jnp.float32)))[None, :] * (0.5 + 0.5 * tf[:, :, 0])
            kf = k.astype(jnp.float32)
            vf = v.astype(jnp.float32)
            ek = jnp.exp(jnp.minimum(kf, 30.0))
            ekv = ek * vf

            def step(carry, x):
                a, b = carry
                ekv_t, ek_t = x
                a = a * decay + ekv_t
                b = b * decay + ek_t
                return ((a, b), (a, b))
            ekv_t = jnp.swapaxes(ekv, 0, 1)
            ek_t = jnp.swapaxes(ek, 0, 1)
            init = (jnp.zeros_like(decay), jnp.zeros_like(decay))
            _, (nf, df) = lax.scan(step, init, (ekv_t, ek_t))
            _, (nb, db) = lax.scan(step, init, (ekv_t, ek_t), reverse=True)
            nf = jnp.swapaxes(nf, 0, 1)
            df = jnp.swapaxes(df, 0, 1)
            nb = jnp.swapaxes(nb, 0, 1)
            db = jnp.swapaxes(db, 0, 1)
            euk = jnp.exp(jnp.minimum(u.astype(jnp.float32)[None, None, :] + kf, 30.0))
            num = nf + nb - ekv + euk * vf
            den = df + db - ek + euk
            base = jax.nn.sigmoid(r.astype(jnp.float32)) * (num / jnp.maximum(den, 1e-08))
            out = base * (0.8 + 0.2 * tf)
            return out.astype(r.dtype)
        return _bi_wkv(r, k, v, w, u, time_emb)

    def _L2_attn_ref(x, w_qkv, w_o, q_norm_w, q_norm_b, k_norm_w, k_norm_b):
        import math
        import jax, jax.numpy as jnp
        import numpy as np
        H, KV, D = (16, 4, 128)
        HID = 256
        ROPE_BASE = 1000000.0
        EPS = 1e-06

        def _layernorm(x, w, b):
            mu = jnp.mean(x, axis=-1, keepdims=True)
            xc = x - mu
            var = jnp.mean(xc * xc, axis=-1, keepdims=True)
            return xc * jax.lax.rsqrt(var + EPS) * w + b

        def _rope(x, cos, sin):
            xr, xi = (x[..., 0::2], x[..., 1::2])
            c, s = (cos[None, None], sin[None, None])
            out = jnp.stack([xr * c - xi * s, xr * s + xi * c], axis=-1)
            return out.reshape(x.shape)
        B, S, _ = x.shape
        qkv = x @ w_qkv.T
        qg, k, v = jnp.split(qkv, [2 * H * D, 2 * H * D + KV * D], axis=-1)
        q, gate = jnp.split(qg, 2, axis=-1)
        q = q.reshape(B, S, H, D).transpose(0, 2, 1, 3)
        k = k.reshape(B, S, KV, D).transpose(0, 2, 1, 3)
        v = v.reshape(B, S, KV, D).transpose(0, 2, 1, 3)
        q = _layernorm(q, q_norm_w, q_norm_b)
        k = _layernorm(k, k_norm_w, k_norm_b)
        inv = 1.0 / ROPE_BASE ** (jnp.arange(0, D, 2, dtype=jnp.float32) / D)
        freqs = jnp.outer(jnp.arange(S, dtype=jnp.float32), inv)
        cos, sin = (jnp.cos(freqs), jnp.sin(freqs))
        q = _rope(q, cos, sin)
        k = _rope(k, cos, sin)
        rep = H // KV
        k = jnp.repeat(k, rep, axis=1)
        v = jnp.repeat(v, rep, axis=1)
        scores = jnp.einsum('bhqd,bhkd->bhqk', q, k) / math.sqrt(D)
        causal = jnp.tril(jnp.ones((S, S), bool))
        scores = jnp.where(causal[None, None], scores, -jnp.inf)
        attn = jax.nn.softmax(scores, axis=-1)
        out = jnp.einsum('bhqk,bhkd->bhqd', attn, v)
        out = out.transpose(0, 2, 1, 3).reshape(B, S, H * D)
        out = out * jax.nn.sigmoid(gate)
        return out @ w_o.T

    def _L2_cond2_ref(r, k, v, w, u, time_emb):
        import jax, jax.numpy as jnp
        from jax import lax
        import numpy as np
        B, T, C, TD = (8, 256, 256, 64)

        def _bi_wkv(r, k, v, w, u, time_emb):
            tf = jax.nn.sigmoid(jnp.sum(time_emb, axis=-1))[:, None, None]
            decay = jnp.exp(-jnp.exp(w.astype(jnp.float32)))[None, :] * (0.5 + 0.5 * tf[:, :, 0])
            kf = k.astype(jnp.float32)
            vf = v.astype(jnp.float32)
            ek = jnp.exp(jnp.minimum(kf, 30.0))
            ekv = ek * vf

            def step(carry, x):
                a, b = carry
                ekv_t, ek_t = x
                a = a * decay + ekv_t
                b = b * decay + ek_t
                return ((a, b), (a, b))
            ekv_t = jnp.swapaxes(ekv, 0, 1)
            ek_t = jnp.swapaxes(ek, 0, 1)
            init = (jnp.zeros_like(decay), jnp.zeros_like(decay))
            _, (nf, df) = lax.scan(step, init, (ekv_t, ek_t))
            _, (nb, db) = lax.scan(step, init, (ekv_t, ek_t), reverse=True)
            nf = jnp.swapaxes(nf, 0, 1)
            df = jnp.swapaxes(df, 0, 1)
            nb = jnp.swapaxes(nb, 0, 1)
            db = jnp.swapaxes(db, 0, 1)
            euk = jnp.exp(jnp.minimum(u.astype(jnp.float32)[None, None, :] + kf, 30.0))
            num = nf + nb - ekv + euk * vf
            den = df + db - ek + euk
            base = jax.nn.sigmoid(r.astype(jnp.float32)) * (num / jnp.maximum(den, 1e-08))
            out = base * (0.8 + 0.2 * tf)
            return out.astype(r.dtype)
        return _bi_wkv(r, k, v, w, u, time_emb)

    def _L2_ffn_ref(x, w_gate_up, w_down):
        import jax, jax.numpy as jnp
        import numpy as np
        QMAX = 127.0
        EPS = 1e-08

        def _quant_dequant(v, axis):
            scale = jnp.max(jnp.abs(v), axis=axis, keepdims=True) / QMAX
            scale = jnp.maximum(scale, EPS)
            q = jnp.clip(jnp.round(v / scale), -QMAX, QMAX)
            return q * scale

        def _ste(v, axis):
            return v + jax.lax.stop_gradient(_quant_dequant(v, axis) - v)
        I = w_down.shape[1]
        xq = _ste(x, axis=-1)
        w1q = _ste(w_gate_up, axis=-1)
        gate_up = jnp.einsum('bsh,oh->bso', xq, w1q)
        gate, up = (gate_up[..., :I], gate_up[..., I:])
        h = jax.nn.silu(gate) * up
        hq = _ste(h, axis=-1)
        w2q = _ste(w_down, axis=-1)
        return jnp.einsum('bsi,oi->bso', hq, w2q)

    def _L3_cond_ref(r, k, v, w, u, time_emb):
        import jax, jax.numpy as jnp
        from jax import lax
        import numpy as np
        B, T, C, TD = (8, 256, 256, 64)

        def _bi_wkv(r, k, v, w, u, time_emb):
            tf = jax.nn.sigmoid(jnp.sum(time_emb, axis=-1))[:, None, None]
            decay = jnp.exp(-jnp.exp(w.astype(jnp.float32)))[None, :] * (0.5 + 0.5 * tf[:, :, 0])
            kf = k.astype(jnp.float32)
            vf = v.astype(jnp.float32)
            ek = jnp.exp(jnp.minimum(kf, 30.0))
            ekv = ek * vf

            def step(carry, x):
                a, b = carry
                ekv_t, ek_t = x
                a = a * decay + ekv_t
                b = b * decay + ek_t
                return ((a, b), (a, b))
            ekv_t = jnp.swapaxes(ekv, 0, 1)
            ek_t = jnp.swapaxes(ek, 0, 1)
            init = (jnp.zeros_like(decay), jnp.zeros_like(decay))
            _, (nf, df) = lax.scan(step, init, (ekv_t, ek_t))
            _, (nb, db) = lax.scan(step, init, (ekv_t, ek_t), reverse=True)
            nf = jnp.swapaxes(nf, 0, 1)
            df = jnp.swapaxes(df, 0, 1)
            nb = jnp.swapaxes(nb, 0, 1)
            db = jnp.swapaxes(db, 0, 1)
            euk = jnp.exp(jnp.minimum(u.astype(jnp.float32)[None, None, :] + kf, 30.0))
            num = nf + nb - ekv + euk * vf
            den = df + db - ek + euk
            base = jax.nn.sigmoid(r.astype(jnp.float32)) * (num / jnp.maximum(den, 1e-08))
            out = base * (0.8 + 0.2 * tf)
            return out.astype(r.dtype)
        return _bi_wkv(r, k, v, w, u, time_emb)

    def _L3_attn_ref(x, norm_w, W_skip, W_in, conv_w, conv_b, Wd1, Wd2, bd2, WB, WC, A_log, W_D, W_out):
        import jax, jax.numpy as jnp
        import numpy as np
        B, L, D = (4, 256, 256)
        E, N, DT, DC = (512, 16, 128, 4)
        EPS = 1e-05
        xn = x * jax.lax.rsqrt(jnp.mean(x * x, axis=-1, keepdims=True) + EPS) * norm_w
        skip = xn @ W_skip.T
        u = xn @ W_in.T
        uc = jax.lax.conv_general_dilated(u.transpose(0, 2, 1), conv_w, (1,), [(DC - 1, 0)], dimension_numbers=('NCH', 'OIH', 'NCH'), feature_group_count=E)
        u = jax.nn.silu(uc.transpose(0, 2, 1) + conv_b)
        delta = jax.nn.softplus(u @ Wd1.T @ Wd2.T + bd2)
        Bt = u @ WB.T
        Ct = u @ WC.T
        A = -jnp.exp(A_log)

        def step(h, inps):
            d_l, b_l, c_l, u_l = inps
            h = jnp.exp(d_l[..., None] * A) * h + (d_l * u_l)[..., None] * b_l[:, None, :]
            y_l = jnp.einsum('ben,bn->be', h, c_l)
            return (h, y_l)
        h0 = jnp.zeros((x.shape[0], E, N), u.dtype)
        _, ys = jax.lax.scan(step, h0, (delta.transpose(1, 0, 2), Bt.transpose(1, 0, 2), Ct.transpose(1, 0, 2), u.transpose(1, 0, 2)))
        y = ys.transpose(1, 0, 2)
        y = (y + u * W_D) * jax.nn.silu(skip)
        return y @ W_out.T

    def _L3_cond2_ref(r, k, v, w, u, time_emb):
        import jax, jax.numpy as jnp
        from jax import lax
        import numpy as np
        B, T, C, TD = (8, 256, 256, 64)

        def _bi_wkv(r, k, v, w, u, time_emb):
            tf = jax.nn.sigmoid(jnp.sum(time_emb, axis=-1))[:, None, None]
            decay = jnp.exp(-jnp.exp(w.astype(jnp.float32)))[None, :] * (0.5 + 0.5 * tf[:, :, 0])
            kf = k.astype(jnp.float32)
            vf = v.astype(jnp.float32)
            ek = jnp.exp(jnp.minimum(kf, 30.0))
            ekv = ek * vf

            def step(carry, x):
                a, b = carry
                ekv_t, ek_t = x
                a = a * decay + ekv_t
                b = b * decay + ek_t
                return ((a, b), (a, b))
            ekv_t = jnp.swapaxes(ekv, 0, 1)
            ek_t = jnp.swapaxes(ek, 0, 1)
            init = (jnp.zeros_like(decay), jnp.zeros_like(decay))
            _, (nf, df) = lax.scan(step, init, (ekv_t, ek_t))
            _, (nb, db) = lax.scan(step, init, (ekv_t, ek_t), reverse=True)
            nf = jnp.swapaxes(nf, 0, 1)
            df = jnp.swapaxes(df, 0, 1)
            nb = jnp.swapaxes(nb, 0, 1)
            db = jnp.swapaxes(db, 0, 1)
            euk = jnp.exp(jnp.minimum(u.astype(jnp.float32)[None, None, :] + kf, 30.0))
            num = nf + nb - ekv + euk * vf
            den = df + db - ek + euk
            base = jax.nn.sigmoid(r.astype(jnp.float32)) * (num / jnp.maximum(den, 1e-08))
            out = base * (0.8 + 0.2 * tf)
            return out.astype(r.dtype)
        return _bi_wkv(r, k, v, w, u, time_emb)

    def _L3_ffn_ref(x, rg_w, ru_w, extra_scale, extra_bias, Wg, Wu, Wd, Sg, Su, Sd):
        import jax, jax.numpy as jnp
        import numpy as np
        from jax import lax
        H = 256
        I = 176
        E = 16
        K = 4
        ISH = 2 * I
        B, S = (4, 256)

        def _router(xf, rg_w, ru_w, extra_scale, extra_bias):
            g = xf @ rg_w.T
            u = xf @ ru_w.T
            scores = jnp.abs(u * jax.nn.silu(g))
            probs = jax.nn.softmax(scores.astype(jnp.float32), axis=-1)
            biased = probs + extra_bias[None, :]
            _, idx = lax.top_k(biased, K)
            orig = 1.0 + probs * extra_scale[None, :]
            w = jnp.take_along_axis(orig, idx, axis=1).astype(xf.dtype)
            return (w, idx)
        shape = x.shape
        xf = x.reshape(-1, H)
        w, idx = _router(xf, rg_w, ru_w, extra_scale, extra_bias)
        coeff = jnp.einsum('tk,tke->te', w, jax.nn.one_hot(idx, E, dtype=w.dtype))

        def step(y, ew):
            wg, wu, wd, c = ew
            h = jax.nn.silu(xf @ wg.T) * (xf @ wu.T)
            return (y + h @ wd.T * c[:, None], None)
        y0 = jnp.zeros_like(xf)
        y, _ = lax.scan(step, y0, (Wg, Wu, Wd, coeff.T))
        z = jax.nn.silu(xf @ Sg.T) * (xf @ Su.T) @ Sd.T
        return (y + z).reshape(shape)
    x = x + _L0_attn_ref(_L0_cond_ref(x, fside_BxSxS_0, fside_BxSxS_0, L0_cond_w, L0_cond_u, cond_512), L0_attn_qkv_w, L0_attn_qkv_norm_w, L0_attn_proj_w, L0_attn_proj_norm_w, L0_attn_norm_w, L0_attn_s)
    x = x + _L0_ffn_ref(_L0_cond2_ref(x, fside_BxSxS_0, fside_BxSxS_0, L0_cond2_w, L0_cond2_u, cond_512), L0_ffn_router_w, L0_ffn_w_gate_up, L0_ffn_w_down, L0_ffn_shared_gate_up, L0_ffn_shared_down)
    x = x + _L1_attn_ref(_L1_cond_ref(x, fside_BxSxS_0, fside_BxSxS_0, L1_cond_w, L1_cond_u, cond_512), L1_attn_global_tokens, L1_attn_ln_scale, L1_attn_ln_bias, L1_attn_Wq, L1_attn_Wk, L1_attn_Wv, L1_attn_Wo)
    x = x + _L1_ffn_ref(_L1_cond2_ref(x, fside_BxSxS_0, fside_BxSxS_0, L1_cond2_w, L1_cond2_u, cond_512), L1_ffn_Wg, L1_ffn_W1, L1_ffn_W2, L1_ffn_W3, L1_ffn_A1, L1_ffn_B1, L1_ffn_A2, L1_ffn_B2, L1_ffn_A3, L1_ffn_B3)
    x = x + _L2_attn_ref(_L2_cond_ref(x, fside_BxSxS_0, fside_BxSxS_0, L2_cond_w, L2_cond_u, cond_512), L2_attn_w_qkv, L2_attn_w_o, L2_attn_q_norm_w, L2_attn_q_norm_b, L2_attn_k_norm_w, L2_attn_k_norm_b)
    x = x + _L2_ffn_ref(_L2_cond2_ref(x, fside_BxSxS_0, fside_BxSxS_0, L2_cond2_w, L2_cond2_u, cond_512), L2_ffn_w_gate_up, L2_ffn_w_down)
    x = x + _L3_attn_ref(_L3_cond_ref(x, fside_BxSxS_0, fside_BxSxS_0, L3_cond_w, L3_cond_u, cond_512), L3_attn_norm_w, L3_attn_W_skip, L3_attn_W_in, L3_attn_conv_w, L3_attn_conv_b, L3_attn_Wd1, L3_attn_Wd2, L3_attn_bd2, L3_attn_WB, L3_attn_WC, L3_attn_A_log, L3_attn_W_D, L3_attn_W_out)
    x = x + _L3_ffn_ref(_L3_cond2_ref(x, fside_BxSxS_0, fside_BxSxS_0, L3_cond2_w, L3_cond2_u, cond_512), L3_ffn_rg_w, L3_ffn_ru_w, L3_ffn_extra_scale, L3_ffn_extra_bias, L3_ffn_Wg, L3_ffn_Wu, L3_ffn_Wd, L3_ffn_Sg, L3_ffn_Su, L3_ffn_Sd)
    return x

_drawn_inputs = setup_inputs


def setup_inputs(seed=0):
    import zlib

    import numpy as np

    out = dict(_drawn_inputs(seed))
    spreads = {'L0_attn_qkv_norm_w': (1.0, 0.2),
     'L0_attn_proj_norm_w': (1.0, 0.2),
     'L0_attn_norm_w': (1.0, 0.2),
     'L0_attn_s': (0.019999999552965164, 0.2),
     'L1_attn_ln_scale': (1.0, 0.2),
     'L1_attn_ln_bias': (0.0, 0.1),
     'L2_attn_q_norm_w': (1.0, 0.2),
     'L2_attn_q_norm_b': (0.0, 0.1),
     'L2_attn_k_norm_w': (1.0, 0.2),
     'L2_attn_k_norm_b': (0.0, 0.1),
     'L3_attn_norm_w': (1.0, 0.2),
     'L3_attn_conv_b': (0.0, 0.1),
     'L3_attn_bd2': (0.0, 0.1),
     'L3_attn_W_D': (1.0, 0.2),
     'L3_ffn_extra_scale': (0.0, 0.1),
     'L3_ffn_extra_bias': (0.0, 0.1)}
    factors = {}
    for name, (base, spread) in spreads.items():
        noise = np.random.default_rng([zlib.crc32(name.encode()), seed]).standard_normal(out[name].shape)
        drawn = base * np.exp(spread * noise) if base else spread * noise
        out[name] = jnp.asarray(drawn.astype(out[name].dtype))
    for name, factor in factors.items():
        out[name] = (out[name] * factor).astype(out[name].dtype)
    return out
```

```python
from concourse import mybir

F32 = mybir.dt.float32
BF16 = mybir.dt.bfloat16
ALU = mybir.AluOpType
ACT = mybir.ActivationFunctionType
AX = mybir.AxisListType.X

P = 128
C = 256
CT = C // P
NB, T = 4, 256
TOK = NB * T
TT = TOK // P
HALF = 512
NH = TOK // HALF
NCOND = 8
ROUND = 1.5 * 2.0 ** 23
BIG = 1e30
STOP = 99


class Counter:

    def __init__(self, nc, name):
        self.sem, self.n, self.name = nc.alloc_semaphore(name), 0, name
        self.base, self.per = 0, 0


class Token:

    def __init__(self, counter, n, loop, back=0):
        self.counter, self.n, self.loop, self.back = counter, n, loop, back


class Loop:
    def __init__(self, count):
        self.count, self.var, self.dry, self.done = count, None, True, False
        self.base, self.per = {}, {}


class Machine:
    def __init__(self, nc):
        self.nc, self.loop, self.counters, self.free = nc, None, [], {}
        self.pe, self.act, self.dve = Lane(self, nc.tensor, "pe"), Lane(self, nc.scalar, "act"), Lane(self, nc.vector, "dve")
        self.pool, self.sp = Lane(self, nc.gpsimd, "pool"), Lane(self, nc.sync, "sp")
        self.lanes = [self.pe, self.act, self.dve, self.pool]

    def counter(self, name):
        c = Counter(self.nc, name)
        self.counters.append(c)
        if self.loop is not None:
            self.loop.base[c] = 0
        return c

    def release(self, name, *tokens):
        self.free[name] = tokens

    def freed(self, name):
        return self.free.get(name, ())

    def fence(self, sp=True):
        for lane in self.lanes + ([self.sp] if sp else []):
            for other in self.lanes:
                lane.wait(Token(other.counter, other.counter.n, None))
        self.free = {}

    def run_loop(self, count, body):
        assert self.loop is None
        self.fence()
        loop = Loop(count)
        for c in self.counters:
            loop.base[c] = c.n
            c.n = 0
        self.loop = loop
        for lane in self.lanes + [self.sp]:
            lane.local = {}
        body(0)
        last = {k: tuple(Token(t.counter, t.n, loop, 1) for t in v) for k, v in self.free.items()}
        for c in self.counters:
            loop.per[c] = c.n
            c.n = 0
        for lane in self.lanes:
            c = lane.counter
            short = loop.per[c] + 1 - loop.base[c]
            if short > 0:
                lane.eng.sem_inc(c.sem, short)
                loop.base[c] += short
        for lane in self.lanes + [self.sp]:
            lane.local = {}
        self.free, loop.dry = last, False
        with self.nc.Fori(0, count) as i:
            loop.var = i
            body(i)
        for c in self.counters:
            assert c.n == loop.per[c], c.name
            c.n = loop.base[c] + count * loop.per[c]
        self.loop, loop.done = None, True
        self.fence()


class Lane:

    def __init__(self, m, eng, name):
        self.m, self.eng, self.counter = m, eng, m.counter("done_" + name)
        self.known, self.local = {}, {}

    def wait(self, t):
        if t is None:
            return
        c, loop = t.counter, t.loop
        if loop is not None and not loop.done:
            assert loop is self.m.loop
            v = t.n - t.back * 10 ** 6
            if self.local.get(c, -10 ** 9) >= v:
                return
            self.local[c] = v
            if not loop.dry:
                off = loop.base[c] + t.n - t.back * loop.per[c]
                self.eng.wait_ge(c.sem, loop.var * loop.per[c] + off)
            return
        v = t.n if loop is None else loop.base[c] + (loop.count - 1) * loop.per[c] + t.n
        if self.known.get(c, 0) >= v or v == 0:
            return
        if self.m.loop is not None:
            assert v <= self.m.loop.base[c]
            if self.m.loop.dry:
                return
        else:
            self.known[c] = v
        self.eng.wait_ge(c.sem, v)

    def issue(self, build, *waits, count=1, counter=None):
        for t in waits:
            self.wait(t)
        loop = self.m.loop
        if loop is None or not loop.dry:
            ins = build(self.eng)
            if count:
                ins.then_inc((counter or self.counter).sem, count)
        c = counter or self.counter
        c.n += count
        return Token(c, c.n, loop)

    def do(self, build, *waits):
        return self.issue(build, *waits)

    def quiet(self, build, *waits):
        return self.issue(build, *waits, count=0)

    def here(self):
        return Token(self.counter, self.counter.n, self.m.loop)


def build_program(nc, d, out):
    m = Machine(nc)
    PE, A, V, G, SP = m.pe, m.act, m.dve, m.pool, m.sp

    def sb(name, shape, dt=F32):
        return nc.alloc_sbuf_tensor(name, shape, dt)

    banks = [nc.alloc_psum_tensor(f"bank{i}", [P, 512], F32) for i in range(8)]

    class Phase:

        def __init__(self):
            self.open = []

        def __enter__(self):
            return self

        def __call__(self, name, shape, dt=F32):
            g = nc.sbuf_tensor(name, shape, dt)
            self.open.append(g)
            return g.__enter__()

        def __exit__(self, *e):
            for g in reversed(self.open):
                g.__exit__(None, None, None)
            m.fence()

    def load(counter, dst, src, *waits):
        return SP.issue(lambda e: e.dma_start(dst() if callable(dst) else dst, src() if callable(src) else src),
                        *waits, count=16, counter=counter)

    ld = {}

    def ctr(name):
        if name not in ld:
            ld[name] = m.counter("load_" + name)
        return ld[name]

    def mm(out_ap, pairs, *waits, start=True, stop=True):
        for n, (lhs, rhs) in enumerate(pairs):
            last = n == len(pairs) - 1
            f = lambda e, l=lhs, r=rhs, s=(start and n == 0), z=(stop and last): e.matmul(
                out_ap, l, r, start=s, stop=z, skip_group_check=True)
            tok = (PE.do if last else PE.quiet)(f, *(waits if n == 0 else ()))
        return tok

    def half(h):
        return slice(h * HALF, (h + 1) * HALF)

    XT = sb("residual", [P, CT, TOK])
    XC = sb("conditioned", [P, CT, TOK])
    ident = sb("ident", [P, P])
    identb = sb("identb", [P, P], BF16)
    ones = sb("ones", [P, P])
    vecs = sb("vecs", [P, d["vecs"].shape[1]])
    eps = sb("eps", [P, 4])
    cond = sb("cond", [P, NB, 64])
    tf = sb("tf", [P, NB])
    decay = sb("decay", [P, NCOND, CT, NB])
    gain = sb("gain", [P, NB])
    factor = sb("factor", [P, CT, TOK])
    side = Phase()
    kv = side("side", [P, CT, TOK])
    ek = side("ek", [P, CT, TOK])
    ekv = side("ekv", [P, CT, TOK])
    vofs = d["vec_offsets"]

    def vcol(name, n=0):
        return vecs[:, vofs[name] + n:vofs[name] + n + 1]

    c0 = ctr("start")
    load(c0, XT[:, :, :], d["x"])
    load(c0, kv[:, :, :], d["side"])
    load(c0, ident[:, :], d["ident"])
    load(c0, vecs[:, :], d["vecs"])
    t_start = load(c0, cond[:, :, :], d["cond"].partition_broadcast(P))
    V.do(lambda e: e.memset(ones[:, :], 1.0))
    EPS = {2.0 ** -23: 0, 1e-6: 1, 1e-5: 2, 1.0: 3}
    for v, n in EPS.items():
        t_eps = V.do(lambda e, v=v, n=n: e.memset(eps[:, n:n + 1], v))

    def eps_col(v):
        return eps[:, EPS[v]:EPS[v] + 1]

    t_identb = V.do(lambda e: e.tensor_copy(identb[:, :], ident[:, :]), t_start)

    t = V.do(lambda e: e.reduce_sum(tf[:, :], cond[:, :, :], AX), t_start)
    t = A.do(lambda e: e.activation(tf[:, :], tf[:, :], ACT.Sigmoid), t)
    t_gain = V.do(lambda e: e.tensor_scalar(gain[:, :], tf[:, :], 0.2, 0.8, ALU.mult, ALU.add), t)
    t = V.do(lambda e: e.tensor_scalar(tf[:, :], tf[:, :], 0.5, 0.5, ALU.mult, ALU.add), t_gain)
    wv = vecs[:, vofs["cond_w"]:vofs["cond_w"] + NCOND * CT]
    ta = A.do(lambda e: e.activation(wv, wv, ACT.Exp), t_start)
    ta = A.do(lambda e: e.activation(wv, wv, ACT.Exp, scale=-1.0), ta)
    for b in range(NB):
        t_decay = V.do(lambda e, b=b: e.tensor_scalar(
            decay[:, :, :, b], wv.rearrange("p (l c) -> p l c", c=CT), tf[:, b:b + 1], None, ALU.mult), ta, t)
    for ct in range(CT):
        t = V.do(lambda e, ct=ct: e.tensor_scalar(ek[:, ct, :], kv[:, ct, :], 30.0, None, ALU.min), t_start)
        t = A.do(lambda e, ct=ct: e.activation(ek[:, ct, :], ek[:, ct, :], ACT.Exp), t)
        t = V.do(lambda e, ct=ct: e.tensor_tensor(ekv[:, ct, :], ek[:, ct, :], kv[:, ct, :], ALU.mult), t)
    m.fence()

    def wkv_factor(l):
        with Phase() as buf:
            euk = buf(f"w{l}_euk", [P, TOK])
            f1 = buf(f"w{l}_f1", [P, TOK])
            f2 = buf(f"w{l}_f2", [P, TOK])
            f3 = buf(f"w{l}_f3", [P, TOK])
            f4 = buf(f"w{l}_f4", [P, TOK])
            for ct in range(CT):
                t = V.do(lambda e: e.tensor_scalar(euk[:, :], kv[:, ct, :], vcol("cond_u", l * CT + ct), 30.0,
                                                   ALU.add, ALU.min), *m.freed("euk"))
                t_euk = A.do(lambda e: e.activation(euk[:, :], euk[:, :], ACT.Exp), t)
                for b in range(NB):
                    s = slice(b * T, (b + 1) * T)
                    dec = decay[:, l, ct, b:b + 1].to_broadcast([P, T])
                    for dst, src, back in ((f1, ekv, False), (f2, ekv, True), (f3, ek, False), (f4, ek, True)):
                        o, i = dst[:, s], src[:, ct, s]
                        if back:
                            o, i = o[:, ::-1], i[:, ::-1]
                        t_scan = V.do(lambda e: e.tensor_tensor_scan(o, dec, i, 0.0, ALU.mult, ALU.add), *m.freed("euk"))
                t1 = G.do(lambda e: e.tensor_tensor(f1[:, :], f1[:, :], f2[:, :], ALU.add), t_scan)
                t3 = V.do(lambda e: e.tensor_tensor(f3[:, :], f3[:, :], f4[:, :], ALU.add), t_scan)
                te = V.do(lambda e: e.tensor_tensor(euk[:, :], euk[:, :], ek[:, ct, :], ALU.subtract), t_euk)
                t3 = V.do(lambda e: e.tensor_tensor(f3[:, :], f3[:, :], euk[:, :], ALU.add), te, t3)
                te = G.do(lambda e: e.tensor_tensor(euk[:, :], euk[:, :], kv[:, ct, :], ALU.mult), t3)
                t1 = G.do(lambda e: e.tensor_tensor(f1[:, :], f1[:, :], euk[:, :], ALU.add), te, t1)
                t3 = V.do(lambda e: e.tensor_scalar(f3[:, :], f3[:, :], 1e-8, None, ALU.max), t3)
                t3 = A.do(lambda e: e.activation(f3[:, :], f3[:, :], ACT.Ln), t3)
                t3 = A.do(lambda e: e.activation(f3[:, :], f3[:, :], ACT.Exp, scale=-1.0), t3)
                for b in range(NB):
                    s = slice(b * T, (b + 1) * T)
                    t = V.do(lambda e: e.scalar_tensor_tensor(factor[:, ct, s], f1[:, s], gain[:, b:b + 1], f3[:, s],
                                                              ALU.mult, ALU.mult), t1, t3)
                m.release("euk", t)

    def condition(l):
        if l < NCOND - 1:
            wkv_factor(l)
        toks = []
        for ct in range(CT):
            t = A.do(lambda e: e.activation(XC[:, ct, :], XT[:, ct, :], ACT.Sigmoid))
            toks.append(V.do(lambda e: e.tensor_tensor(XC[:, ct, :], XC[:, ct, :], factor[:, ct, :], ALU.mult), t))
        return toks

    def inverse_root(src, ready, sq, dst, e_value, width=C, bank0=0):
        for ct in range(CT):
            t = A.do(lambda e: e.activation(sq[:, ct, :], src[:, ct, :], ACT.Square), ready[ct])
        for h in range(NH):
            bk = f"bank{bank0 + h}"
            t2 = mm(banks[bank0 + h][:, :], [(ones[:, :], sq[:, ct, half(h)]) for ct in range(CT)], t, *m.freed(bk))
            t2 = A.do(lambda e: e.activation(dst[:, half(h)], banks[bank0 + h][:, :], ACT.Ln, scale=1.0 / width,
                                             bias=eps_col(e_value)), t2)
            m.release(bk, t2)
            t3 = A.do(lambda e: e.activation(dst[:, half(h)], dst[:, half(h)], ACT.Exp, scale=-0.5), t2)
        return t3

    def scale_rows(src, rs, wname, dst, t):
        return [V.do(lambda e: e.scalar_tensor_tensor(dst[:, ct, :], src[:, ct, :], vcol(wname, ct), rs[:, :],
                                                      ALU.mult, ALU.mult), t) for ct in range(CT)]

    def to_channels(src, dst, ready, bank0=4):
        toks = []
        for tt in range(TT):
            b = bank0 + tt % 4
            for ct in range(CT):
                t = PE.do(lambda e: e.transpose(banks[b][:, ct * P:(ct + 1) * P], src[:, tt, ct * P:(ct + 1) * P], ident[:, :]),
                          ready[tt], *m.freed(f"bank{b}"))
            lane, f = ((A, "copy"), (V, "tensor_copy"))[tt % 2]
            o = dst[:, :, tt * P:(tt + 1) * P]
            i = banks[b][:, 0:C].rearrange("p (c t) -> p c t", c=CT)
            t = A.do(lambda e: e.copy(o, i), t) if tt % 2 else V.do(lambda e: e.tensor_copy(o, i), t)
            m.release(f"bank{b}", t)
            toks.append(t)
        return toks

    def project_residual(w, kt, src, ready, add=None, bank0=0):
        for ct in range(CT):
            for h in range(NH):
                b = bank0 + ct * NH + h
                t = mm(banks[b][:, :], [(w[:, k, ct * P:(ct + 1) * P], src[:, k, half(h)]) for k in range(kt)],
                       *ready, *m.freed(f"bank{b}"))
                o = XT[:, ct, half(h)]
                t = V.do(lambda e: e.tensor_tensor(o, o, banks[b][:, :], ALU.add), t)
                m.release(f"bank{b}", t)
                if add is not None:
                    V.do(lambda e: e.tensor_tensor(o, o, add[:, ct, half(h)], ALU.add), t)

    def pad_heads(w, k, tile):
        return w[:, k, tile * 64:tile * 64 + 64]

    def ternary(w, n, total, buf, name, t_w):
        part = buf(name + "_part", [P, 2])
        wf = w[:, :, :].rearrange("p c n -> p (c n)")
        t = V.do(lambda e: e.tensor_reduce(part[:, 0:1], wf, AX, ALU.add, apply_absolute_value=True), t_w)
        t = mm(banks[7][:, 0:1], [(ones[:, :], part[:, 0:1])], t, *m.freed("bank7"))
        t = V.do(lambda e: e.tensor_scalar(part[:, 0:1], banks[7][:, 0:1], 1.0 / total, 1e-5, ALU.mult, ALU.max), t)
        m.release("bank7", t)
        t = V.do(lambda e: e.reciprocal(part[:, 1:2], part[:, 0:1]), t)
        t = V.do(lambda e: e.tensor_scalar(wf, wf, part[:, 1:2], ROUND, ALU.mult, ALU.add), t)
        t = V.do(lambda e: e.tensor_scalar(wf, wf, -ROUND, -1.0, ALU.add, ALU.max), t)
        return V.do(lambda e: e.tensor_scalar(wf, wf, 1.0, part[:, 0:1], ALU.min, ALU.mult), t)

    def linear_attention():
        with Phase() as buf:
            wqkv = buf("l0_wqkv", [P, CT, d["l0_qkv"].shape[2]])
            wp = buf("l0_wp", [P, CT, C])
            srow = buf("l0_s", [P, 16])
            dist = buf("l0_dist", [P, T])
            decm = buf("l0_decm", [P, 16, T])
            t_w = load(ctr("l0"), wqkv[:, :, :], d["l0_qkv"])
            t_s = load(ctr("l0s"), srow[:, :], d["l0_s"].partition_broadcast(P))
            t_p = load(ctr("l0p"), wp[:, :, :], d["l0_proj"])
            t_d = load(ctr("l0d"), dist[:, :], d["dist"])
            ts = V.do(lambda e: e.tensor_scalar(srow[:, :], srow[:, :], -1.0, None, ALU.mult), t_s)
            for h in range(16):
                t = A.do(lambda e: e.activation(decm[:, h, :], dist[:, :], ACT.Exp, scale=srow[:, h:h + 1]), ts, t_d)
                t_m = G.do(lambda e: e.affine_select(out=decm[:, h, :], in_=decm[:, h, :], compare_op=ALU.is_ge, fill=0.0,
                                                     base=0, pattern=[[1, T]], channel_multiplier=-1), t)
            tq = ternary(wqkv, 768, 768 * C, buf, "l0q", t_w)
            tp = ternary(wp, C, C * C, buf, "l0p", t_p)
            q4 = buf("l0_q4", [P, 4, TOK])
            k4 = buf("l0_k4", [P, 4, TOK])
            v = buf("l0_v", [P, TT, C])
            ready = condition(0)
            with Phase() as b2:
                sq = b2("l0_sq", [P, CT, TOK])
                rs = b2("l0_rs", [P, TOK])
                t = inverse_root(XC, ready, sq, rs, 2.0 ** -23)
                rdy = scale_rows(XC, rs, "l0_qkv_norm", sq, t)
                wq = wqkv
                n = 0
                for dst, base in ((q4, 0), (k4, C)):
                    for tile in range(4):
                        for h in range(NH):
                            b = n % 4
                            n += 1
                            for j in range(4):
                                col = base + (tile * 4 + j) * 16
                                t = mm(banks[b][32 * j:32 * j + 16, :],
                                       [(wq[:, k, col:col + 16], sq[:, k, half(h)]) for k in range(CT)],
                                       *rdy, tq, *m.freed(f"bank{b}"))
                                o, i = dst[32 * j:32 * j + 16, tile, half(h)], banks[b][32 * j:32 * j + 16, :]
                                t = A.do(lambda e: e.copy(o, i), t) if j % 2 else V.do(lambda e: e.tensor_copy(o, i), t)
                                if j == 0:
                                    rel = []
                                rel.append(t)
                            m.release(f"bank{b}", *rel)
                for tt in range(TT):
                    b = 4 + tt % 4
                    t = mm(banks[b][:, 0:C], [(sq[:, k, tt * P:(tt + 1) * P], wq[:, k, 2 * C:3 * C]) for k in range(CT)],
                           *rdy, tq, *m.freed(f"bank{b}"))
                    t = V.do(lambda e: e.tensor_copy(v[:, tt, :], banks[b][:, 0:C]), t)
                    m.release(f"bank{b}", t)
            with Phase() as b2:
                sm = [b2(f"l0_sm{i}", [P, 384]) for i in range(4)]
                o = b2("l0_o", [P, TT, C])
                o_ready = []
                units = [(b, h) for b in range(NB) for h in range(16)]

                def scores(n):
                    b, h = units[n]
                    j, tile, t0 = 32 * (h % 4), h // 4, b * T
                    bk = n % 4
                    PE.quiet(lambda e: e.matmul(banks[bk][:, 0:T], k4[j:j + 16, tile, t0:t0 + P],
                                                q4[j:j + 16, tile, t0:t0 + T], start=True, stop=True,
                                                skip_group_check=True), *m.freed(f"bank{bk}"))
                    t = PE.do(lambda e: e.matmul(banks[bk][:, T:T + P], k4[j:j + 16, tile, t0 + P:t0 + T],
                                                 q4[j:j + 16, tile, t0 + P:t0 + T], start=False, stop=True,
                                                 skip_group_check=True))
                    s = sm[n % 4]
                    t1 = V.do(lambda e: e.tensor_tensor(s[:, 0:T], banks[bk][:, 0:T], decm[:, h, :], ALU.mult),
                              t, t_m, *m.freed(f"sm{n % 4}"))
                    t = V.do(lambda e: e.tensor_tensor(s[:, T:T + P], banks[bk][:, T:T + P], decm[:, h, 0:P], ALU.mult))
                    m.release(f"bank{bk}", t)
                    return t

                def mix(n, t):
                    b, h = units[n]
                    s = sm[n % 4]
                    hs = slice(h * 16, h * 16 + 16)
                    bk = 4 + 2 * (b % 2)
                    vb = [v[:, 2 * b + i, hs] for i in range(2)]
                    st = h == 0
                    fr = (m.freed(f"bank{bk}") + m.freed(f"bank{bk + 1}")) if st else ()
                    PE.quiet(lambda e: e.matmul(banks[bk][:, hs], s[:, 0:P], vb[0], start=st, stop=True,
                                                skip_group_check=True), t, *fr)
                    PE.quiet(lambda e: e.matmul(banks[bk + 1][:, hs], s[:, P:T], vb[0], start=st, stop=False,
                                                skip_group_check=True))
                    t = PE.do(lambda e: e.matmul(banks[bk + 1][:, hs], s[:, T:T + P], vb[1], start=False, stop=True,
                                                 skip_group_check=True))
                    m.release(f"sm{n % 4}", t)
                    if h == 15:
                        for i in range(2):
                            t2 = A.do(lambda e: e.mul(o[:, 2 * b + i, :], banks[bk + i][:, 0:C], 0.25), t)
                            m.release(f"bank{bk + i}", t2)
                            o_ready.append(t2)

                pend = []
                for n in range(len(units)):
                    pend.append((n, scores(n)))
                    if len(pend) > 2:
                        mix(*pend.pop(0))
                for p in pend:
                    mix(*p)
                m.fence()
                ot = b2("l0_ot", [P, CT, TOK])
                sq = b2("l0_sq2", [P, CT, TOK])
                rs = b2("l0_rs2", [P, TOK])
                toks = to_channels(o, ot, o_ready)
                m.fence()
                t = inverse_root(ot, [None, None], sq, rs, 1e-6)
                rdy = scale_rows(ot, rs, "l0_norm", ot, t)
                t = inverse_root(ot, rdy, sq, rs, 2.0 ** -23)
                rdy = scale_rows(ot, rs, "l0_proj_norm", ot, t)
                project_residual(wp, CT, ot, rdy + [tp])

    def pick_top(scores, taken, hot, revi, tmp, E, t):
        def bc(a):
            return a.unsqueeze(2).to_broadcast([P, TT, E])
        mx = tmp[:, 0, :, 0]
        w = tmp[:, 1, :, 0:E]
        if taken is not None:
            t = V.do(lambda e: e.scalar_tensor_tensor(w, taken, -BIG, scores, ALU.mult, ALU.add), t)
            src = w
        else:
            src = scores
        t = V.do(lambda e: e.tensor_reduce(mx, src, AX, ALU.max), t)
        t = V.do(lambda e: e.tensor_tensor(hot, src, bc(mx), ALU.is_equal), t)
        t = V.do(lambda e: e.tensor_tensor(hot, hot, revi, ALU.mult), t)
        t = V.do(lambda e: e.tensor_reduce(mx, hot, AX, ALU.max), t)
        return V.do(lambda e: e.tensor_tensor(hot, revi, bc(mx), ALU.is_equal), t)

    def token_logits(w, n, ready, bank=0):
        for tt in range(TT):
            for k in range(CT):
                f = lambda e: e.matmul(banks[bank][:, tt * n:(tt + 1) * n], XC[:, k, tt * P:(tt + 1) * P], w[:, k, :],
                                       start=(tt == 0 and k == 0), stop=(k == CT - 1), skip_group_check=True)
                wt = (*ready, *m.freed(f"bank{bank}")) if tt == 0 and k == 0 else ()
                t = (PE.do if (tt == TT - 1 and k == CT - 1) else PE.quiet)(f, *wt)
        return t

    def rows_from_tokens(src, n, dst, t):
        for tt in range(TT):
            b = 6 + tt // 4
            t2 = PE.do(lambda e: e.transpose(banks[b][0:n, (tt % 4) * P:(tt % 4 + 1) * P], src[:, tt, :], ident[:, :]), t,
                       *m.freed(f"bank{b}"))
            if tt % 4 == 3:
                h = tt // 4
                t2 = V.do(lambda e: e.tensor_copy(dst[0:n, half(h)], banks[b][0:n, :]), t2)
                m.release(f"bank{b}", t2)
        return t2

    def gated_unit(src, wg, wu, rows, h, n, coef, hbuf, sbuf, waits):
        b = 4 + 2 * (n % 2)
        bk = f"pair{n % 2}"
        mm(banks[b][0:rows, :], [(wg[k], src[:, k, half(h)]) for k in range(CT)], *waits, *m.freed(bk))
        t = mm(banks[b + 1][0:rows, :], [(wu[k], src[:, k, half(h)]) for k in range(CT)])
        s, o = sbuf[n % 2], hbuf[n % 3]
        t = A.do(lambda e: e.activation(s[0:rows, :], banks[b][0:rows, :], ACT.Silu), t, *m.freed(f"s{n % 2}"))
        t = V.do(lambda e: e.tensor_tensor(o[0:rows, :] if coef is None else s[0:rows, :], s[0:rows, :],
                                           banks[b + 1][0:rows, :], ALU.mult), t, *m.freed(f"h{n % 3}"))
        m.release(bk, t)
        if coef is not None:
            cf, tc = coef
            t = V.do(lambda e: e.tensor_tensor(o[0:rows, :], s[0:rows, :], cf(), ALU.mult), t, tc)
        m.release(f"s{n % 2}", t)
        return t

    def down_unit(wd, rows, h, n, hbuf, first, last, waits):
        for ct in range(CT):
            f = lambda e: e.matmul(banks[ct * NH + h][:, :], wd[0:rows, ct * P:(ct + 1) * P], hbuf[n % 3][0:rows, :],
                                   start=first, stop=last, skip_group_check=True)
            t = PE.quiet(f, *waits) if ct == 0 else PE.do(f)
        m.release(f"h{n % 3}", t)
        return t

    def run_units(units, hbuf, sbuf):
        pend = None
        for n, u in enumerate(units):
            if u.get("before"):
                u["before"]()
            t = gated_unit(u["src"], u["wg"], u["wu"], u["rows"], u["h"], n, u["coef"], hbuf, sbuf, u["waits"])
            if pend:
                down_unit(*pend)
                if pend_after:
                    pend_after()
            pend = (u["wd"], u["rows"], u["h"], n, hbuf, u["first"], u["last"], [t])
            pend_after = u.get("after")
        down_unit(*pend)
        if pend_after:
            pend_after()

    def add_out_banks():
        t0 = PE.here()
        for ct in range(CT):
            for h in range(NH):
                o = XT[:, ct, half(h)]
                V.do(lambda e: e.tensor_tensor(o, o, banks[ct * NH + h][:, :], ALU.add), t0)

    def moe_top1():
        E, F = 8, 512
        FT = F // P
        with Phase() as buf:
            wr = buf("m0_wr", [P, CT, E])
            sg = buf("m0_sg", [P, CT, 2 * F])
            sd = buf("m0_sd", [P, FT, C])
            revi = buf("m0_revi", [P, TT, E])
            selm = buf("m0_sel", [16, 9, P])
            t_w = load(ctr("m0"), wr[:, :, :], d["m0_router"])
            load(ctr("m0"), revi[:, :, :], d["revi8"])
            t_w = load(ctr("m0"), selm[:, :, :], d["sel16"][:, 0:9, :])
            load(ctr("m0s"), sg[:, :, :], d["m0_shared_gu"])
            t_s = load(ctr("m0s"), sd[:, :, :], d["m0_shared_down"])
            ready = condition(1)
            xs = buf("m0_xs", [P, CT, TOK])
            maskb = buf("m0_mask", [P, E, TOK])
            rows = buf("m0_rows", [16, TOK])
            with Phase() as b2:
                lg = b2("m0_lg", [P, TT, E])
                hot = b2("m0_hot", [P, TT, 9])
                tmp = b2("m0_tmp", [P, 2, TT, 16])
                t = token_logits(wr, E, ready + [t_w])
                t = V.do(lambda e: e.tensor_copy(lg[:, :, :].rearrange("p t e -> p (t e)"), banks[0][:, 0:TT * E]), t)
                m.release("bank0", t)
                tm = V.do(lambda e: e.tensor_reduce(hot[:, :, 8], lg[:, :, :], AX, ALU.max), t)
                ta = A.do(lambda e: e.activation(hot[:, :, 8], hot[:, :, 8], ACT.Sigmoid), tm)
                t = pick_top(lg[:, :, :], None, hot[:, :, 0:8], revi[:, :, :], tmp, E, tm)
                V.wait(ta)
                t = rows_from_tokens(hot, 9, rows, t if False else V.do(lambda e: e.tensor_copy(tmp[:, 0, :, 1], hot[:, :, 8]), ta))
            for e_ in range(9):
                for h in range(NH):
                    b = (e_ * NH + h) % 4
                    t = mm(banks[b][:, :], [(selm[0:9, e_, :], rows[0:9, half(h)])], *m.freed(f"bank{b}"))
                    if e_ < 8:
                        t = A.do(lambda e: e.copy(maskb[:, e_, half(h)], banks[b][:, :]), t)
                    else:
                        for ct in range(CT):
                            t = V.do(lambda e: e.tensor_tensor(xs[:, ct, half(h)], XC[:, ct, half(h)], banks[b][:, :],
                                                               ALU.mult), t)
                    m.release(f"bank{b}", t)
            m.fence()
            wgu = [buf(f"m0_wgu{j}", [P, CT, 2, P]) for j in range(FT)]
            wd = [buf(f"m0_wd{j}", [P, C]) for j in range(FT)]
            hbuf = [buf(f"m0_h{i}", [P, HALF]) for i in range(3)]
            sbuf = [buf(f"m0_s{i}", [P, HALF]) for i in range(2)]
            units = []
            for ft in range(FT):
                for h in range(NH):
                    units.append(dict(src=XC, wg=[sg[:, k, ft * P:(ft + 1) * P] for k in range(CT)],
                                      wu=[sg[:, k, F + ft * P:F + (ft + 1) * P] for k in range(CT)],
                                      wd=sd[:, ft, :], rows=P, h=h, coef=None, first=ft == 0, last=False, waits=[t_s]))
            run_units(units, hbuf, sbuf)

            def body(i):
                toks = []
                for j in range(FT):
                    load(ctr(f"m0w{j}"), wgu[j][:, :, :, :], lambda: d["m0_gu"][i, j], *m.freed(f"wgu{j}"))
                    toks.append(load(ctr(f"m0w{j}"), wd[j][:, :], lambda: d["m0_down"][i, j], *m.freed(f"wd{j}")))
                units = []
                for ft in range(FT):
                    for h in range(NH):
                        cf = (lambda h=h: maskb[:, i, half(h)])
                        units.append(dict(src=xs, wg=[wgu[ft][:, k, 0, :] for k in range(CT)],
                                          wu=[wgu[ft][:, k, 1, :] for k in range(CT)], wd=wd[ft], rows=P, h=h,
                                          coef=(cf, None), first=False, last=True, waits=[toks[ft]],
                                          after=(lambda ft=ft: (m.release(f"wgu{ft}", PE.here()), m.release(f"wd{ft}", PE.here()))) if h == 1 else None))
                run_units(units, hbuf, sbuf)

            m.run_loop(E, body)
            add_out_banks()

    def banded_attention():
        NG, W = 16, 32
        KS = P + W + NG
        with Phase() as buf:
            wq = buf("b_wq", [P, CT, C])
            wk = buf("b_wk", [P, CT, C])
            wv = buf("b_wv", [P, CT, C])
            wo = buf("b_wo", [P, CT, C])
            msk = buf("b_msk", [P, 2, KS])
            small = buf("b_small", [P, CT, NB, W + NG])
            load(ctr("b"), wq[:, :, :], d["b_wq"])
            load(ctr("b"), wk[:, :, :], d["b_wk"])
            load(ctr("b"), wv[:, :, :], d["b_wv"])
            for b in range(NB):
                load(ctr("b"), small[:, :, b, W:W + NG], d["b_global"])
            load(ctr("b"), msk[:, :, :], d["b_mask"])
            t_w = load(ctr("b"), wo[:, :, :], d["b_wo"])
            ready = condition(2)
            q4 = buf("b_q4", [P, 4, TOK])
            k4 = buf("b_k4", [P, 4, TOK])
            ks4 = buf("b_ks4", [P, 4, NB * (W + NG)])
            v = buf("b_v", [P, TT, C])
            vs = buf("b_vs", [W + NG, NB, C])
            with Phase() as b2:
                xn = b2("b_xn", [P, CT, TOK])
                sq = b2("b_sq", [P, CT, TOK])
                rs = b2("b_rs", [P, TOK])
                for h in range(NH):
                    t = mm(banks[h][:, :], [(ones[:, :], XC[:, k, half(h)]) for k in range(CT)], *ready, *m.freed(f"bank{h}"))
                    t = A.do(lambda e: e.mul(rs[:, half(h)], banks[h][:, :], 1.0 / C), t)
                    m.release(f"bank{h}", t)
                rdy = [V.do(lambda e: e.tensor_tensor(xn[:, ct, :], XC[:, ct, :], rs[:, :], ALU.subtract), t) for ct in range(CT)]
                A.wait(rdy[-1])
                t = inverse_root(xn, rdy, sq, rs, 1e-5)
                rdy = scale_rows(xn, rs, "b_ln_scale", xn, t)
                rdy = [A.do(lambda e: e.activation(xn[:, ct, :], xn[:, ct, :], ACT.Identity, bias=vcol("b_ln_bias", ct)), rdy[ct])
                       for ct in range(CT)]
                t_sm = V.do(lambda e: e.tensor_copy(
                    small[:, :, :, 0:W], xn[:, :, :].rearrange("p c (b t) -> p c b t", b=NB)[:, :, :, P - W:P]), *rdy, t_w)
                n = 0
                jobs = [(q4, wq, xn, half(h), tile) for tile in range(4) for h in range(NH)]
                jobs += [(k4, wk, xn, half(h), tile) for tile in range(4) for h in range(NH)]
                smf = small[:, :, :, :].rearrange("p c b t -> p c (b t)")
                jobs += [(ks4, wk, smf, slice(0, NB * (W + NG)), tile) for tile in range(4)]
                for dst, w, src, cols, tile in jobs:
                    b = n % 4
                    n += 1
                    nn = cols.stop - cols.start
                    rel = []
                    for j in range(4):
                        col = (tile * 4 + j) * 16
                        t = mm(banks[b][32 * j:32 * j + 16, 0:nn],
                               [(w[:, k, col:col + 16], src[:, k, cols]) for k in range(CT)],
                               *rdy, t_w, t_sm, *m.freed(f"bank{b}"))
                        o, i = dst[32 * j:32 * j + 16, tile, cols], banks[b][32 * j:32 * j + 16, 0:nn]
                        rel.append(A.do(lambda e: e.copy(o, i), t) if j % 2 else V.do(lambda e: e.tensor_copy(o, i), t))
                    m.release(f"bank{b}", *rel)
                for tt in range(TT):
                    b = 4 + tt % 4
                    t = mm(banks[b][:, 0:C], [(xn[:, k, tt * P:(tt + 1) * P], wv[:, k, :]) for k in range(CT)], *m.freed(f"bank{b}"))
                    t = V.do(lambda e: e.tensor_copy(v[:, tt, :], banks[b][:, 0:C]), t)
                    m.release(f"bank{b}", t)
                for b_ in range(NB):
                    b = 4 + b_
                    t = mm(banks[b][0:W + NG, 0:C], [(small[:, k, b_, :], wv[:, k, :]) for k in range(CT)], *m.freed(f"bank{b}"))
                    t = V.do(lambda e: e.tensor_copy(vs[:, b_, :], banks[b][0:W + NG, 0:C]), t)
                    m.release(f"bank{b}", t)
            with Phase() as b2:
                s_ = [b2(f"b_s{i}", [P, KS]) for i in range(4)]
                mx = b2("b_mx", [P, 8])
                sums = b2("b_sums", [P, 2, 16])
                rinv = b2("b_rinv", [P, 2, 16])
                pt = [b2(f"b_pt{i}", [P, 2 * P]) for i in range(3)]
                o = b2("b_o", [P, TT, C])
                o_ready = []
                units = [(tt, h) for tt in range(TT) for h in range(16)]

                def scores(n):
                    tt, h = units[n]
                    b, j, tile = tt // 2, 32 * (h % 4), h // 4
                    bk, s = n % 3, s_[n % 4]
                    ql = q4[j:j + 16, tile, tt * P:(tt + 1) * P]
                    PE.quiet(lambda e: e.matmul(banks[bk][:, 0:P], ql, k4[j:j + 16, tile, tt * P:(tt + 1) * P],
                                                start=True, stop=True, skip_group_check=True), *m.freed(f"bank{bk}"))
                    t = PE.do(lambda e: e.matmul(banks[bk][:, P:KS], ql, ks4[j:j + 16, tile, b * (W + NG):(b + 1) * (W + NG)],
                                                 start=False, stop=True, skip_group_check=True))
                    mc, nm = mx[:, n % 4:n % 4 + 1], mx[:, 4 + n % 4:5 + n % 4]
                    t = V.do(lambda e: e.tensor_tensor_reduce(s[:, :], banks[bk][:, 0:KS], msk[:, tt % 2, :], 1.0, -BIG,
                                                              ALU.add, ALU.max, mc), t, *m.freed(f"s{n % 4}"))
                    m.release(f"bank{bk}", t)
                    t = V.do(lambda e: e.tensor_scalar(nm, mc, -0.25, None, ALU.mult), t)
                    sl = tt % 2
                    return A.do(lambda e: e.activation(s[:, :], s[:, :], ACT.Exp, bias=nm, scale=0.25,
                                                       accum_out=sums[:, sl, h:h + 1]), t, *(m.freed(f"sums{sl}") if h == 0 else ()))

                def turn(n, t):
                    bk, s, p_ = 3 + n % 2, s_[n % 4], pt[n % 3]
                    PE.quiet(lambda e: e.transpose(banks[bk][:, 0:P], s[:, 0:P], ident[:, :]), t, *m.freed(f"bank{bk}"))
                    t = PE.do(lambda e: e.transpose(banks[bk][0:W + NG, P:2 * P], s[:, P:KS], ident[:, :]))
                    m.release(f"s{n % 4}", t)
                    lane = (V, A)[n % 2]
                    cp = (lambda e, o, i: e.copy(o, i)) if n % 2 else (lambda e, o, i: e.tensor_copy(o, i))
                    t1 = lane.do(lambda e: cp(e, p_[:, 0:P], banks[bk][:, 0:P]), t, *m.freed(f"pt{n % 3}"))
                    t2 = lane.do(lambda e: cp(e, p_[0:W + NG, P:2 * P], banks[bk][0:W + NG, P:2 * P]))
                    m.release(f"bank{bk}", t2)
                    return t1, t2

                def mix(n, t1, t2):
                    tt, h = units[n]
                    hs = slice(h * 16, h * 16 + 16)
                    bk, p_ = 6 + tt % 2, pt[n % 3]
                    PE.quiet(lambda e: e.matmul(banks[bk][:, hs], p_[:, 0:P], v[:, tt, hs], start=(h == 0), stop=False,
                                                skip_group_check=True), t1, t2, *(m.freed(f"bank{bk}") if h == 0 else ()))
                    t = PE.do(lambda e: e.matmul(banks[bk][:, hs], p_[0:W + NG, P:2 * P], vs[:, tt // 2, hs], start=False,
                                                 stop=True, skip_group_check=True))
                    m.release(f"pt{n % 3}", t)
                    if h == 15:
                        sl = tt % 2
                        tr = V.do(lambda e: e.reciprocal(rinv[:, sl, :], sums[:, sl, :]), t)
                        m.release(f"sums{sl}", tr)
                        t = V.do(lambda e: e.tensor_tensor(
                            o[:, tt, :].rearrange("p (h d) -> p h d", h=16),
                            banks[bk][:, 0:C].rearrange("p (h d) -> p h d", h=16),
                            rinv[:, sl, :].unsqueeze(2).to_broadcast([P, 16, 16]), ALU.mult), t, tr)
                        m.release(f"bank{bk}", t)
                        o_ready.append(t)

                p1, p2 = [], []
                for n in range(len(units)):
                    p1.append((n, scores(n)))
                    if len(p1) > 2:
                        a = p1.pop(0)
                        p2.append((a[0], *turn(*a)))
                    if len(p2) > 1:
                        mix(*p2.pop(0))
                for a in p1:
                    p2.append((a[0], *turn(*a)))
                    mix(*p2.pop(0))
                for a in p2:
                    mix(*a)
                m.fence()
                ot = b2("b_ot", [P, CT, TOK])
                toks = to_channels(o, ot, o_ready)
                project_residual(wo, CT, ot, toks, add=XC)

    def lora_ffn():
        E, F = 8, 896
        FT = F // P
        with Phase() as buf:
            wr = buf("r_wr", [P, CT, E])
            w1 = buf("r_w1", [P, CT, F])
            w3 = buf("r_w3", [P, CT, F])
            w2 = buf("r_w2", [P, FT, C])
            b1 = buf("r_b1", [P, CT, F])
            b3 = buf("r_b3", [P, CT, F])
            a2 = buf("r_a2", [P, FT, C])
            b2w = buf("r_b2", [P, CT, C])
            for dst, name in ((wr, "r_router"), (w1, "r_w1"), (w3, "r_w3"), (b1, "r_b1"), (b3, "r_b3"), (a2, "r_a2"),
                              (b2w, "r_b2"), (w2, "r_w2")):
                t_w = load(ctr("r"), dst[:, :, :], d[name])
            ready = condition(3)
            rwb = buf("r_rwb", [P, 2, TOK])
            am = [[buf(f"r_am{k}{j}", [P, CT, TOK]) for j in range(2)] for k in range(2)]
            with Phase() as bb:
                a1 = bb("r_a1", [P, CT, C])
                a3 = bb("r_a3", [P, CT, C])
                revi = bb("r_revi", [P, TT, E])
                sel = bb("r_sel", [18, 2, P])
                selx = bb("r_selx", [18, 2, CT, P])
                load(ctr("r2"), a1[:, :, :], d["r_a1"])
                load(ctr("r2"), a3[:, :, :], d["r_a3"])
                load(ctr("r2"), revi[:, :, :], d["revi8"])
                load(ctr("r2"), sel[:, :, :], d["r_sel"])
                t_w2 = load(ctr("r2"), selx[:, :, :, :], d["r_selx"])
                pr = bb("r_pr", [P, TT, E])
                hot = bb("r_hot", [P, TT, 18])
                tmp = bb("r_tmp", [P, 2, TT, 16])
                st = bb("r_st", [P, 4, TT])
                rows = bb("r_rows", [18, TOK])
                mk = bb("r_mk", [P, 2, HALF])

                def bc(a, n=E):
                    return a.unsqueeze(2).to_broadcast([P, TT, n])
                t = token_logits(wr, E, ready + [t_w])
                t = V.do(lambda e: e.tensor_copy(pr[:, :, :].rearrange("p t e -> p (t e)"), banks[0][:, 0:TT * E]), t)
                m.release("bank0", t)
                t = V.do(lambda e: e.tensor_reduce(st[:, 0, :], pr[:, :, :], AX, ALU.max), t)
                t = V.do(lambda e: e.tensor_tensor(pr[:, :, :], pr[:, :, :], bc(st[:, 0, :]), ALU.subtract), t)
                t = A.do(lambda e: e.activation(pr[:, :, :], pr[:, :, :], ACT.Exp), t)
                t = V.do(lambda e: e.tensor_reduce(st[:, 0, :], pr[:, :, :], AX, ALU.add), t)
                t = V.do(lambda e: e.reciprocal(st[:, 0, :], st[:, 0, :]), t)
                t = V.do(lambda e: e.tensor_tensor(pr[:, :, :], pr[:, :, :], bc(st[:, 0, :]), ALU.mult), t)
                V.wait(t_w2)
                t = pick_top(pr[:, :, :], None, hot[:, :, 0:8], revi[:, :, :], tmp, E, t)
                t = pick_top(pr[:, :, :], hot[:, :, 0:8], hot[:, :, 8:16], revi[:, :, :], tmp, E, t)
                for k in range(2):
                    t = V.do(lambda e: e.tensor_tensor(tmp[:, 1, :, 0:8], pr[:, :, :], hot[:, :, 8 * k:8 * k + 8], ALU.mult), t)
                    t = V.do(lambda e: e.tensor_reduce(st[:, k, :], tmp[:, 1, :, 0:8], AX, ALU.add), t)
                t = V.do(lambda e: e.tensor_tensor(st[:, 2, :], st[:, 0, :], st[:, 1, :], ALU.add), t)
                t = V.do(lambda e: e.reciprocal(st[:, 2, :], st[:, 2, :]), t)
                for k in range(2):
                    t = V.do(lambda e: e.tensor_tensor(hot[:, :, 16 + k], st[:, k, :], st[:, 2, :], ALU.mult), t)
                t = rows_from_tokens(hot, 18, rows, t)
                for k in range(2):
                    for h in range(NH):
                        b = h
                        t2 = mm(banks[b][:, :], [(sel[:, k, :], rows[:, half(h)])], t, t_w2, *m.freed(f"bank{b}"))
                        t2 = A.do(lambda e: e.copy(rwb[:, k, half(h)], banks[b][:, :]), t2)
                        m.release(f"bank{b}", t2)
                for ct in range(CT):
                    for h in range(NH):
                        for k in range(2):
                            t2 = mm(banks[2 + k][:, :], [(selx[:, k, ct, :], rows[:, half(h)])], t, *m.freed(f"bank{2 + k}"))
                            t2 = A.do(lambda e: e.copy(mk[:, k, :], banks[2 + k][:, :]), t2, *m.freed("mk"))
                            m.release(f"bank{2 + k}", t2)
                        td = V.do(lambda e: e.tensor_tensor(mk[:, 1, :], mk[:, 1, :], mk[:, 0, :], ALU.subtract), t2)
                        for j, w in enumerate((a1, a3)):
                            b = 4 + j
                            t3 = mm(banks[b][:, :], [(w[:, k2, ct * P:(ct + 1) * P], XC[:, k2, half(h)]) for k2 in range(CT)],
                                    t_w2, *m.freed(f"bank{b}"))
                            for k in range(2):
                                t3 = V.do(lambda e: e.tensor_tensor(am[k][j][:, ct, half(h)], mk[:, k, :], banks[b][:, :],
                                                                    ALU.mult), t3, td)
                            m.release(f"bank{b}", t3)
                        m.release("mk", t3)
                m.fence()
                maskx = buf_mask
                for k in range(2):
                    for ct in range(CT):
                        for h in range(NH):
                            b = (k * 4 + ct * 2 + h) % 4
                            t2 = mm(banks[b][:, :], [(selx[:, k, ct, :], rows[:, half(h)])], *m.freed(f"bank{b}"))
                            t2 = A.do(lambda e: e.copy(maskx[:, k, ct, half(h)], banks[b][:, :]), t2)
                            m.release(f"bank{b}", t2)
            with Phase() as bb:
                ys = bb("r_ys", [P, FT, HALF])
                y = [[bb(f"r_y{k}{i}", [P, HALF]) for i in range(3)] for k in range(2)]
                sl = [bb(f"r_sl{i}", [P, HALF]) for i in range(2)]
                u2 = bb("r_u2", [P, CT, HALF])
                u3 = bb("r_u3", [P, HALF])
                for h in range(NH):
                    def up(ft, k):
                        pr_ = ft % 2
                        b = 2 * pr_
                        fs = slice(ft * P, (ft + 1) * P)
                        first = [(w1, b1), (w3, b3)]
                        for j, (w, lw) in enumerate(first):
                            pairs = [(lw[:, c, fs], am[k][j][:, c, half(h)]) for c in range(CT)]
                            if k == 0:
                                pairs = [(w[:, c, fs], XC[:, c, half(h)]) for c in range(CT)] + pairs
                            t = mm(banks[b + j][:, :], pairs, *m.freed(f"pair{pr_}"), start=(k == 0))
                        s, yy = sl[k], y[k][ft % 3]
                        t1 = A.do(lambda e: e.activation(s[:, :], banks[b][:, :], ACT.Silu), t, *m.freed(f"sl{k}"))
                        t1 = V.do(lambda e: e.tensor_tensor(s[:, :], s[:, :], banks[b + 1][:, :], ALU.mult), t1)
                        m.release(f"pair{pr_}", t1)
                        t2 = V.do(lambda e: e.tensor_tensor(yy[:, :], s[:, :], rwb[:, k, half(h)], ALU.mult), t1, *m.freed(f"y{k}{ft % 3}"))
                        m.release(f"sl{k}", t2)
                        return t2

                    def low(ft, k, t, t0):
                        pr_ = ft % 3
                        rel = ()
                        if k == 1:
                            rel = (G.do(lambda e: e.tensor_tensor(ys[:, ft, :], y[0][pr_][:, :], y[1][pr_][:, :], ALU.add), t, t0,
                                        *m.freed("ys")),)
                        for ct in range(CT):
                            f = lambda e: e.matmul(banks[4 + 2 * k + ct][:, :], a2[:, ft, ct * P:(ct + 1) * P], y[k][pr_][:, :],
                                                   start=(ft == 0), stop=(ft == FT - 1), skip_group_check=True)
                            tt_ = (PE.do if ct else PE.quiet)(f, t, *m.freed(f"bank{4 + 2 * k + ct}"))
                        if k == 1:
                            m.release(f"y1{pr_}", tt_, *rel)
                            m.release(f"y0{pr_}", tt_, *rel)
                        return rel[0] if rel else None

                    t0 = {}
                    tg = None
                    order = []
                    for ft in range(FT + 1):
                        if ft < FT:
                            order.append((ft, 0))
                        if ft > 0:
                            order.append((ft - 1, 1))
                    for ft, k in order:
                        t0[ft, k] = up(ft, k)
                        if (ft, k) == (0, 0):
                            continue
                        if k == 1:
                            low(ft, 0, t0[ft, 0], None)
                            if ft > 0:
                                tg = low(ft - 1, 1, t0[ft - 1, 1], t0[ft - 1, 0])
                    tg = low(FT - 1, 1, t0[FT - 1, 1], t0[FT - 1, 0])
                    t = PE.here()
                    for ct in range(CT):
                        ta = V.do(lambda e: e.tensor_tensor(u2[:, ct, :], maskx[:, 0, ct, half(h)], banks[4 + ct][:, :], ALU.mult),
                                  t, *m.freed("u2"))
                        tb = V.do(lambda e: e.tensor_tensor(u3[:, :], maskx[:, 1, ct, half(h)], banks[6 + ct][:, :], ALU.mult), ta)
                        ta = V.do(lambda e: e.tensor_tensor(u2[:, ct, :], u2[:, ct, :], u3[:, :], ALU.add), ta, tb)
                    for b in range(4, 8):
                        m.release(f"bank{b}", ta)
                    for ct in range(CT):
                        cs = slice(ct * P, (ct + 1) * P)
                        t = mm(banks[4 + ct][:, :], [(w2[:, ft, cs], ys[:, ft, :]) for ft in range(FT)] +
                               [(b2w[:, c, cs], u2[:, c, :]) for c in range(CT)], tg, ta)
                        o = XT[:, ct, half(h)]
                        t4 = V.do(lambda e: e.tensor_tensor(o, o, banks[4 + ct][:, :], ALU.add), t)
                        m.release(f"bank{4 + ct}", t4)
                    m.release("u2", t)
                    m.release("ys", t)

    def grouped_attention():
        D, KV, R = 128, 4, 4
        SC = float(D) ** -0.5
        with Phase() as buf:
            wqk = buf("g_wqk", [P, CT, (R + 1) * D])
            wgv = buf("g_wgv", [P, CT, (R + 1) * D])
            wo = buf("g_wo", [P, R, C])
            rc = buf("g_rc", [P, T])
            rsn = buf("g_rsn", [P, T])
            rot = buf("g_rot", [P, P])
            msk = buf("g_msk", [P, P + T])
            load(ctr("g"), rc[:, :], d["rope_cos"])
            load(ctr("g"), rsn[:, :], d["rope_sin"])
            load(ctr("g"), rot[:, :], d["rope_rot"])
            t_c = load(ctr("g"), msk[:, :], d["causal"])
            ready = condition(4)
            q = buf("g_q", [P, R + 1, TOK])
            v = buf("g_v", [P, TT, D])
            th = buf("g_th", [P, R, TOK])
            xc = [buf(f"g_xc{i}", [P, HALF]) for i in range(2)]
            sq = [buf(f"g_sq{i}", [P, HALF]) for i in range(2)]
            pp = [buf(f"g_p{i}", [P, 384]) for i in range(3)]
            pt = [buf(f"g_pt{i}", [P, 384]) for i in range(2)]
            st = buf("g_st", [P, 3, 8])
            gate = buf("g_gate", [P, 2])
            m.fence()
            for lane in (PE, V, G, A):
                lane.wait(t_c)

            def body(g):
                t_qk = load(ctr("gqk"), wqk[:, :, :], lambda: d["g_qk"][g], *m.freed("wqk"))
                t_gv = load(ctr("ggv"), wgv[:, :, :], lambda: d["g_gv"][g], *m.freed("wgv"))
                t_wo = load(ctr("gwo"), wo[:, :, :], lambda: d["g_wo"][g], *m.freed("wo"))
                n = 0
                q_ready = {}
                for hd in [R] + list(range(R)):
                    wn, bn = ("g_kn_w", "g_kn_b") if hd == R else ("g_qn_w", "g_qn_b")
                    for h in range(NH):
                        i = n % 2
                        n += 1
                        b = 4 * i
                        x_, s_ = xc[i], sq[i]
                        o = q[:, hd, half(h)]
                        bks = (*m.freed(f"set{i}"),)
                        t = mm(banks[b][:, :], [(wqk[:, k, hd * D:(hd + 1) * D], XC[:, k, half(h)]) for k in range(CT)], t_qk, *bks)
                        t = A.do(lambda e: e.copy(x_[:, :], banks[b][:, :]), t, *m.freed(f"x{i}"))
                        t = mm(banks[b + 1][:, :], [(ones[:, :], x_[:, :])], t)
                        t = V.do(lambda e: e.scalar_tensor_tensor(x_[:, :], banks[b + 1][:, :], -1.0 / D, x_[:, :], ALU.mult, ALU.add), t)
                        t2 = A.do(lambda e: e.activation(s_[:, :], x_[:, :], ACT.Square), t)
                        t2 = mm(banks[b + 2][:, :], [(ones[:, :], s_[:, :])], t2)
                        t2 = A.do(lambda e: e.activation(s_[:, :], banks[b + 2][:, :], ACT.Ln, scale=1.0 / D, bias=eps_col(1e-6)), t2)
                        t2 = A.do(lambda e: e.activation(s_[:, :], s_[:, :], ACT.Exp, scale=-0.5), t2)
                        t = V.do(lambda e: e.tensor_tensor(x_[:, :], x_[:, :], s_[:, :], ALU.mult), t2)
                        t = V.do(lambda e: e.tensor_scalar(x_[:, :], x_[:, :], vcol(wn), vcol(bn), ALU.mult, ALU.add), t)
                        t2 = mm(banks[b + 3][:, :], [(rot[:, :], x_[:, :])], t)
                        o3 = o.rearrange("p (b t) -> p b t", b=2)
                        tg = G.do(lambda e: e.tensor_tensor(o3, x_[:, :].rearrange("p (b t) -> p b t", b=2),
                                                            rc[:, :].unsqueeze(1).to_broadcast([P, 2, T]), ALU.mult), t, *m.freed("q"))
                        t2 = V.do(lambda e: e.tensor_tensor(s_[:, :].rearrange("p (b t) -> p b t", b=2),
                                                            banks[b + 3][:, :].rearrange("p (b t) -> p b t", b=2),
                                                            rsn[:, :].unsqueeze(1).to_broadcast([P, 2, T]), ALU.mult), t2)
                        m.release(f"set{i}", t2)
                        t2 = V.do(lambda e: e.tensor_tensor(o, o, s_[:, :], ALU.add), t2, tg)
                        m.release(f"x{i}", t2)
                        q_ready[hd, h] = t2
                m.release("wqk", PE.here())
                for hd in range(R):
                    for h in range(NH):
                        i = n % 2
                        n += 1
                        b = 4 * i
                        t = mm(banks[b][:, :], [(wgv[:, k, hd * D:(hd + 1) * D], XC[:, k, half(h)]) for k in range(CT)], t_gv,
                               *m.freed(f"set{i}"))
                        t = A.do(lambda e: e.activation(th[:, hd, half(h)], banks[b][:, :], ACT.Tanh, scale=0.5), t, *m.freed("th"))
                        m.release(f"set{i}", t)
                t_th = t
                for tt in range(TT):
                    i = tt % 2
                    b = 4 * i + 1
                    t = mm(banks[b][:, 0:D], [(XC[:, k, tt * P:(tt + 1) * P], wgv[:, k, R * D:(R + 1) * D]) for k in range(CT)],
                           *m.freed(f"set{i}"))
                    t = A.do(lambda e: e.copy(v[:, tt, :], banks[b][:, 0:D]), t, *m.freed("v"))
                    m.release(f"set{i}", t)
                t_v = t
                m.release("wgv", PE.here())
                set_free = m.freed("set0") + m.freed("set1")
                for b in range(8):
                    m.release(f"bank{b}", *set_free)
                units = [(b, hd) for b in range(NB) for hd in range(R)]

                def scores(n):
                    b, hd = units[n]
                    t0 = b * T
                    bk, s, c = n % 3, pp[n % 3], 2 * (n % 4)
                    kk = q[:, R, t0:t0 + T]
                    rdy = (q_ready[hd, b // 2], q_ready[R, b // 2])
                    PE.quiet(lambda e: e.matmul(banks[bk][:, 0:P], q[:, hd, t0:t0 + P], kk[:, 0:P], start=True, stop=True,
                                                skip_group_check=True), *rdy, *m.freed(f"bank{bk}"))
                    t = PE.do(lambda e: e.matmul(banks[bk][:, P:P + T], q[:, hd, t0 + P:t0 + T], kk, start=False, stop=True,
                                                 skip_group_check=True))
                    V.do(lambda e: e.memset(gate[:, n % 2:n % 2 + 1], 0.0), t, *m.freed(f"p{n % 3}"))
                    for i, cols in enumerate((slice(0, P), slice(P, P + T))):
                        t = V.do(lambda e: e.tensor_tensor_reduce(s[:, cols], banks[bk][:, cols], msk[:, cols], 1.0, -BIG,
                                                                  ALU.add, ALU.max, st[:, 0, c + i:c + i + 1]))
                    m.release(f"bank{bk}", t)
                    t = V.do(lambda e: e.tensor_scalar(st[:, 0, c:c + 2], st[:, 0, c:c + 2], -SC, None, ALU.mult), t)
                    for i, cols in enumerate((slice(0, P), slice(P, P + T))):
                        ta = A.do(lambda e: e.activation(s[:, cols], s[:, cols], ACT.Exp, bias=st[:, 0, c + i:c + i + 1], scale=SC,
                                                         accum_out=st[:, 1, c + i:c + i + 1]), t)
                    return ta

                def turn(n, ta):
                    c, s, p_ = 2 * (n % 4), pp[n % 3], pt[n % 2]
                    bk = 3 + n % 2
                    t = V.do(lambda e: e.reciprocal(st[:, 2, c:c + 2], st[:, 1, c:c + 2]), ta)
                    for i, cols in enumerate((slice(0, P), slice(P, P + T))):
                        t1 = V.do(lambda e: e.tensor_scalar(s[:, cols], s[:, cols], st[:, 2, c + i:c + i + 1], None, ALU.mult), t)
                    for i in range(3):
                        t = PE.do(lambda e: e.transpose(banks[bk][:, i * P:(i + 1) * P], s[:, i * P:(i + 1) * P], ident[:, :]), t1,
                                  *m.freed(f"bank{bk}"))
                    m.release(f"p{n % 3}", t)
                    t = A.do(lambda e: e.copy(p_[:, :], banks[bk][:, 0:384]), t, *m.freed(f"pt{n % 2}"))
                    m.release(f"bank{bk}", t)
                    return t

                def mix(n, t):
                    b, hd = units[n]
                    p_, bk = pt[n % 2], 5 + n % 2
                    v0, v1 = v[:, 2 * b, :], v[:, 2 * b + 1, :]
                    PE.quiet(lambda e: e.matmul(banks[bk][:, 0:P], v0, p_[:, 0:P], start=True, stop=True, skip_group_check=True),
                             t, t_v, *m.freed(f"bank{bk}"))
                    PE.quiet(lambda e: e.matmul(banks[bk][:, P:T], v0, p_[:, P:2 * P], start=False, stop=False, skip_group_check=True))
                    t = PE.do(lambda e: e.matmul(banks[bk][:, P:T], v1, p_[:, 2 * P:3 * P], start=False, stop=True, skip_group_check=True))
                    m.release(f"pt{n % 2}", t)
                    o = th[:, hd, b * T:(b + 1) * T]
                    t = V.do(lambda e: e.scalar_tensor_tensor(o, o, 1.0, banks[bk][:, 0:T], ALU.add, ALU.mult), t, t_th)
                    m.release(f"bank{bk}", t)
                    return t

                p1, p2 = [], []
                for n in range(len(units)):
                    p1.append((n, scores(n)))
                    if len(p1) > 2:
                        a = p1.pop(0)
                        p2.append((a[0], turn(*a)))
                    if len(p2) > 1:
                        mix(*p2.pop(0))
                for a in p1:
                    p2.append((a[0], turn(*a)))
                    mix(*p2.pop(0))
                for a in p2:
                    t = mix(*a)
                m.release("q", PE.here())
                m.release("v", PE.here())
                for ct in range(CT):
                    for h in range(NH):
                        b = ct * NH + h
                        t2 = mm(banks[b][:, :], [(wo[:, hd, ct * P:(ct + 1) * P], th[:, hd, half(h)]) for hd in range(R)],
                                t, t_wo, *m.freed(f"bank{b}"))
                        o = XT[:, ct, half(h)]
                        t3 = V.do(lambda e: e.scalar_tensor_tensor(o, banks[b][:, :], 0.5, o, ALU.mult, ALU.add), t2)
                        m.release(f"bank{b}", t3)
                m.release("wo", t2)
                m.release("th", t2)
                every = sum((m.freed(f"bank{b}") for b in range(8)), ())
                m.release("set0", *every)
                m.release("set1", *every)

            m.run_loop(KV, body)

    def quantised_ffn():
        I = 704
        OT = 2 * I // P
        IT = 6
        CH = [(0, 512), (512, 192)]
        with Phase() as buf:
            w1t = buf("q_w1t", [P, CT, 2 * I], BF16)
            w2t = buf("q_w2t", [P, IT, C], BF16)
            s1b = buf("q_s1b", [P, 2 * I])
            s2b = buf("q_s2b", [P, C])
            st = buf("q_st", [P, 4, 16])

            def quantise(src, dst, tmp, c, t, *more):
                t = V.do(lambda e: e.tensor_reduce(st[:, 0, c:c + 1], src, AX, ALU.max, apply_absolute_value=True), t)
                t = V.do(lambda e: e.tensor_scalar(st[:, 0, c:c + 1], st[:, 0, c:c + 1], 1.0 / 127.0, 1e-8, ALU.mult, ALU.max), t)
                t = V.do(lambda e: e.reciprocal(st[:, 1, c:c + 1], st[:, 0, c:c + 1]), t)
                t = V.do(lambda e: e.tensor_scalar(tmp, src, st[:, 1, c:c + 1], ROUND, ALU.mult, ALU.add), t)
                t = V.do(lambda e: e.tensor_scalar(tmp, tmp, -ROUND, 127.0, ALU.add, ALU.min), t)
                return V.do(lambda e: e.tensor_scalar(dst, tmp, -127.0, None, ALU.max), t, *more)

            with Phase() as b2:
                w1 = b2("q_w1", [P, OT, C])
                w2 = b2("q_w2", [P, CT, I])
                wb = [b2(f"q_wb{i}", [P, I], BF16) for i in range(2)]
                tmp = b2("q_tmp", [P, I])
                diag = b2("q_diag", [P, P])
                pb = [banks[6][:, :].bitcast(BF16), banks[7][:, :].bitcast(BF16)]
                load(ctr("q"), w1[:, :, :], d["q_w1"])
                t_w = load(ctr("q"), w2[:, :, :], d["q_w2"])
                n = 0
                for o in range(OT + CT):
                    first = o < OT
                    src = w1[:, o, :] if first else w2[:, o - OT, :]
                    ncol = C if first else I
                    i = n % 2
                    t = quantise(src, wb[i][:, 0:ncol], tmp[:, 0:ncol], o, t_w, *m.freed(f"wb{i}"))
                    td = V.do(lambda e: e.tensor_scalar(diag[:, :], ident[:, :], st[:, 0, o:o + 1], None, ALU.mult), t, *m.freed("diag"))
                    t2 = mm(banks[0][:, 0:P], [(ones[:, :], diag[:, :])], td, *m.freed("bank0"))
                    m.release("diag", t2)
                    ds = s1b[:, o * P:(o + 1) * P] if first else s2b[:, (o - OT) * P:(o - OT + 1) * P]
                    t2 = A.do(lambda e: e.copy(ds, banks[0][:, 0:P]), t2)
                    m.release("bank0", t2)
                    blocks = [(c, min(P, ncol - c * P)) for c in range((ncol + P - 1) // P)]
                    for c, w_ in blocks:
                        t3 = PE.do(lambda e: e.transpose(pb[i][0:w_, c * P:(c + 1) * P], wb[i][:, c * P:c * P + w_], identb[:, :]),
                                   t, *m.freed(f"pb{i}"))
                    m.release(f"wb{i}", t3)
                    for c, w_ in blocks:
                        dt = w1t[:, c, o * P:(o + 1) * P] if first else w2t[0:w_, c, (o - OT) * P:(o - OT + 1) * P]
                        t4 = A.do(lambda e: e.copy(dt, pb[i][0:w_, c * P:(c + 1) * P]), t3)
                    m.release(f"pb{i}", t4)
                    n += 1
            ready = condition(5)
            with Phase() as b2:
                xt = [b2(f"q_x{i}", [P, C]) for i in range(2)]
                xb = [b2(f"q_xb{i}", [P, C], BF16) for i in range(2)]
                xqt = [b2(f"q_xqt{i}", [P, CT, P], BF16) for i in range(2)]
                tmp = [b2(f"q_t{i}", [P, I]) for i in range(2)]
                g = [b2(f"q_g{i}", [P, 2 * I]) for i in range(2)]
                hb = [b2(f"q_hb{i}", [P, I], BF16) for i in range(2)]
                hqt = [b2(f"q_hqt{i}", [P, IT, P], BF16) for i in range(2)]
                ob = [b2(f"q_ob{i}", [P, C]) for i in range(2)]
                pb = [banks[5][:, :].bitcast(BF16), banks[6][:, :].bitcast(BF16)]

                def stage1(tt):
                    i = tt % 2
                    for ct in range(CT):
                        t = PE.do(lambda e: e.transpose(banks[4][:, ct * P:(ct + 1) * P], XC[:, ct, tt * P:(tt + 1) * P], ident[:, :]),
                                  *ready, *m.freed("bank4"))
                    t = A.do(lambda e: e.copy(xt[i][:, :], banks[4][:, 0:C]), t, *m.freed(f"xt{i}"))
                    m.release("bank4", t)
                    t = quantise(xt[i][:, :], xb[i][:, :], xt[i][:, :], i, t, *m.freed(f"xb{i}"))
                    m.release(f"xt{i}", t)
                    for ct in range(CT):
                        t = PE.do(lambda e: e.transpose(pb[0][:, ct * P:(ct + 1) * P], xb[i][:, ct * P:(ct + 1) * P], identb[:, :]),
                                  t, *m.freed("pb0"))
                    m.release(f"xb{i}", t)
                    t = A.do(lambda e: e.copy(xqt[i][:, :, :].rearrange("p c t -> p (c t)"), pb[0][:, 0:C]), t, *m.freed(f"xqt{i}"))
                    m.release("pb0", t)
                    for j in range(2):
                        for n, (c0_, w_) in enumerate(CH):
                            b = 2 * j + n
                            t2 = mm(banks[b][:, 0:w_], [(xqt[i][:, k, :], w1t[:, k, j * I + c0_:j * I + c0_ + w_]) for k in range(CT)],
                                    t, *m.freed(f"bank{b}"))
                            gs = g[i][:, j * I + c0_:j * I + c0_ + w_]
                            t3 = V.do(lambda e: e.scalar_tensor_tensor(gs, banks[b][:, 0:w_], st[:, 0, i:i + 1],
                                                                       s1b[:, j * I + c0_:j * I + c0_ + w_], ALU.mult, ALU.mult),
                                      t2, *m.freed(f"g{i}"))
                            m.release(f"bank{b}", t3)
                            if j == 0 and n == 1:
                                m.release(f"xqt{i}", t2)
                                ta = A.do(lambda e: e.activation(tmp[i][:, :], g[i][:, 0:I], ACT.Silu), t3, *m.freed(f"tmp{i}"))
                    m.release(f"xqt{i}", t2)
                    t = V.do(lambda e: e.tensor_tensor(tmp[i][:, :], tmp[i][:, :], g[i][:, I:2 * I], ALU.mult), ta, t3)
                    m.release(f"g{i}", t)
                    return t

                def stage2(tt, t):
                    i = tt % 2
                    t = quantise(tmp[i][:, :], hb[i][:, :], tmp[i][:, :], 2 + i, t, *m.freed(f"hb{i}"))
                    m.release(f"tmp{i}", t)
                    for c in range(IT):
                        w_ = min(P, I - c * P)
                        t2 = PE.do(lambda e: e.transpose(pb[1][0:w_, c * P:(c + 1) * P], hb[i][:, c * P:c * P + w_], identb[:, :]),
                                   t, *m.freed("pb1"))
                    m.release(f"hb{i}", t2)
                    t3 = A.do(lambda e: e.copy(hqt[i][:, 0:IT - 1, :].rearrange("p c t -> p (c t)"), pb[1][:, 0:(IT - 1) * P]), t2,
                              *m.freed(f"hqt{i}"))
                    t3 = A.do(lambda e: e.copy(hqt[i][0:64, IT - 1, :], pb[1][0:64, (IT - 1) * P:IT * P]), t2)
                    m.release("pb1", t3)
                    pairs = [(hqt[i][0:min(P, I - c * P), c, :], w2t[0:min(P, I - c * P), c, :]) for c in range(IT)]
                    t3 = mm(banks[7][:, 0:C], pairs, t3, *m.freed("bank7"))
                    m.release(f"hqt{i}", t3)
                    t3 = V.do(lambda e: e.scalar_tensor_tensor(ob[i][:, :], banks[7][:, 0:C], st[:, 0, 2 + i:3 + i], s2b[:, :],
                                                               ALU.mult, ALU.mult), t3, *m.freed(f"ob{i}"))
                    for ct in range(CT):
                        t4 = PE.do(lambda e: e.transpose(banks[7][:, C + ct * P:C + (ct + 1) * P], ob[i][:, ct * P:(ct + 1) * P],
                                                         ident[:, :]), t3)
                    m.release(f"ob{i}", t4)
                    o = XT[:, :, tt * P:(tt + 1) * P]
                    t4 = V.do(lambda e: e.tensor_tensor(o, o, banks[7][:, C:2 * C].rearrange("p (c t) -> p c t", c=CT), ALU.add), t4)
                    m.release("bank7", t4)

                pend = None
                for tt in range(TT):
                    t = stage1(tt)
                    if pend:
                        stage2(*pend)
                    pend = (tt, t)
                stage2(*pend)

    def selective_scan():
        EI, N, ET = 512, 16, 4
        GN = 4
        HB = NB // 2
        ready = condition(6)
        wkv_factor(7)
        side.__exit__()
        with Phase() as buf:
            u = buf("s_u", [P, ET, TOK])
            dl = buf("s_dl", [P, ET, TOK])
            y = buf("s_y", [P, ET, TOK])
            bcr = buf("s_bcr", [2 * N, TOK])
            with Phase() as b2:
                sq = b2("s_sq", [P, CT, TOK])
                rs = b2("s_rs", [P, TOK])
                win = b2("s_win", [P, CT, EI])
                wd1 = b2("s_wd1", [P, ET, P])
                wd2 = b2("s_wd2", [P, 1, EI])
                wbc = b2("s_wbc", [P, ET, 2 * N])
                up = [b2(f"s_up{i}", [P, NB, T + 3]) for i in range(2)]
                r1 = b2("s_r1", [P, TOK])
                tmp = [b2(f"s_tmp{i}", [P, HALF]) for i in range(2)]
                load(ctr("s"), win[:, :, :], d["s_win"])
                load(ctr("s"), wd1[:, :, :], d["s_wd1"])
                load(ctr("s"), wd2[:, :, :], d["s_wd2"])
                t_w = load(ctr("s"), wbc[:, :, :], d["s_wbc"])
                t = inverse_root(XC, ready, sq, rs, 1e-5)
                rdy = scale_rows(XC, rs, "s_norm", sq, t)
                for i in range(2):
                    t_z = V.do(lambda e: e.memset(up[i][:, :, 0:3], 0.0))
                for et in range(ET):
                    i = et % 2
                    for h in range(NH):
                        b = (2 * et + h) % 4
                        t = mm(banks[b][:, :], [(win[:, k, et * P:(et + 1) * P], sq[:, k, half(h)]) for k in range(CT)],
                               *rdy, t_w, *m.freed(f"bank{b}"))
                        t = A.do(lambda e: e.copy(up[i][:, 2 * h:2 * h + 2, 3:T + 3],
                                                  banks[b][:, :].rearrange("p (b t) -> p b t", b=2)), t, t_z, *m.freed(f"up{i}"))
                        m.release(f"bank{b}", t)
                    uo = u[:, et, :].rearrange("p (b t) -> p b t", b=NB)
                    t = V.do(lambda e: e.tensor_scalar(uo, up[i][:, :, 0:T], vcol("s_conv", et * 4), vcol("s_conv_b", et),
                                                       ALU.mult, ALU.add), t)
                    for j in range(1, 4):
                        t = V.do(lambda e: e.scalar_tensor_tensor(uo, up[i][:, :, j:j + T], vcol("s_conv", et * 4 + j), uo,
                                                                  ALU.mult, ALU.add), t)
                    m.release(f"up{i}", t)
                    t_u = A.do(lambda e: e.activation(u[:, et, :], u[:, et, :], ACT.Silu), t)
                for h in range(NH):
                    b = 4 + h
                    t = mm(banks[b][:, :], [(wd1[:, k, :], u[:, k, half(h)]) for k in range(ET)], t_u)
                    t_r = A.do(lambda e: e.copy(r1[:, half(h)], banks[b][:, :]), t)
                    t = mm(banks[b + 2][0:2 * N, :], [(wbc[:, k, :], u[:, k, half(h)]) for k in range(ET)])
                    A.do(lambda e: e.copy(bcr[:, half(h)], banks[b + 2][0:2 * N, :]), t)
                for et in range(ET):
                    for h in range(NH):
                        b = (2 * et + h) % 4
                        i = h
                        o = dl[:, et, half(h)]
                        t = mm(banks[b][:, :], [(wd2[:, 0, et * P:(et + 1) * P], r1[:, half(h)])], t_r, *m.freed(f"bank{b}"))
                        t = A.do(lambda e: e.activation(o, banks[b][:, :], ACT.Identity, bias=vcol("s_bd2", et)), t)
                        m.release(f"bank{b}", t)
                        t2 = A.do(lambda e: e.activation(tmp[i][:, :], o, ACT.Abs), t, *m.freed(f"tmp{i}"))
                        t2 = A.do(lambda e: e.activation(tmp[i][:, :], tmp[i][:, :], ACT.Exp, scale=-1.0), t2)
                        t2 = A.do(lambda e: e.activation(tmp[i][:, :], tmp[i][:, :], ACT.Ln, bias=eps_col(1.0)), t2)
                        t2 = V.do(lambda e: e.scalar_tensor_tensor(o, o, 0.0, tmp[i][:, :], ALU.max, ALU.add), t2)
                        m.release(f"tmp{i}", t2)
            with Phase() as b2:
                rep = b2("s_rep", [P, 2, N, HALF])
                sel = b2("s_sel", [2 * N, 2 * N, P])
                an = b2("s_an", [P, ET, N])
                du = b2("s_du", [P, HALF])
                da = [b2(f"s_da{i}", [P, GN, HALF]) for i in range(2)]
                bu = [b2(f"s_bu{i}", [P, GN, HALF]) for i in range(2)]
                load(ctr("s2"), sel[:, :, :], d["sel32"])
                t_w = load(ctr("s2"), an[:, :, :], d["s_alog"])
                t = A.do(lambda e: e.activation(an[:, :, :], an[:, :, :], ACT.Exp), t_w)
                t_an = V.do(lambda e: e.tensor_scalar(an[:, :, :], an[:, :, :], -1.0, None, ALU.mult), t)
                for h in range(NH):
                    for n in range(2 * N):
                        b = n % 4
                        t = mm(banks[b][:, :], [(sel[:, n, :], bcr[:, half(h)])], t_w, *m.freed(f"bank{b}"))
                        o = rep[:, n // N, n % N, :]
                        t = A.do(lambda e: e.copy(o, banks[b][:, :]), t, *m.freed("rep")) if n % 2 else \
                            V.do(lambda e: e.tensor_copy(o, banks[b][:, :]), t, *m.freed("rep"))
                        m.release(f"bank{b}", t)
                    m.fence()
                    k = 0
                    for et in range(ET):
                        bk = 4 + et
                        t_du = V.do(lambda e: e.tensor_tensor(du[:, :], dl[:, et, half(h)], u[:, et, half(h)], ALU.mult), *m.freed("du"))
                        for gn in range(N // GN):
                            i = k % 2
                            k += 1
                            for n in range(GN):
                                t = A.do(lambda e: e.activation(da[i][:, n, :], dl[:, et, half(h)], ACT.Exp,
                                                                scale=an[:, et, gn * GN + n:gn * GN + n + 1]), t_an, *m.freed(f"da{i}"))
                            dz = da[i][:, :, :].rearrange("p n (b t) -> p (n b) t", b=HB)[:, :, 0:1]
                            t = V.do(lambda e: e.memset(dz, 0.0), t)
                            tb = G.do(lambda e: e.tensor_tensor(bu[i][:, :, :], rep[:, 0, gn * GN:(gn + 1) * GN, :],
                                                                du[:, :].unsqueeze(1).to_broadcast([P, GN, HALF]), ALU.mult),
                                      t_du, *m.freed(f"bu{i}"))
                            m.release("du", tb)
                            fl = lambda a: a[:, :, :].rearrange("p n t -> p (n t)")
                            t = V.do(lambda e: e.tensor_tensor_scan(fl(bu[i]), fl(da[i]), fl(bu[i]), 0.0, ALU.mult, ALU.add), t, tb)
                            m.release(f"da{i}", t)
                            t = V.do(lambda e: e.tensor_tensor(bu[i][:, :, :], bu[i][:, :, :], rep[:, 1, gn * GN:(gn + 1) * GN, :],
                                                               ALU.mult), t)
                            m.release("rep", t)
                            for n in range(GN):
                                f = lambda e: e.matmul(banks[bk][:, :], ident[:, :], bu[i][:, n, :], start=(gn == 0 and n == 0),
                                                       stop=(gn == N // GN - 1 and n == GN - 1), skip_group_check=True)
                                tp = (PE.do if n == GN - 1 else PE.quiet)(f, t, *m.freed(f"bank{bk}"))
                            m.release(f"bu{i}", tp)
                        o = y[:, et, half(h)]
                        t = V.do(lambda e: e.scalar_tensor_tensor(o, u[:, et, half(h)], vcol("s_wd", et), banks[bk][:, :],
                                                                  ALU.mult, ALU.add), tp)
                        m.release(f"bank{bk}", t)
            with Phase() as b2:
                sq = b2("s_sq3", [P, CT, TOK])
                rs = b2("s_rs3", [P, TOK])
                wsk = b2("s_wsk", [P, CT, EI])
                wout = b2("s_wout", [P, ET, C])
                sk = [b2(f"s_sk{i}", [P, HALF]) for i in range(2)]
                load(ctr("s3"), wsk[:, :, :], d["s_wskip"])
                t_w = load(ctr("s3"), wout[:, :, :], d["s_wout"])
                t = inverse_root(XC, [None, None], sq, rs, 1e-5)
                rdy = scale_rows(XC, rs, "s_norm", sq, t)
                n = 0
                for et in range(ET):
                    for h in range(NH):
                        b = n % 4
                        i = n % 2
                        n += 1
                        t = mm(banks[b][:, :], [(wsk[:, k, et * P:(et + 1) * P], sq[:, k, half(h)]) for k in range(CT)],
                               *rdy, t_w, *m.freed(f"bank{b}"))
                        t = A.do(lambda e: e.activation(sk[i][:, :], banks[b][:, :], ACT.Silu), t, *m.freed(f"sk{i}"))
                        m.release(f"bank{b}", t)
                        o = y[:, et, half(h)]
                        t = V.do(lambda e: e.tensor_tensor(o, o, sk[i][:, :], ALU.mult), t)
                        m.release(f"sk{i}", t)
                project_residual(wout, ET, y, [t], bank0=4)

    def moe_top4():
        E, I, K = 16, 176, 4
        UT = E * I // P
        PER = 2
        SI = 2 * I
        with Phase() as buf:
            wr = buf("e_wr", [P, CT, 2 * E])
            srow = buf("e_row", [P, 2, E])
            revi = buf("e_revi", [P, TT, E])
            sg = buf("e_sg", [P, CT, 2 * SI])
            sd = buf("e_sd", [P, 3, C])
            load(ctr("e"), wr[:, :, :], d["e_router"])
            load(ctr("e"), srow[:, :, :], d["e_extra"].partition_broadcast(P))
            load(ctr("e"), sg[:, :, :], d["e_shared_gu"])
            load(ctr("e"), sd[:, :, :], d["e_shared_down"])
            t_w = load(ctr("e"), revi[:, :, :], d["revi16"])
            ready = condition(7)
            rows = buf("e_rows", [E, TOK])
            with Phase() as b2:
                lg = b2("e_lg", [P, TT, 2 * E])
                pr = b2("e_pr", [P, TT, E])
                bi = b2("e_bi", [P, TT, E])
                hot = b2("e_hot", [P, TT, E])
                tk = b2("e_tk", [P, TT, E])
                tmp = b2("e_tmp", [P, 2, TT, 16])
                st = b2("e_st", [P, TT])

                def bc(a):
                    return a.unsqueeze(2).to_broadcast([P, TT, E])

                def rowb(n):
                    return srow[:, n, :].unsqueeze(1).to_broadcast([P, TT, E])
                t = token_logits(wr, 2 * E, ready + [t_w])
                t = V.do(lambda e: e.tensor_copy(lg[:, :, :].rearrange("p t e -> p (t e)"), banks[0][:, 0:TT * 2 * E]), t)
                m.release("bank0", t)
                t = A.do(lambda e: e.activation(pr[:, :, :], lg[:, :, 0:E], ACT.Silu), t)
                t = V.do(lambda e: e.tensor_tensor(pr[:, :, :], pr[:, :, :], lg[:, :, E:2 * E], ALU.mult), t)
                t = A.do(lambda e: e.activation(pr[:, :, :], pr[:, :, :], ACT.Abs), t)
                t = V.do(lambda e: e.tensor_reduce(st[:, :], pr[:, :, :], AX, ALU.max), t)
                t = V.do(lambda e: e.tensor_tensor(pr[:, :, :], pr[:, :, :], bc(st[:, :]), ALU.subtract), t)
                t = A.do(lambda e: e.activation(pr[:, :, :], pr[:, :, :], ACT.Exp), t)
                t = V.do(lambda e: e.tensor_reduce(st[:, :], pr[:, :, :], AX, ALU.add), t)
                t = V.do(lambda e: e.reciprocal(st[:, :], st[:, :]), t)
                t = V.do(lambda e: e.tensor_tensor(pr[:, :, :], pr[:, :, :], bc(st[:, :]), ALU.mult), t)
                t = V.do(lambda e: e.tensor_tensor(bi[:, :, :], pr[:, :, :], rowb(1), ALU.add), t)
                t = pick_top(bi[:, :, :], None, tk[:, :, :], revi[:, :, :], tmp, E, t)
                for k in range(1, K):
                    t = pick_top(bi[:, :, :], tk[:, :, :], hot[:, :, :], revi[:, :, :], tmp, E, t)
                    t = V.do(lambda e: e.tensor_tensor(tk[:, :, :], tk[:, :, :], hot[:, :, :], ALU.add), t)
                t = V.do(lambda e: e.tensor_tensor(pr[:, :, :], pr[:, :, :], rowb(0), ALU.mult), t)
                t = V.do(lambda e: e.scalar_tensor_tensor(pr[:, :, :], pr[:, :, :], 1.0, tk[:, :, :], ALU.add, ALU.mult), t)
                t = rows_from_tokens(pr, E, rows, t)
            wgu = [buf(f"e_wgu{j}", [P, CT, 2, P]) for j in range(PER)]
            wd = [buf(f"e_wd{j}", [P, C]) for j in range(PER)]
            sel = [buf(f"e_sel{j}", [E, P]) for j in range(PER)]
            cf = [[buf(f"e_cf{j}{h}", [P, HALF]) for h in range(NH)] for j in range(PER)]
            hbuf = [buf(f"e_h{i}", [P, HALF]) for i in range(3)]
            sbuf = [buf(f"e_s{i}", [P, HALF]) for i in range(2)]
            units = []
            for ft in range(3):
                rws = min(P, SI - ft * P)
                for h in range(NH):
                    units.append(dict(src=XC, wg=[sg[:, k, ft * P:ft * P + rws] for k in range(CT)],
                                      wu=[sg[:, k, SI + ft * P:SI + ft * P + rws] for k in range(CT)],
                                      wd=sd[:, ft, :], rows=rws, h=h, coef=None, first=ft == 0, last=False, waits=[t_w]))
            run_units(units, hbuf, sbuf)

            def body(i):
                toks = []
                for j in range(PER):
                    load(ctr(f"e{j}"), wgu[j][:, :, :, :], lambda: d["e_gu"][i, j], *m.freed(f"w{j}"))
                    load(ctr(f"e{j}"), sel[j][:, :], lambda: d["e_sel"][i, j], *m.freed(f"w{j}"))
                    toks.append(load(ctr(f"e{j}"), wd[j][:, :], lambda: d["e_down"][i, j], *m.freed(f"w{j}")))
                units = []
                for ft in range(PER):
                    for h in range(NH):
                        u = dict(src=XC, wg=[wgu[ft][:, k, 0, :] for k in range(CT)],
                                 wu=[wgu[ft][:, k, 1, :] for k in range(CT)], wd=wd[ft], rows=P, h=h,
                                 first=False, last=True, waits=[toks[ft]])

                        def before(ft=ft, h=h, u=u):
                            nn = ft * NH + h
                            b = 4 + 2 * (nn % 2)
                            t = mm(banks[b][:, :], [(sel[ft][:, :], rows[:, half(h)])], toks[ft], *m.freed(f"pair{nn % 2}"))
                            t = A.do(lambda e: e.copy(cf[ft][h][:, :], banks[b][:, :]), t, *m.freed(f"cf{ft}{h}"))
                            u["coef"] = ((lambda: cf[ft][h][:, :]), t)
                            m.release(f"pair{nn % 2}", t)
                        u["before"] = before
                        u["after"] = (lambda ft=ft, h=h: (m.release(f"w{ft}", PE.here()) if h == 1 else None,
                                                          m.release(f"cf{ft}{h}", V.here())))
                        units.append(u)
                run_units(units, hbuf, sbuf)

            m.run_loop(UT // PER, body)
            add_out_banks()

    stages = [linear_attention, moe_top1, banded_attention, lora_ffn, grouped_attention, quantised_ffn,
              selective_scan, moe_top4]
    buf_mask = None
    for n, stage in enumerate(stages):
        if n >= STOP:
            break
        if stage is lora_ffn:
            ph = Phase()
            buf_mask = ph("r_maskx", [P, 2, CT, TOK])
            stage()
            ph.__exit__()
            continue
        stage()
    m.fence()
    t = SP.issue(lambda e: e.dma_start(out, XT[:, :, :]), count=16, counter=ctr("out"))
    SP.wait(t)


def _constants(np):
    c = {}
    c["ident"] = np.eye(128, dtype=np.float32)
    c["dist"] = (np.arange(256)[None, :] - np.arange(128)[:, None]).astype(np.float32)
    for n in (8, 16):
        c[f"revi{n}"] = np.broadcast_to((n - np.arange(n)).astype(np.float32), (128, 8, n)).copy()
    c["sel16"] = np.broadcast_to(np.eye(16, dtype=np.float32)[:, :, None], (16, 16, 128)).copy()
    c["sel32"] = np.broadcast_to(np.eye(32, dtype=np.float32)[:, :, None], (32, 32, 128)).copy()
    i, j = np.arange(128)[:, None], np.arange(128)[None, :]
    own = (j <= i) & (j >= i - 31)
    prev = (np.arange(32)[None, :] - 32) >= i - 31
    mask = np.full((128, 2, 176), -1e30, np.float32)
    for t in range(2):
        mask[:, t, 0:128][own] = 0.0
        if t:
            mask[:, t, 128:160][prev] = 0.0
        mask[:, t, 160:176] = 0.0
    c["b_mask"] = mask
    diag = np.where(j <= i, 0.0, -1e30).astype(np.float32)
    c["causal"] = np.concatenate([diag, np.zeros((128, 128), np.float32), diag], 1)
    sel = np.zeros((18, 2, 128), np.float32)
    sel[16, 0], sel[17, 1] = 1.0, 1.0
    c["r_sel"] = sel
    selx = np.zeros((18, 2, 2, 128), np.float32)
    for k in range(2):
        for ct in range(2):
            for p in range(128):
                selx[8 * k + ct * 4 + p // 32, k, ct, p] = 1.0
    c["r_selx"] = selx
    inv = 1.0 / 1000000.0 ** (np.arange(0, 128, 2, dtype=np.float32) / 128)
    fr = np.outer(inv, np.arange(256, dtype=np.float32)).astype(np.float32)
    c["rope_cos"] = np.concatenate([np.cos(fr), np.cos(fr)], 0).astype(np.float32)
    c["rope_sin"] = np.concatenate([np.sin(fr), np.sin(fr)], 0).astype(np.float32)
    rot = np.zeros((128, 128), np.float32)
    for p in range(64):
        rot[p + 64, p], rot[p, p + 64] = -1.0, 1.0
    c["rope_rot"] = rot
    es = np.zeros((11, 2, 16, 128), np.float32)
    for f in range(16 * 176):
        es[f // 256, (f // 128) % 2, f // 176, f % 128] = 1.0
    c["e_sel"] = es
    return c


def _layout(inputs, np):
    a = {k: np.asarray(v) for k, v in inputs.items()}

    def km(wt):
        k, o = wt.shape
        return np.ascontiguousarray(wt.reshape(k // 128, 128, o).transpose(1, 0, 2))

    def cols(v, n):
        return v.reshape(n, 128).T

    def acts(x):
        return km(x.transpose(2, 0, 1).reshape(256, 1024))
    r = dict(_constants(np))
    r["x"] = acts(a["x"])
    r["side"] = acts(a["fside_BxSxS_0"])
    r["cond"] = a["cond_512"]
    blocks = [f"L{l}_{c}" for l in range(4) for c in ("cond", "cond2")]
    vec = {"cond_w": np.concatenate([cols(a[f"{b}_w"], 2) for b in blocks], 1),
           "cond_u": np.concatenate([cols(a[f"{b}_u"], 2) for b in blocks], 1),
           "l0_qkv_norm": cols(a["L0_attn_qkv_norm_w"], 2), "l0_norm": cols(a["L0_attn_norm_w"], 2),
           "l0_proj_norm": cols(a["L0_attn_proj_norm_w"], 2),
           "b_ln_scale": cols(a["L1_attn_ln_scale"], 2), "b_ln_bias": cols(a["L1_attn_ln_bias"], 2),
           "s_norm": cols(a["L3_attn_norm_w"], 2), "s_bd2": cols(a["L3_attn_bd2"], 4), "s_wd": cols(a["L3_attn_W_D"], 4),
           "s_conv_b": cols(a["L3_attn_conv_b"], 4),
           "s_conv": a["L3_attn_conv_w"].reshape(4, 128, 4).transpose(1, 0, 2).reshape(128, 16)}
    order = np.concatenate([np.arange(0, 128, 2), np.arange(1, 128, 2)])
    for n, s in (("g_qn_w", "q_norm_w"), ("g_qn_b", "q_norm_b"), ("g_kn_w", "k_norm_w"), ("g_kn_b", "k_norm_b")):
        vec[n] = a["L2_attn_" + s][order][:, None]
    ofs, at = {}, 0
    for n, v in vec.items():
        ofs[n] = at
        at += v.shape[1]
    r["vecs"] = np.ascontiguousarray(np.concatenate(list(vec.values()), 1))
    r["l0_qkv"] = km(a["L0_attn_qkv_w"].T)
    r["l0_proj"] = km(a["L0_attn_proj_w"].T)
    r["l0_s"] = a["L0_attn_s"]
    r["m0_router"] = km(a["L0_ffn_router_w"].T)
    gu = a["L0_ffn_w_gate_up"].reshape(8, 2, 128, 2, 4, 128)
    r["m0_gu"] = np.ascontiguousarray(gu.transpose(0, 4, 2, 1, 3, 5))
    r["m0_down"] = np.ascontiguousarray(a["L0_ffn_w_down"].reshape(8, 4, 128, 256))
    r["m0_shared_gu"] = km(a["L0_ffn_shared_gate_up"])
    r["m0_shared_down"] = km(a["L0_ffn_shared_down"])
    for n, s in (("b_wq", "Wq"), ("b_wk", "Wk"), ("b_wv", "Wv"), ("b_wo", "Wo")):
        r[n] = km(a["L1_attn_" + s].T)
    r["b_global"] = km(a["L1_attn_global_tokens"][0].T)
    r["r_router"] = km(a["L1_ffn_Wg"].T)
    r["r_w1"], r["r_w3"], r["r_w2"] = km(a["L1_ffn_W1"].T), km(a["L1_ffn_W3"].T), km(a["L1_ffn_W2"].T)
    r["r_a1"], r["r_a3"] = km(a["L1_ffn_A1"].reshape(256, 256).T), km(a["L1_ffn_A3"].reshape(256, 256).T)
    r["r_a2"] = km(a["L1_ffn_A2"].reshape(256, 896).T)
    for n, s in (("r_b1", "B1"), ("r_b3", "B3"), ("r_b2", "B2")):
        w = a["L1_ffn_" + s]
        r[n] = km(w.transpose(0, 2, 1).reshape(256, w.shape[1]))
    wqkv = a["L2_attn_w_qkv"]
    wq, wg, wk, wv = wqkv[0:2048], wqkv[2048:4096], wqkv[4096:4608], wqkv[4608:5120]
    wq, wk = wq.reshape(16, 128, 256)[:, order], wk.reshape(4, 128, 256)[:, order]
    wg, wv = wg.reshape(16, 128, 256), wv.reshape(4, 128, 256)
    r["g_qk"] = np.stack([km(np.concatenate([wq[4 * g:4 * g + 4].reshape(512, 256), wk[g]], 0).T) for g in range(4)])
    r["g_gv"] = np.stack([km(np.concatenate([wg[4 * g:4 * g + 4].reshape(512, 256), wv[g]], 0).T) for g in range(4)])
    r["g_wo"] = np.ascontiguousarray(a["L2_attn_w_o"].T.reshape(4, 4, 128, 256).transpose(0, 2, 1, 3))
    r["q_w1"] = km(a["L2_ffn_w_gate_up"])
    r["q_w2"] = km(a["L2_ffn_w_down"])
    r["s_win"], r["s_wskip"] = km(a["L3_attn_W_in"].T), km(a["L3_attn_W_skip"].T)
    r["s_wd1"], r["s_wd2"] = km(a["L3_attn_Wd1"].T), km(a["L3_attn_Wd2"].T)
    r["s_wbc"] = km(np.concatenate([a["L3_attn_WB"], a["L3_attn_WC"]], 0).T)
    r["s_alog"] = km(a["L3_attn_A_log"])
    r["s_wout"] = km(a["L3_attn_W_out"].T)
    r["e_router"] = km(np.concatenate([a["L3_ffn_rg_w"], a["L3_ffn_ru_w"]], 0).T)
    r["e_extra"] = np.stack([a["L3_ffn_extra_scale"], a["L3_ffn_extra_bias"]])
    eg = np.stack([a["L3_ffn_Wg"].reshape(2816, 256), a["L3_ffn_Wu"].reshape(2816, 256)])
    eg = eg.reshape(2, 11, 2, 128, 2, 128)
    r["e_gu"] = np.ascontiguousarray(eg.transpose(1, 2, 5, 4, 0, 3))
    r["e_down"] = np.ascontiguousarray(a["L3_ffn_Wd"].transpose(0, 2, 1).reshape(11, 2, 128, 256))
    r["e_shared_gu"] = km(np.concatenate([a["L3_ffn_Sg"], a["L3_ffn_Su"]], 0).T)
    sd = a["L3_ffn_Sd"].T
    r["e_shared_down"] = km(np.concatenate([sd, np.zeros((32, 256), np.float32)], 0))
    return r, ofs


def kernel(**inputs):
    import numpy as np
    import concourse.bacc as bacc
    from concourse.bass_utils import run_bass_kernel_spmd as run
    arrays, offsets = _layout(inputs, np)
    nc = bacc.Bacc("TRN2", target_bir_lowering=False, num_devices=1)
    arrays = {k: np.ascontiguousarray(v) for k, v in arrays.items()}
    d = {k: nc.dram_tensor("in_" + k, v.shape, mybir.dt.from_np(v.dtype), kind="ExternalInput").ap()
         for k, v in arrays.items()}
    d["vec_offsets"] = offsets
    out = nc.dram_tensor("out_x", [128, 2, 1024], F32, kind="ExternalOutput").ap()
    build_program(nc, d, out)
    r = run(nc, [{"in_" + k: v for k, v in arrays.items()}], core_ids=[0])
    y = np.asarray(r.results[0]["out_x"])
    return np.ascontiguousarray(y.transpose(2, 1, 0).reshape(4, 256, 256))
```

```python
import concourse.bass as bass
from concourse import mybir

F32 = mybir.dt.float32
BF16 = mybir.dt.bfloat16
ALU = mybir.AluOpType
ACT = mybir.ActivationFunctionType
AX = mybir.AxisListType.X

P = 128
C = 256
CT = C // P
NB, T = 4, 256
TOK = NB * T
TT = TOK // P
HALF = 512
NH = TOK // HALF
NCOND = 8
ROUND = 1.5 * 2.0 ** 23
BIG = 1e30
STOP = 99


class Counter:

    def __init__(self, nc, name):
        self.sem, self.n, self.name = nc.alloc_semaphore(name), 0, name
        self.base, self.per = 0, 0


class Token:

    def __init__(self, counter, n, loop, back=0):
        self.counter, self.n, self.loop, self.back = counter, n, loop, back


class Loop:
    def __init__(self, count):
        self.count, self.var, self.dry, self.done = count, None, True, False
        self.base, self.per = {}, {}


class Machine:
    def __init__(self, nc):
        self.nc, self.loop, self.counters, self.free = nc, None, [], {}
        self.pe, self.act, self.dve = Lane(self, nc.tensor, "pe"), Lane(self, nc.scalar, "act"), Lane(self, nc.vector, "dve")
        self.pool, self.sp = Lane(self, nc.gpsimd, "pool"), Lane(self, nc.sync, "sp")
        self.lanes = [self.pe, self.act, self.dve, self.pool]

    def counter(self, name):
        c = Counter(self.nc, name)
        self.counters.append(c)
        if self.loop is not None:
            self.loop.base[c] = 0
        return c

    def release(self, name, *tokens):
        self.free[name] = tokens

    def freed(self, name):
        return self.free.get(name, ())

    def fence(self, sp=True):
        for lane in self.lanes + ([self.sp] if sp else []):
            for other in self.lanes:
                lane.wait(Token(other.counter, other.counter.n, None))
        self.free = {}

    def run_loop(self, count, body):
        assert self.loop is None
        self.fence(sp=False)
        loop = Loop(count)
        for c in self.counters:
            loop.base[c] = c.n
            c.n = 0
        self.loop = loop
        for lane in self.lanes + [self.sp]:
            lane.local = {}
        body(0)
        last = {k: tuple(Token(t.counter, t.n, loop, 1) for t in v) for k, v in self.free.items()}
        for c in self.counters:
            loop.per[c] = c.n
            c.n = 0
        for lane in self.lanes:
            c = lane.counter
            short = loop.per[c] + 1 - loop.base[c]
            if short > 0:
                lane.eng.sem_inc(c.sem, short)
                loop.base[c] += short
        for lane in self.lanes + [self.sp]:
            lane.local = {}
        self.free, loop.dry = last, False
        with self.nc.Fori(0, count) as i:
            loop.var = i
            body(i)
        for c in self.counters:
            assert c.n == loop.per[c], c.name
            c.n = loop.base[c] + count * loop.per[c]
        self.loop, loop.done = None, True
        self.fence()


class Lane:

    def __init__(self, m, eng, name):
        self.m, self.eng, self.counter = m, eng, m.counter("done_" + name)
        self.known, self.local = {}, {}

    def wait(self, t):
        if t is None:
            return
        c, loop = t.counter, t.loop
        if loop is not None and not loop.done:
            assert loop is self.m.loop
            v = t.n - t.back * 10 ** 6
            if self.local.get(c, -10 ** 9) >= v:
                return
            self.local[c] = v
            if not loop.dry:
                off = loop.base[c] + t.n - t.back * loop.per[c]
                self.eng.wait_ge(c.sem, loop.var * loop.per[c] + off)
            return
        v = t.n if loop is None else loop.base[c] + (loop.count - 1) * loop.per[c] + t.n
        if self.known.get(c, 0) >= v or v == 0:
            return
        if self.m.loop is not None:
            assert v <= self.m.loop.base[c]
            if self.m.loop.dry:
                return
        else:
            self.known[c] = v
        self.eng.wait_ge(c.sem, v)

    def issue(self, build, *waits, count=1, counter=None):
        for t in waits:
            self.wait(t)
        loop = self.m.loop
        if loop is None or not loop.dry:
            ins = build(self.eng)
            if count:
                ins.then_inc((counter or self.counter).sem, count)
        c = counter or self.counter
        c.n += count
        return Token(c, c.n, loop)

    def do(self, build, *waits):
        return self.issue(build, *waits)

    def quiet(self, build, *waits):
        return self.issue(build, *waits, count=0)

    def here(self):
        return Token(self.counter, self.counter.n, self.m.loop)


def build_program(nc, d, out):
    m = Machine(nc)
    PE, A, V, G, SP = m.pe, m.act, m.dve, m.pool, m.sp

    def sb(name, shape, dt=F32):
        return nc.alloc_sbuf_tensor(name, shape, dt)

    banks = [nc.alloc_psum_tensor(f"bank{i}", [P, 512], F32) for i in range(8)]

    class Phase:

        def __init__(self):
            self.open = []

        def __enter__(self):
            return self

        def __call__(self, name, shape, dt=F32):
            g = nc.sbuf_tensor(name, shape, dt)
            self.open.append(g)
            return g.__enter__()

        def __exit__(self, *e):
            for g in reversed(self.open):
                g.__exit__(None, None, None)
            m.fence()

    def load(counter, dst, src, *waits):
        return SP.issue(lambda e: e.dma_start(dst() if callable(dst) else dst, src() if callable(src) else src),
                        *waits, count=16, counter=counter)

    ld = {}

    def ctr(name):
        if name not in ld:
            ld[name] = m.counter("load_" + name)
        return ld[name]

    def mm(out_ap, pairs, *waits, start=True, stop=True):
        for n, (lhs, rhs) in enumerate(pairs):
            last = n == len(pairs) - 1
            f = lambda e, l=lhs, r=rhs, s=(start and n == 0), z=(stop and last): e.matmul(
                out_ap, l, r, start=s, stop=z, skip_group_check=True)
            tok = (PE.do if last else PE.quiet)(f, *(waits if n == 0 else ()))
        return tok

    def half(h):
        return slice(h * HALF, (h + 1) * HALF)

    XT = sb("residual", [P, CT, TOK])
    XC = sb("conditioned", [P, CT, TOK])
    ident = sb("ident", [P, P])
    identb = sb("identb", [P, P], BF16)
    ones = sb("ones", [P, P])
    vecs = sb("vecs", [P, d["vecs"].shape[1]])
    eps = sb("eps", [P, 4])
    cond = sb("cond", [P, NB, 64])
    tf = sb("tf", [P, NB])
    decay = sb("decay", [P, NCOND, CT, NB])
    gain = sb("gain", [P, NB])
    factors = [sb(f"factor{i}", [P, CT, TOK]) for i in range(3)]
    SLOT = (0, 1, 0, 1, 0, 1, 2, 0)
    gain8 = sb("gain8", [P, CT * NB])
    side = Phase()
    kv = side("side", [P, CT, TOK])
    ek = side("ek", [P, CT, TOK])
    ekv = side("ekv", [P, CT, TOK])
    wkt = side("wkv_temps", [P, 8, T])
    vofs = d["vec_offsets"]

    def vcol(name, n=0):
        return vecs[:, vofs[name] + n:vofs[name] + n + 1]

    c0 = ctr("start")
    load(c0, XT[:, :, :], d["x"])
    load(c0, kv[:, :, :], d["side"])
    load(c0, ident[:, :], d["ident"])
    load(c0, vecs[:, :], d["vecs"])
    t_start = load(c0, cond[:, :, :], d["cond"].partition_broadcast(P))
    V.do(lambda e: e.memset(ones[:, :], 1.0))
    EPS = {2.0 ** -23: 0, 1e-6: 1, 1e-5: 2, 1.0: 3}
    for v, n in EPS.items():
        t_eps = V.do(lambda e, v=v, n=n: e.memset(eps[:, n:n + 1], v))

    def eps_col(v):
        return eps[:, EPS[v]:EPS[v] + 1]

    t_identb = V.do(lambda e: e.tensor_copy(identb[:, :], ident[:, :]), t_start)

    t = V.do(lambda e: e.reduce_sum(tf[:, :], cond[:, :, :], AX), t_start)
    t = A.do(lambda e: e.activation(tf[:, :], tf[:, :], ACT.Sigmoid), t)
    t_gain = V.do(lambda e: e.tensor_scalar(gain[:, :], tf[:, :], 0.2, 0.8, ALU.mult, ALU.add), t)
    t = V.do(lambda e: e.tensor_scalar(tf[:, :], tf[:, :], 0.5, 0.5, ALU.mult, ALU.add), t_gain)
    wv = vecs[:, vofs["cond_w"]:vofs["cond_w"] + NCOND * CT]
    ta = A.do(lambda e: e.activation(wv, wv, ACT.Exp), t_start)
    ta = A.do(lambda e: e.activation(wv, wv, ACT.Exp, scale=-1.0), ta)
    for b in range(NB):
        t_decay = V.do(lambda e, b=b: e.tensor_scalar(
            decay[:, :, :, b], wv.rearrange("p (l c) -> p l c", c=CT), tf[:, b:b + 1], None, ALU.mult), ta, t)
    for ct in range(CT):
        t = V.do(lambda e, ct=ct: e.tensor_scalar(ek[:, ct, :], kv[:, ct, :], 30.0, None, ALU.min), t_start)
        t = A.do(lambda e, ct=ct: e.activation(ek[:, ct, :], ek[:, ct, :], ACT.Exp), t)
        t = V.do(lambda e, ct=ct: e.tensor_tensor(ekv[:, ct, :], ek[:, ct, :], kv[:, ct, :], ALU.mult), t)
    m.fence()

    def by_unit(a):
        return a[:, :, :].rearrange("p c (b t) -> p (c b) t", t=T)

    for ct in range(CT):
        V.do(lambda e: e.tensor_copy(gain8[:, ct * NB:(ct + 1) * NB], gain[:, :]))

    def wkv_start(l, euk):
        for ct in range(CT):
            t = V.do(lambda e: e.tensor_scalar(euk[:, ct, :], kv[:, ct, :], vcol("cond_u", l * CT + ct), 30.0, ALU.add, ALU.min))
            t = A.do(lambda e: e.activation(euk[:, ct, :], euk[:, ct, :], ACT.Exp), t)
        V.wait(t)

    def wkv_unit(l, u, euk):
        dst = by_unit(factors[SLOT[l]])
        at = lambda a: by_unit(a)[:, bass.ts(u, 1), :].rearrange("p a t -> p (a t)")
        col = lambda a: a[:, bass.ts(u, 1)]
        dec = lambda: decay[:, l, :, :].rearrange("p c b -> p (c b)")[:, bass.ts(u, 1)].to_broadcast([P, T])
        w = [wkt[:, n, :] for n in range(8)]
        t6 = V.do(lambda e: e.tensor_scalar(w[6], at(ekv), 1.0, None, ALU.mult), *m.freed("wkt"))
        t7 = V.do(lambda e: e.tensor_scalar(w[7], at(ek), 1.0, None, ALU.mult))
        yield
        scans = {}
        for n, src, t in ((0, ekv, None), (2, ek, None), (1, w[6], t6), (3, w[7], t7)):
            if t is None:
                scans[n] = V.do(lambda e: e.tensor_tensor_scan(w[n], dec(), at(src), 0.0, ALU.mult, ALU.add), *m.freed("wkt"))
            else:
                scans[n] = V.do(lambda e: e.tensor_tensor_scan(w[n][:, ::-1], dec(), src[:, ::-1], 0.0, ALU.mult, ALU.add), t)
            yield
        te = V.do(lambda e: e.tensor_tensor(w[4], at(euk), at(ek), ALU.subtract))
        yield
        t1 = G.do(lambda e: e.tensor_tensor(w[0], w[0], w[1], ALU.add), scans[0], scans[1], te)
        t3 = V.do(lambda e: e.tensor_tensor(w[2], w[2], w[3], ALU.add), scans[2], scans[3])
        t5 = V.do(lambda e: e.tensor_tensor(w[5], w[4], at(kv), ALU.mult), te)
        yield
        t3 = V.do(lambda e: e.tensor_tensor(w[2], w[2], w[4], ALU.add), t3)
        t1 = G.do(lambda e: e.tensor_tensor(w[0], w[0], w[5], ALU.add), t5, t1)
        yield
        t3 = V.do(lambda e: e.tensor_scalar(w[2], w[2], 1e-8, None, ALU.max), t3)
        yield
        t3 = V.do(lambda e: e.reciprocal(w[2], w[2]), t3)
        yield
        t = V.do(lambda e: e.scalar_tensor_tensor(at(factors[SLOT[l]]), w[0], col(gain8), w[2], ALU.mult, ALU.mult), t1, t3)
        m.release("wkt", t)
        yield

    def wkv_units(jobs):
        for l, u, euk in jobs:
            yield from wkv_unit(l, u, euk)

    def step(background, n):
        for _ in range(n):
            next(background, None)

    def wkv_factor(l):
        with Phase() as buf:
            euk = buf(f"w{l}_euk", [P, CT, TOK])
            wkv_start(l, euk)
            for _ in wkv_units([(l, u, euk) for u in range(CT * NB)]):
                pass

    def condition(l):
        factor = factors[SLOT[l]]
        toks = []
        for ct in range(CT):
            t = A.do(lambda e: e.activation(XC[:, ct, :], XT[:, ct, :], ACT.Sigmoid))
            toks.append(V.do(lambda e: e.tensor_tensor(XC[:, ct, :], XC[:, ct, :], factor[:, ct, :], ALU.mult), t))
        return toks

    def inverse_root(src, ready, sq, dst, e_value, width=C, bank0=0, tiles=CT):
        for ct in range(tiles):
            t = A.do(lambda e: e.activation(sq[:, ct, :], src[:, ct, :], ACT.Square), ready[ct])
        for h in range(NH):
            bk = f"bank{bank0 + h}"
            t2 = mm(banks[bank0 + h][:, :], [(ones[:, :], sq[:, ct, half(h)]) for ct in range(tiles)], t, *m.freed(bk))
            t2 = A.do(lambda e: e.activation(dst[:, half(h)], banks[bank0 + h][:, :], ACT.Ln, scale=1.0 / width,
                                             bias=eps_col(e_value)), t2)
            m.release(bk, t2)
            t3 = A.do(lambda e: e.activation(dst[:, half(h)], dst[:, half(h)], ACT.Exp, scale=-0.5), t2)
        return t3

    def scale_rows(src, rs, wname, dst, t, tiles=CT):
        return [V.do(lambda e: e.scalar_tensor_tensor(dst[:, ct, :], src[:, ct, :], vcol(wname, ct), rs[:, :],
                                                      ALU.mult, ALU.mult), t) for ct in range(tiles)]

    def to_channels(src, dst, ready, bank0=4):
        toks = []
        for tt in range(TT):
            b = bank0 + tt % 4
            for ct in range(CT):
                t = PE.do(lambda e: e.transpose(banks[b][:, ct * P:(ct + 1) * P], src[:, tt, ct * P:(ct + 1) * P], ident[:, :]),
                          ready[tt], *m.freed(f"bank{b}"))
            lane, f = ((A, "copy"), (V, "tensor_copy"))[tt % 2]
            o = dst[:, :, tt * P:(tt + 1) * P]
            i = banks[b][:, 0:C].rearrange("p (c t) -> p c t", c=CT)
            t = A.do(lambda e: e.copy(o, i), t) if tt % 2 else V.do(lambda e: e.tensor_copy(o, i), t)
            m.release(f"bank{b}", t)
            toks.append(t)
        return toks

    def project_residual(w, kt, src, ready, add=None, bank0=0):
        for ct in range(CT):
            for h in range(NH):
                b = bank0 + ct * NH + h
                t = mm(banks[b][:, :], [(w[:, k, ct * P:(ct + 1) * P], src[:, k, half(h)]) for k in range(kt)],
                       *ready, *m.freed(f"bank{b}"))
                o = XT[:, ct, half(h)]
                t = V.do(lambda e: e.tensor_tensor(o, o, banks[b][:, :], ALU.add), t)
                m.release(f"bank{b}", t)
                if add is not None:
                    V.do(lambda e: e.tensor_tensor(o, o, add[:, ct, half(h)], ALU.add), t)

    def ternary(w, n, total, buf, name, t_w):
        part = buf(name + "_part", [P, 2])
        wf = w[:, :, :].rearrange("p c n -> p (c n)")
        t = V.do(lambda e: e.tensor_reduce(part[:, 0:1], wf, AX, ALU.add, apply_absolute_value=True), t_w)
        t = mm(banks[7][:, 0:1], [(ones[:, :], part[:, 0:1])], t, *m.freed("bank7"))
        t = V.do(lambda e: e.tensor_scalar(part[:, 0:1], banks[7][:, 0:1], 1.0 / total, 1e-5, ALU.mult, ALU.max), t)
        m.release("bank7", t)
        t = V.do(lambda e: e.reciprocal(part[:, 1:2], part[:, 0:1]), t)
        t = V.do(lambda e: e.tensor_scalar(wf, wf, part[:, 1:2], ROUND, ALU.mult, ALU.add), t)
        t = V.do(lambda e: e.tensor_scalar(wf, wf, -ROUND, -1.0, ALU.add, ALU.max), t)
        return V.do(lambda e: e.tensor_scalar(wf, wf, 1.0, part[:, 0:1], ALU.min, ALU.mult), t)

    def linear_attention():
        with Phase() as buf:
            wqkv = buf("l0_wqkv", [P, CT, d["l0_qkv"].shape[2]])
            wp = buf("l0_wp", [P, 4, C])
            srow = buf("l0_s", [P, 16])
            dist = buf("l0_dist", [P, T + P])
            decm = buf("l0_decm", [P, 16, T + P])
            t_w = load(ctr("l0"), wqkv[:, :, :], d["l0_qkv"])
            t_s = load(ctr("l0s"), srow[:, :], d["l0_s"].partition_broadcast(P))
            t_p = load(ctr("l0p"), wp[:, :, :], d["l0_proj"])
            t_d = load(ctr("l0d"), dist[:, :], d["dist"])
            ts = V.do(lambda e: e.tensor_scalar(srow[:, :], srow[:, :], -1.0, None, ALU.mult), t_s)
            for h in range(16):
                t = A.do(lambda e: e.activation(decm[:, h, :], dist[:, :], ACT.Exp, scale=srow[:, h:h + 1]), ts, t_d)
                for c_, w_ in ((0, T), (T, P)):
                    t_m = G.do(lambda e: e.affine_select(out=decm[:, h, c_:c_ + w_], in_=decm[:, h, c_:c_ + w_], compare_op=ALU.is_ge,
                                                         fill=0.0, base=0, pattern=[[1, w_]], channel_multiplier=-1), t)
            tq = ternary(wqkv, 768, 768 * C, buf, "l0q", t_w)
            tp = ternary(wp, C, C * C, buf, "l0p", t_p)
            q4 = buf("l0_q4", [P, 4, TOK])
            k4 = buf("l0_k4", [P, 4, TOK])
            v = buf("l0_v", [P, TT, 2 * C])
            heads = lambda a: a.rearrange("p (h d) -> p h d", d=32)[:, :, 0:16]
            t_v0 = G.do(lambda e: e.memset(v[:, :, :], 0.0))
            wkv_factor(0)
            ready = condition(0)
            euk = buf("l0_euk", [P, CT, TOK])
            wkv_start(1, euk)
            with Phase() as b2:
                sq = b2("l0_sq", [P, CT, TOK])
                rs = b2("l0_rs", [P, TOK])
                t = inverse_root(XC, ready, sq, rs, 2.0 ** -23)
                rdy = scale_rows(XC, rs, "l0_qkv_norm", sq, t)
                wq = wqkv
                n = 0
                for dst, base in ((q4, 0), (k4, 2 * C)):
                    for tile in range(4):
                        for h in range(NH):
                            b = n % 4
                            n += 1
                            t = mm(banks[b][:, :], [(wq[:, k, base + tile * P:base + (tile + 1) * P], sq[:, k, half(h)])
                                                    for k in range(CT)], *rdy, tq, *m.freed(f"bank{b}"))
                            o = dst[:, tile, half(h)]
                            t = A.do(lambda e: e.copy(o, banks[b][:, :]), t) if h else V.do(lambda e: e.tensor_copy(o, banks[b][:, :]), t)
                            m.release(f"bank{b}", t)
                for tt in range(TT):
                    b = 4 + tt % 4
                    t = mm(banks[b][:, 0:C], [(sq[:, k, tt * P:(tt + 1) * P], wq[:, k, 4 * C:5 * C]) for k in range(CT)],
                           *rdy, tq, *m.freed(f"bank{b}"))
                    t = V.do(lambda e: e.tensor_copy(heads(v[:, tt, :]), banks[b][:, 0:C].rearrange("p (h d) -> p h d", d=16)), t, t_v0)
                    m.release(f"bank{b}", t)
            with Phase() as b2:
                NPR = 3
                sm = [b2(f"l0_sm{i}", [P, T + P]) for i in range(2 * NPR)]
                o = b2("l0_o", [P, 4, TOK])
                pairs = [(b, tile, jj) for b in range(NB) for tile in range(4) for jj in range(2)]

                def scores(n):
                    b, tile, jj = pairs[n]
                    t0 = b * T
                    for part in range(2):
                        for k in range(2):
                            j, bk = 32 * (2 * jj + k), 2 * (n % NPR) + k
                            ks = slice(t0 + part * P, t0 + (part + 1) * P)
                            cols = slice(T, T + P) if part else slice(0, T)
                            t = PE.do(lambda e: e.matmul(banks[bk][:, cols], k4[j:j + 16, tile, ks],
                                                         q4[j:j + 16, tile, t0 + part * P:t0 + T], start=part == 0, stop=True,
                                                         skip_group_check=True), *m.freed(f"bank{bk}"))
                    for k in range(2):
                        i = 2 * (n % NPR) + k
                        tv = V.do(lambda e: e.tensor_tensor(sm[i][:, :], banks[i][:, 0:T + P], decm[:, 4 * tile + 2 * jj + k, :],
                                                            ALU.mult), t, t_m, *m.freed(f"sm{i}"))
                        m.release(f"bank{i}", tv)
                    return tv

                def mix(n, t):
                    b, tile, jj = pairs[n]
                    bk = 6 + (n // 2) % 2
                    for part in range(2):
                        for k in range(2):
                            j, i, h = 32 * (2 * jj + k), 2 * (n % NPR) + k, 4 * tile + 2 * jj + k
                            cols, src = (slice(P, T), slice(T, T + P)) if part else (slice(0, T), slice(0, T))
                            tp = PE.do(lambda e: e.matmul(banks[bk][j:j + 32, cols], v[:, 2 * b + part, 32 * h:32 * h + 32],
                                                          sm[i][:, src], start=part == 0, stop=True, skip_group_check=True),
                                       t, *(m.freed(f"bank{bk}") if jj == 0 else ()))
                            m.release(f"sm{i}", tp)
                    if jj:
                        t2 = A.do(lambda e: e.mul(o[:, tile, b * T:(b + 1) * T], banks[bk][:, 0:T], 0.25), tp)
                        m.release(f"bank{bk}", t2)

                background = wkv_units([(1, u_, euk) for u_ in range(CT * NB)])
                done = {}
                for n in range(len(pairs) + 2):
                    if n < len(pairs):
                        done[n] = scores(n)
                        step(background, 3)
                    if n >= 2:
                        mix(n - 2, done[n - 2])
                for _ in background:
                    pass
                m.fence()
                sq = q4
                rs = b2("l0_rs2", [P, TOK])
                t = inverse_root(o, [None] * 4, sq, rs, 1e-6, tiles=4)
                rdy = scale_rows(o, rs, "l0_norm", o, t, tiles=4)
                t = inverse_root(o, rdy, sq, rs, 2.0 ** -23, tiles=4)
                rdy = scale_rows(o, rs, "l0_proj_norm", o, t, tiles=4)
                project_residual(wp, 4, o, rdy + [tp])

    def pick_top(scores, taken, hot, revi, tmp, E, t):
        def bc(a):
            return a.unsqueeze(2).to_broadcast([P, TT, E])
        mx = tmp[:, 0, :, 0]
        w = tmp[:, 1, :, 0:E]
        if taken is not None:
            t = V.do(lambda e: e.scalar_tensor_tensor(w, taken, -BIG, scores, ALU.mult, ALU.add), t)
            src = w
        else:
            src = scores
        t = V.do(lambda e: e.tensor_reduce(mx, src, AX, ALU.max), t)
        t = V.do(lambda e: e.tensor_tensor(hot, src, bc(mx), ALU.is_equal), t)
        t = V.do(lambda e: e.tensor_tensor(hot, hot, revi, ALU.mult), t)
        t = V.do(lambda e: e.tensor_reduce(mx, hot, AX, ALU.max), t)
        return V.do(lambda e: e.tensor_tensor(hot, revi, bc(mx), ALU.is_equal), t)

    def token_logits(w, n, ready, bank=0):
        for tt in range(TT):
            for k in range(CT):
                f = lambda e: e.matmul(banks[bank][:, tt * n:(tt + 1) * n], XC[:, k, tt * P:(tt + 1) * P], w[:, k, :],
                                       start=(tt == 0 and k == 0), stop=(k == CT - 1), skip_group_check=True)
                wt = (*ready, *m.freed(f"bank{bank}")) if tt == 0 and k == 0 else ()
                t = (PE.do if (tt == TT - 1 and k == CT - 1) else PE.quiet)(f, *wt)
        return t

    def rows_from_tokens(src, n, dst, t):
        for tt in range(TT):
            b = 6 + tt // 4
            t2 = PE.do(lambda e: e.transpose(banks[b][0:n, (tt % 4) * P:(tt % 4 + 1) * P], src[:, tt, :], ident[:, :]), t,
                       *m.freed(f"bank{b}"))
            if tt % 4 == 3:
                h = tt // 4
                t2 = V.do(lambda e: e.tensor_copy(dst[0:n, half(h)], banks[b][0:n, :]), t2)
                m.release(f"bank{b}", t2)
        return t2

    def gated_unit(src, wg, wu, rows, h, n, coef, hbuf, sbuf, waits):
        b = 4 + 2 * (n % 2)
        bk = f"pair{n % 2}"
        mm(banks[b][0:rows, :], [(wg[k], src[:, k, half(h)]) for k in range(CT)], *waits, *m.freed(bk))
        t = mm(banks[b + 1][0:rows, :], [(wu[k], src[:, k, half(h)]) for k in range(CT)])
        s, o = sbuf[n % 2], hbuf[n % 3]
        t = A.do(lambda e: e.activation(s[0:rows, :], banks[b][0:rows, :], ACT.Silu), t, *m.freed(f"s{n % 2}"))
        t = V.do(lambda e: e.tensor_tensor(o[0:rows, :] if coef is None else s[0:rows, :], s[0:rows, :],
                                           banks[b + 1][0:rows, :], ALU.mult), t, *m.freed(f"h{n % 3}"))
        m.release(bk, t)
        if coef is not None:
            cf, tc = coef
            t = V.do(lambda e: e.tensor_tensor(o[0:rows, :], s[0:rows, :], cf(), ALU.mult), t, tc)
        m.release(f"s{n % 2}", t)
        return t

    def down_unit(wd, rows, h, n, hbuf, first, last, waits):
        for ct in range(CT):
            f = lambda e: e.matmul(banks[ct * NH + h][:, :], wd[0:rows, ct * P:(ct + 1) * P], hbuf[n % 3][0:rows, :],
                                   start=first, stop=last, skip_group_check=True)
            t = PE.quiet(f, *waits) if ct == 0 else PE.do(f)
        m.release(f"h{n % 3}", t)
        return t

    def run_units(units, hbuf, sbuf, background=iter(()), pace=0):
        pend = None
        for n, u in enumerate(units):
            if u.get("before"):
                u["before"]()
            t = gated_unit(u["src"], u["wg"], u["wu"], u["rows"], u["h"], n, u["coef"], hbuf, sbuf, u["waits"])
            step(background, pace)
            if pend:
                down_unit(*pend)
                if pend_after:
                    pend_after()
            pend = (u["wd"], u["rows"], u["h"], n, hbuf, u["first"], u["last"], [t])
            pend_after = u.get("after")
        down_unit(*pend)
        if pend_after:
            pend_after()

    def add_out_banks():
        t0 = PE.here()
        for ct in range(CT):
            for h in range(NH):
                o = XT[:, ct, half(h)]
                V.do(lambda e: e.tensor_tensor(o, o, banks[ct * NH + h][:, :], ALU.add), t0)

    def moe_top1():
        E, F = 8, 512
        FT = F // P
        with Phase() as buf:
            wr = buf("m0_wr", [P, CT, E])
            sg = buf("m0_sg", [P, CT, 2 * F])
            sd = buf("m0_sd", [P, FT, C])
            revi = buf("m0_revi", [P, TT, E])
            selm = buf("m0_sel", [16, 9, P])
            t_w = load(ctr("m0"), wr[:, :, :], d["m0_router"])
            load(ctr("m0"), revi[:, :, :], d["revi8"])
            t_w = load(ctr("m0"), selm[:, :, :], d["sel16"][:, 0:9, :])
            load(ctr("m0s"), sg[:, :, :], d["m0_shared_gu"])
            t_s = load(ctr("m0s"), sd[:, :, :], d["m0_shared_down"])
            euk2 = [buf(f"m0_euk{i}", [P, CT, TOK]) for i in range(2)]
            wkv_start(2, euk2[0])
            wkv_start(3, euk2[1])
            ready = condition(1)
            xs = buf("m0_xs", [P, CT, TOK])
            maskb = buf("m0_mask", [P, E, TOK])
            rows = buf("m0_rows", [16, TOK])
            with Phase() as b2:
                lg = b2("m0_lg", [P, TT, E])
                hot = b2("m0_hot", [P, TT, 9])
                tmp = b2("m0_tmp", [P, 2, TT, 16])
                t = token_logits(wr, E, ready + [t_w])
                t = V.do(lambda e: e.tensor_copy(lg[:, :, :].rearrange("p t e -> p (t e)"), banks[0][:, 0:TT * E]), t)
                m.release("bank0", t)
                tm = V.do(lambda e: e.tensor_reduce(hot[:, :, 8], lg[:, :, :], AX, ALU.max), t)
                ta = A.do(lambda e: e.activation(hot[:, :, 8], hot[:, :, 8], ACT.Sigmoid), tm)
                t = pick_top(lg[:, :, :], None, hot[:, :, 0:8], revi[:, :, :], tmp, E, tm)
                V.wait(ta)
                t = rows_from_tokens(hot, 9, rows, t if False else V.do(lambda e: e.tensor_copy(tmp[:, 0, :, 1], hot[:, :, 8]), ta))
            for e_ in range(9):
                for h in range(NH):
                    b = (e_ * NH + h) % 4
                    t = mm(banks[b][:, :], [(selm[0:9, e_, :], rows[0:9, half(h)])], *m.freed(f"bank{b}"))
                    if e_ < 8:
                        t = A.do(lambda e: e.copy(maskb[:, e_, half(h)], banks[b][:, :]), t)
                    else:
                        for ct in range(CT):
                            t = V.do(lambda e: e.tensor_tensor(xs[:, ct, half(h)], XC[:, ct, half(h)], banks[b][:, :],
                                                               ALU.mult), t)
                    m.release(f"bank{b}", t)
            m.fence()
            wgu = [buf(f"m0_wgu{j}", [P, CT, 2, P]) for j in range(FT)]
            wd = [buf(f"m0_wd{j}", [P, C]) for j in range(FT)]
            hbuf = [buf(f"m0_h{i}", [P, HALF]) for i in range(3)]
            sbuf = [buf(f"m0_s{i}", [P, HALF]) for i in range(2)]
            units = []
            for ft in range(FT):
                for h in range(NH):
                    units.append(dict(src=XC, wg=[sg[:, k, ft * P:(ft + 1) * P] for k in range(CT)],
                                      wu=[sg[:, k, F + ft * P:F + (ft + 1) * P] for k in range(CT)],
                                      wd=sd[:, ft, :], rows=P, h=h, coef=None, first=ft == 0, last=False, waits=[t_s]))
            run_units(units, hbuf, sbuf)

            def body(i):
                toks = []
                for j in range(FT):
                    load(ctr(f"m0w{j}"), wgu[j][:, :, :, :], lambda: d["m0_gu"][i, j], *m.freed(f"wgu{j}"))
                    toks.append(load(ctr(f"m0w{j}"), wd[j][:, :], lambda: d["m0_down"][i, j], *m.freed(f"wd{j}")))
                units = []
                for ft in range(FT):
                    for h in range(NH):
                        cf = (lambda h=h: maskb[:, i, half(h)])
                        units.append(dict(src=xs, wg=[wgu[ft][:, k, 0, :] for k in range(CT)],
                                          wu=[wgu[ft][:, k, 1, :] for k in range(CT)], wd=wd[ft], rows=P, h=h,
                                          coef=(cf, None), first=False, last=True, waits=[toks[ft]],
                                          after=(lambda ft=ft: (m.release(f"wgu{ft}", PE.here()), m.release(f"wd{ft}", PE.here()))) if h == 1 else None))
                background = wkv_units([(2, i, euk2[0]), (3, i, euk2[1])])
                run_units(units, hbuf, sbuf, background, 3)
                for _ in background:
                    pass

            m.run_loop(E, body)
            add_out_banks()

    def banded_attention():
        NG, W = 16, 32
        KS = P + W + NG
        with Phase() as buf:
            wq = buf("b_wq", [P, CT, 2 * C])
            wk = buf("b_wk", [P, CT, 2 * C])
            wv = buf("b_wv", [P, CT, C])
            wo = buf("b_wo", [P, 4, C])
            msk = buf("b_msk", [P, 2, KS])
            small = buf("b_small", [P, CT, NB, W + NG])
            load(ctr("b"), wq[:, :, :], d["b_wq"])
            load(ctr("b"), wk[:, :, :], d["b_wk"])
            load(ctr("b"), wv[:, :, :], d["b_wv"])
            for b in range(NB):
                load(ctr("b"), small[:, :, b, W:W + NG], d["b_global"])
            load(ctr("b"), msk[:, :, :], d["b_mask"])
            t_w = load(ctr("b"), wo[:, :, :], d["b_wo"])
            ready = condition(2)
            q4 = buf("b_q4", [P, 4, TOK])
            k4 = buf("b_k4", [P, 4, TOK])
            ks4 = buf("b_ks4", [P, 4, NB * (W + NG)])
            v = buf("b_v", [P, TT, 2 * C])
            vs = buf("b_vs", [W + NG, NB, 2 * C])
            heads = lambda a: a.rearrange("p (h d) -> p h d", d=32)[:, :, 0:16]
            G.do(lambda e: e.memset(v[:, :, :], 0.0))
            t_v0 = G.do(lambda e: e.memset(vs[:, :, :], 0.0))
            with Phase() as b2:
                xn = b2("b_xn", [P, CT, TOK])
                sq = b2("b_sq", [P, CT, TOK])
                rs = b2("b_rs", [P, TOK])
                for h in range(NH):
                    t = mm(banks[h][:, :], [(ones[:, :], XC[:, k, half(h)]) for k in range(CT)], *ready, *m.freed(f"bank{h}"))
                    t = A.do(lambda e: e.mul(rs[:, half(h)], banks[h][:, :], 1.0 / C), t)
                    m.release(f"bank{h}", t)
                rdy = [V.do(lambda e: e.tensor_tensor(xn[:, ct, :], XC[:, ct, :], rs[:, :], ALU.subtract), t) for ct in range(CT)]
                A.wait(rdy[-1])
                t = inverse_root(xn, rdy, sq, rs, 1e-5)
                rdy = scale_rows(xn, rs, "b_ln_scale", xn, t)
                rdy = [A.do(lambda e: e.activation(xn[:, ct, :], xn[:, ct, :], ACT.Identity, bias=vcol("b_ln_bias", ct)), rdy[ct])
                       for ct in range(CT)]
                t_sm = V.do(lambda e: e.tensor_copy(
                    small[:, :, :, 0:W], xn[:, :, :].rearrange("p c (b t) -> p c b t", b=NB)[:, :, :, P - W:P]), *rdy, t_w)
                n = 0
                jobs = [(q4, wq, xn, half(h), tile) for tile in range(4) for h in range(NH)]
                jobs += [(k4, wk, xn, half(h), tile) for tile in range(4) for h in range(NH)]
                smf = small[:, :, :, :].rearrange("p c b t -> p c (b t)")
                jobs += [(ks4, wk, smf, slice(0, NB * (W + NG)), tile) for tile in range(4)]
                for dst, w, src, cols, tile in jobs:
                    b = n % 4
                    n += 1
                    nn = cols.stop - cols.start
                    t = mm(banks[b][:, 0:nn], [(w[:, k, tile * P:(tile + 1) * P], src[:, k, cols]) for k in range(CT)],
                           *rdy, t_w, t_sm, *m.freed(f"bank{b}"))
                    o = dst[:, tile, cols]
                    t = A.do(lambda e: e.copy(o, banks[b][:, 0:nn]), t) if n % 2 else V.do(lambda e: e.tensor_copy(o, banks[b][:, 0:nn]), t)
                    m.release(f"bank{b}", t)
                for tt in range(TT):
                    b = 4 + tt % 4
                    t = mm(banks[b][:, 0:C], [(xn[:, k, tt * P:(tt + 1) * P], wv[:, k, :]) for k in range(CT)], *m.freed(f"bank{b}"))
                    t = V.do(lambda e: e.tensor_copy(heads(v[:, tt, :]), banks[b][:, 0:C].rearrange("p (h d) -> p h d", d=16)), t, t_v0)
                    m.release(f"bank{b}", t)
                for b_ in range(NB):
                    b = 4 + b_
                    t = mm(banks[b][0:W + NG, 0:C], [(small[:, k, b_, :], wv[:, k, :]) for k in range(CT)], *m.freed(f"bank{b}"))
                    t = V.do(lambda e: e.tensor_copy(heads(vs[:, b_, :]),
                                                     banks[b][0:W + NG, 0:C].rearrange("p (h d) -> p h d", d=16)), t, t_v0)
                    m.release(f"bank{b}", t)
            with Phase() as b2:
                NS = 5
                s_ = [b2(f"b_s{i}", [P, 2, KS]) for i in range(NS)]
                st = b2("b_st", [P, 3, 8])
                pt = [b2(f"b_pt{i}", [P, 4 * P]) for i in range(3)]
                o = b2("b_o", [P, 4, TOK])
                pairs = [(tt, tile, jj) for tt in range(TT) for tile in range(4) for jj in range(2)]

                def scores(n):
                    tt, tile, jj = pairs[n]
                    b, s, c = tt // 2, s_[n % NS], 2 * (n % 4)
                    for part in range(2):
                        for k in range(2):
                            j, bk = 32 * (2 * jj + k), 2 * (n % 2) + k
                            ql = q4[j:j + 16, tile, tt * P:(tt + 1) * P]
                            kk = k4[j:j + 16, tile, tt * P:(tt + 1) * P] if part == 0 else \
                                ks4[j:j + 16, tile, b * (W + NG):(b + 1) * (W + NG)]
                            cols = slice(P, KS) if part else slice(0, P)
                            t = PE.do(lambda e: e.matmul(banks[bk][:, cols], ql, kk, start=part == 0, stop=True,
                                                         skip_group_check=True), *m.freed(f"bank{bk}"))
                    for k in range(2):
                        bk = 2 * (n % 2) + k
                        tv = V.do(lambda e: e.tensor_tensor_reduce(s[:, k, :], banks[bk][:, 0:KS], msk[:, tt % 2, :], 1.0, -BIG,
                                                                   ALU.add, ALU.max, st[:, 0, c + k:c + k + 1]), t,
                                  *m.freed(f"s{n % NS}"))
                        m.release(f"bank{bk}", tv)
                    t = V.do(lambda e: e.tensor_scalar(st[:, 0, c:c + 2], st[:, 0, c:c + 2], -0.25, None, ALU.mult), tv)
                    for k in range(2):
                        ta = A.do(lambda e: e.activation(s[:, k, :], s[:, k, :], ACT.Exp, bias=st[:, 0, c + k:c + k + 1], scale=0.25,
                                                         accum_out=st[:, 1, c + k:c + k + 1]), t)
                    return ta

                def normalise(n, t):
                    s, c = s_[n % NS], 2 * (n % 4)
                    t = V.do(lambda e: e.reciprocal(st[:, 2, c:c + 2], st[:, 1, c:c + 2]), t)
                    return V.do(lambda e: e.tensor_tensor(s[:, :, :], s[:, :, :], st[:, 2, c:c + 2].unsqueeze(2).to_broadcast([P, 2, KS]),
                                                          ALU.mult), t)

                def turn(n, t):
                    bk, s, p_ = 4 + n % 2, s_[n % NS], pt[n % 3]
                    for k in range(2):
                        PE.quiet(lambda e: e.transpose(banks[bk][:, k * P:(k + 1) * P], s[:, k, 0:P], ident[:, :]), t,
                                 *m.freed(f"bank{bk}"))
                        tp = PE.do(lambda e: e.transpose(banks[bk][0:W + NG, (2 + k) * P:(3 + k) * P], s[:, k, P:KS], ident[:, :]))
                    m.release(f"s{n % NS}", tp)
                    A.do(lambda e: e.copy(p_[:, 0:2 * P], banks[bk][:, 0:2 * P]), tp, *m.freed(f"pt{n % 3}"))
                    t = A.do(lambda e: e.copy(p_[0:W + NG, 2 * P:4 * P], banks[bk][0:W + NG, 2 * P:4 * P]))
                    m.release(f"bank{bk}", t)
                    return t

                def mix(n, t):
                    tt, tile, jj = pairs[n]
                    bk, p_ = 6 + (n // 2) % 2, pt[n % 3]
                    for part in range(2):
                        for k in range(2):
                            j, h = 32 * (2 * jj + k), 4 * tile + 2 * jj + k
                            hs = slice(32 * h, 32 * h + 32)
                            lhs = vs[:, tt // 2, hs] if part else v[:, tt, hs]
                            rhs = p_[0:W + NG, (2 + k) * P:(3 + k) * P] if part else p_[:, k * P:(k + 1) * P]
                            tp = PE.do(lambda e: e.matmul(banks[bk][j:j + 32, 0:P], lhs, rhs, start=part == 0, stop=part == 1,
                                                          skip_group_check=True), t, *(m.freed(f"bank{bk}") if jj == 0 else ()))
                    m.release(f"pt{n % 3}", tp)
                    if jj:
                        t2 = V.do(lambda e: e.tensor_copy(o[:, tile, tt * P:(tt + 1) * P], banks[bk][:, 0:P]), tp)
                        m.release(f"bank{bk}", t2)
                    return tp

                exps, norms, turns, last = {}, {}, {}, len(pairs)
                for n in range(last + 4):
                    if 0 <= n - 2 < last:
                        norms[n - 2] = normalise(n - 2, exps[n - 2])
                    if 0 <= n - 3 < last:
                        turns[n - 3] = turn(n - 3, norms[n - 3])
                    if n < last:
                        exps[n] = scores(n)
                    if 0 <= n - 4 < last:
                        mix(n - 4, turns[n - 4])
                m.fence()
                project_residual(wo, 4, o, [], add=XC)

    def lora_ffn():
        E, F = 8, 896
        FT = F // P
        with Phase() as buf:
            wr = buf("r_wr", [P, CT, E])
            w1 = buf("r_w1", [P, CT, F])
            w3 = buf("r_w3", [P, CT, F])
            w2 = buf("r_w2", [P, FT, C])
            b1 = buf("r_b1", [P, CT, F])
            b3 = buf("r_b3", [P, CT, F])
            a2 = buf("r_a2", [P, FT, C])
            b2w = buf("r_b2", [P, CT, C])
            t_wr = load(ctr("rr"), wr[:, :, :], d["r_router"])
            ready = condition(3)
            rows = buf("r_rows", [18, TOK])
            a1 = buf("r_a1", [P, CT, C])
            a3 = buf("r_a3", [P, CT, C])
            sel = buf("r_sel", [18, 2, P])
            selx = buf("r_selx", [18, 2, CT, P])
            load(ctr("r2"), a1[:, :, :], d["r_a1"])
            load(ctr("r2"), a3[:, :, :], d["r_a3"])
            load(ctr("r2"), sel[:, :, :], d["r_sel"])
            load(ctr("r2"), selx[:, :, :, :], d["r_selx"])
            with Phase() as bb:
                revi = bb("r_revi", [P, TT, E])
                t_w2 = load(ctr("r2"), revi[:, :, :], d["revi8"])
                for dst, name in ((w1, "r_w1"), (w3, "r_w3"), (b1, "r_b1"), (b3, "r_b3"), (a2, "r_a2"), (b2w, "r_b2"), (w2, "r_w2")):
                    t_w = load(ctr("r"), dst[:, :, :], d[name])
                pr = bb("r_pr", [P, TT, E])
                hot = bb("r_hot", [P, TT, 18])
                tmp = bb("r_tmp", [P, 2, TT, 16])
                st = bb("r_st", [P, 4, TT])

                def bc(a, n=E):
                    return a.unsqueeze(2).to_broadcast([P, TT, n])
                t = token_logits(wr, E, ready + [t_wr])
                t = V.do(lambda e: e.tensor_copy(pr[:, :, :].rearrange("p t e -> p (t e)"), banks[0][:, 0:TT * E]), t)
                m.release("bank0", t)
                t = V.do(lambda e: e.tensor_reduce(st[:, 0, :], pr[:, :, :], AX, ALU.max), t)
                t = V.do(lambda e: e.tensor_tensor(pr[:, :, :], pr[:, :, :], bc(st[:, 0, :]), ALU.subtract), t)
                t = A.do(lambda e: e.activation(pr[:, :, :], pr[:, :, :], ACT.Exp), t)
                t = V.do(lambda e: e.tensor_reduce(st[:, 0, :], pr[:, :, :], AX, ALU.add), t)
                t = V.do(lambda e: e.reciprocal(st[:, 0, :], st[:, 0, :]), t)
                t = V.do(lambda e: e.tensor_tensor(pr[:, :, :], pr[:, :, :], bc(st[:, 0, :]), ALU.mult), t)
                V.wait(t_w2)
                t = pick_top(pr[:, :, :], None, hot[:, :, 0:8], revi[:, :, :], tmp, E, t)
                t = pick_top(pr[:, :, :], hot[:, :, 0:8], hot[:, :, 8:16], revi[:, :, :], tmp, E, t)
                for k in range(2):
                    t = V.do(lambda e: e.tensor_tensor(tmp[:, 1, :, 0:8], pr[:, :, :], hot[:, :, 8 * k:8 * k + 8], ALU.mult), t)
                    t = V.do(lambda e: e.tensor_reduce(st[:, k, :], tmp[:, 1, :, 0:8], AX, ALU.add), t)
                t = V.do(lambda e: e.tensor_tensor(st[:, 2, :], st[:, 0, :], st[:, 1, :], ALU.add), t)
                t = V.do(lambda e: e.reciprocal(st[:, 2, :], st[:, 2, :]), t)
                for k in range(2):
                    t = V.do(lambda e: e.tensor_tensor(hot[:, :, 16 + k], st[:, k, :], st[:, 2, :], ALU.mult), t)
                t_rows = rows_from_tokens(hot, 18, rows, t)
            maskx = buf("r_maskx", [P, 2, CT, HALF])
            rwb = buf("r_rwb", [P, 2, HALF])
            md = buf("r_md", [P, HALF])
            am = [[buf(f"r_am{k}{j}", [P, CT, HALF]) for j in range(2)] for k in range(2)]
            euk = buf("r_euk", [P, CT, TOK])

            def prepare(h):
                for k in range(2):
                    t2 = mm(banks[k][:, :], [(sel[:, k, :], rows[:, half(h)])], *m.freed(f"bank{k}"), *m.freed("pair0"))
                    t2 = A.do(lambda e: e.copy(rwb[:, k, :], banks[k][:, :]), t2, *m.freed("rwb"))
                    m.release(f"bank{k}", t2)
                for ct in range(CT):
                    for k in range(2):
                        t2 = mm(banks[2 + k][:, :], [(selx[:, k, ct, :], rows[:, half(h)])], *m.freed(f"bank{2 + k}"), *m.freed("pair1"))
                        t2 = A.do(lambda e: e.copy(maskx[:, k, ct, :], banks[2 + k][:, :]), t2, *m.freed("maskx"))
                        m.release(f"bank{2 + k}", t2)
                    td = V.do(lambda e: e.tensor_tensor(md[:, :], maskx[:, 1, ct, :], maskx[:, 0, ct, :], ALU.subtract), t2,
                              *m.freed("md"))
                    for j, w in enumerate((a1, a3)):
                        b = 4 + j
                        t3 = mm(banks[b][:, :], [(w[:, k2, ct * P:(ct + 1) * P], XC[:, k2, half(h)]) for k2 in range(CT)],
                                *m.freed(f"bank{b}"))
                        for k in range(2):
                            src = maskx[:, 0, ct, :] if k == 0 else md[:, :]
                            t3 = V.do(lambda e: e.tensor_tensor(am[k][j][:, ct, :], src, banks[b][:, :], ALU.mult), t3, td,
                                      *m.freed("am"))
                        m.release(f"bank{b}", t3)
                    m.release("md", t3)
                for b in range(2):
                    m.release(f"pair{b}", *m.freed(f"bank{2 * b}"), *m.freed(f"bank{2 * b + 1}"))
                PE.wait(t3)
                PE.wait(t_w)

            with Phase() as bb:
                ys = bb("r_ys", [P, FT, HALF])
                y = [[bb(f"r_y{k}{i}", [P, HALF]) for i in range(3)] for k in range(2)]
                sl = [bb(f"r_sl{i}", [P, HALF]) for i in range(2)]
                u2 = bb("r_u2", [P, CT, HALF])
                u3 = bb("r_u3", [P, HALF])
                wkv_start(4, euk)
                background = wkv_units([(4, u_, euk) for u_ in range(CT * NB)])
                for h in range(NH):
                    if h == 1:
                        wkv_start(5, euk)
                        background = wkv_units([(5, u_, euk) for u_ in range(CT * NB)])
                    prepare(h)

                    def up(ft, k):
                        pr_ = ft % 2
                        b = 2 * pr_
                        fs = slice(ft * P, (ft + 1) * P)
                        first = [(w1, b1), (w3, b3)]
                        for j, (w, lw) in enumerate(first):
                            pairs = [(lw[:, c, fs], am[k][j][:, c, :]) for c in range(CT)]
                            if k == 0:
                                pairs = [(w[:, c, fs], XC[:, c, half(h)]) for c in range(CT)] + pairs
                            t = mm(banks[b + j][:, :], pairs, *m.freed(f"pair{pr_}"), start=(k == 0))
                        s, yy = sl[k], y[k][ft % 3]
                        t1 = A.do(lambda e: e.activation(s[:, :], banks[b][:, :], ACT.Silu), t, *m.freed(f"sl{k}"))
                        t1 = V.do(lambda e: e.tensor_tensor(s[:, :], s[:, :], banks[b + 1][:, :], ALU.mult), t1)
                        m.release(f"pair{pr_}", t1)
                        t2 = V.do(lambda e: e.tensor_tensor(yy[:, :], s[:, :], rwb[:, k, :], ALU.mult), t1, *m.freed(f"y{k}{ft % 3}"))
                        m.release(f"sl{k}", t2)
                        return t2

                    def low(ft, k, t, t0):
                        pr_ = ft % 3
                        rel = ()
                        if k == 1:
                            rel = (G.do(lambda e: e.tensor_tensor(ys[:, ft, :], y[0][pr_][:, :], y[1][pr_][:, :], ALU.add), t, t0,
                                        *m.freed("ys")),)
                        for ct in range(CT):
                            f = lambda e: e.matmul(banks[4 + 2 * k + ct][:, :], a2[:, ft, ct * P:(ct + 1) * P], y[k][pr_][:, :],
                                                   start=(ft == 0), stop=(ft == FT - 1), skip_group_check=True)
                            tt_ = (PE.do if ct else PE.quiet)(f, t, *m.freed(f"bank{4 + 2 * k + ct}"))
                        if k == 1:
                            m.release(f"y1{pr_}", tt_, *rel)
                            m.release(f"y0{pr_}", tt_, *rel)
                        return rel[0] if rel else None

                    t0 = {}
                    tg = None
                    order = []
                    for ft in range(FT + 1):
                        if ft < FT:
                            order.append((ft, 0))
                        if ft > 0:
                            order.append((ft - 1, 1))
                    for ft, k in order:
                        t0[ft, k] = up(ft, k)
                        step(background, 8)
                        if (ft, k) == (0, 0):
                            continue
                        if k == 1:
                            low(ft, 0, t0[ft, 0], None)
                            if ft > 0:
                                tg = low(ft - 1, 1, t0[ft - 1, 1], t0[ft - 1, 0])
                    tg = low(FT - 1, 1, t0[FT - 1, 1], t0[FT - 1, 0])
                    t = PE.here()
                    for ct in range(CT):
                        ta = V.do(lambda e: e.tensor_tensor(u2[:, ct, :], maskx[:, 0, ct, :], banks[4 + ct][:, :], ALU.mult),
                                  t, *m.freed("u2"))
                        tb = V.do(lambda e: e.tensor_tensor(u3[:, :], maskx[:, 1, ct, :], banks[6 + ct][:, :], ALU.mult), ta)
                        ta = V.do(lambda e: e.tensor_tensor(u2[:, ct, :], u2[:, ct, :], u3[:, :], ALU.add), ta, tb)
                    for b in range(4, 8):
                        m.release(f"bank{b}", ta)
                    for ct in range(CT):
                        cs = slice(ct * P, (ct + 1) * P)
                        t = mm(banks[4 + ct][:, :], [(w2[:, ft, cs], ys[:, ft, :]) for ft in range(FT)] +
                               [(b2w[:, c, cs], u2[:, c, :]) for c in range(CT)], tg, ta)
                        o = XT[:, ct, half(h)]
                        t4 = V.do(lambda e: e.tensor_tensor(o, o, banks[4 + ct][:, :], ALU.add), t)
                        m.release(f"bank{4 + ct}", t4)
                    m.release("u2", t)
                    m.release("ys", t)
                    for name in ("maskx", "rwb", "am"):
                        m.release(name, V.here(), PE.here())
                    for _ in background:
                        pass

    def grouped_attention():
        D, KV, R = 128, 4, 4
        SC = float(D) ** -0.5
        with Phase() as buf:
            wqk = buf("g_wqk", [P, CT, (R + 1) * D])
            wgv = buf("g_wgv", [P, CT, (R + 1) * D])
            wo = buf("g_wo", [P, R, C])
            rc = buf("g_rc", [P, T])
            rsn = buf("g_rsn", [P, T])
            rot = buf("g_rot", [P, P])
            msk = buf("g_msk", [P, P + T])
            load(ctr("g"), rc[:, :], d["rope_cos"])
            load(ctr("g"), rsn[:, :], d["rope_sin"])
            load(ctr("g"), rot[:, :], d["rope_rot"])
            t_msk = load(ctr("g"), msk[:, :], d["causal"])
            ready = condition(4)
            q = buf("g_q", [P, R + 1, TOK])
            v = buf("g_v", [P, TT, D])
            th = buf("g_th", [P, R, TOK])
            rs = buf("g_rs", [P, R + 1, TOK])
            sq = [buf(f"g_sq{i}", [P, HALF]) for i in range(2)]
            mean = buf("g_mean", [P, CT * (R + 1)])
            euk2 = [buf(f"g_euk{i}", [P, CT, TOK]) for i in range(2)]
            wkv_start(6, euk2[0])
            wkv_start(7, euk2[1])
            NP = 5
            pp = [buf(f"g_p{i}", [P, 384]) for i in range(NP)]
            pt = [buf(f"g_pt{i}", [P, 384]) for i in range(2)]
            st = buf("g_st", [P, 3, 8])
            gate = buf("g_gate", [P, 2])
            m.fence(sp=False)
            for lane in (PE, V, G, A):
                lane.wait(t_msk)

            def body(g):
                t_qk = load(ctr("gqk"), wqk[:, :, :], lambda: d["g_qk"][g], *m.freed("wqk"))
                t_gv = load(ctr("ggv"), wgv[:, :, :], lambda: d["g_gv"][g], *m.freed("wgv"))
                t_wo = load(ctr("gwo"), wo[:, :, :], lambda: d["g_wo"][g], *m.freed("wo"))
                background = wkv_units([(6, i_, euk2[0]) for i_ in (g * 2, g * 2 + 1)] + [(7, i_, euk2[1]) for i_ in (g * 2, g * 2 + 1)])
                heads = wqk[:, :, :].rearrange("p c (h d) -> p (c h) d", d=D)
                t = V.do(lambda e: e.reduce_sum(mean[:, :], heads, AX), t_qk)
                t = V.do(lambda e: e.tensor_scalar(mean[:, :], mean[:, :], 1.0 / D, None, ALU.mult), t)
                t_c = V.do(lambda e: e.tensor_tensor(heads, heads, mean[:, :].unsqueeze(2).to_broadcast([P, CT * (R + 1), D]),
                                                     ALU.subtract), t)
                jobs = [(hd, h) for hd in [R] + list(range(R)) for h in range(NH)]
                t_ln = {}

                def squares(n, t):
                    (hd, h), b, s_ = jobs[n], n % 2, sq[n % 2]
                    t = mm(banks[2 + b][:, :], [(ones[:, :], s_[:, :])], t, *m.freed(f"set{2 + b}"))
                    m.release(f"sq{b}", t)
                    t_ln[hd, h] = A.do(lambda e: e.activation(rs[:, hd, half(h)], banks[2 + b][:, :], ACT.Ln, scale=1.0 / D,
                                                              bias=eps_col(1e-6)), t, *m.freed("rs"))
                    m.release(f"set{2 + b}", t_ln[hd, h])

                pend = None
                for n, (hd, h) in enumerate(jobs):
                    b = n % 2
                    o, s_ = q[:, hd, half(h)], sq[n % 2]
                    t = mm(banks[b][:, :], [(wqk[:, k, hd * D:(hd + 1) * D], XC[:, k, half(h)]) for k in range(CT)], t_c,
                           *m.freed(f"set{b}"))
                    t = V.do(lambda e: e.tensor_copy(o, banks[b][:, :]), t, *m.freed("q"))
                    m.release(f"set{b}", t)
                    t = A.do(lambda e: e.activation(s_[:, :], o, ACT.Square), t, *m.freed(f"sq{b}"))
                    if pend:
                        squares(*pend)
                    pend = (n, t)
                m.release("wqk", PE.here())
                squares(*pend)
                t_rs = {}
                for hd in [R] + list(range(R)):
                    t = A.do(lambda e: e.activation(rs[:, hd, :], rs[:, hd, :], ACT.Exp, scale=-0.5), t_ln[hd, 0], t_ln[hd, 1])
                    t_rs[hd, 0] = t_rs[hd, 1] = t
                q_ready = {}
                b2t = lambda a: a.rearrange("p (b t) -> p b t", b=2)
                table = lambda a: a[:, :].unsqueeze(1).to_broadcast([P, 2, T])

                def turned(n, t, tg):
                    (hd, h), b = jobs[n], 4 + n % 2
                    o, r_ = q[:, hd, half(h)], rs[:, hd, half(h)]
                    t = V.do(lambda e: e.tensor_tensor(b2t(r_), b2t(banks[b][:, :]), table(rsn), ALU.mult), t, tg)
                    m.release(f"set{b}", t)
                    q_ready[hd, h] = V.do(lambda e: e.tensor_tensor(o, o, r_, ALU.add), t)

                pend = None
                for n, (hd, h) in enumerate(jobs):
                    if n < R * NH:
                        hg, b = n // NH, n % 2
                        t = mm(banks[b][:, :], [(wgv[:, k, hg * D:(hg + 1) * D], XC[:, k, half(h)]) for k in range(CT)], t_gv,
                               *m.freed(f"set{b}"))
                        t_th = A.do(lambda e: e.activation(th[:, hg, half(h)], banks[b][:, :], ACT.Tanh, scale=0.5), t, *m.freed("th"))
                        m.release(f"set{b}", t_th)
                        tt, b = n, 6 + n % 2
                        t = mm(banks[b][:, 0:D], [(XC[:, k, tt * P:(tt + 1) * P], wgv[:, k, R * D:(R + 1) * D]) for k in range(CT)],
                               *m.freed(f"set{b}"))
                        t_v = A.do(lambda e: e.copy(v[:, tt, :], banks[b][:, 0:D]), t, *m.freed("v"))
                        m.release(f"set{b}", t_v)
                    b = 4 + n % 2
                    wn, bn = ("g_kn_w", "g_kn_b") if hd == R else ("g_qn_w", "g_qn_b")
                    o, r_ = q[:, hd, half(h)], rs[:, hd, half(h)]
                    t = V.do(lambda e: e.tensor_tensor(o, o, r_, ALU.mult), t_rs[hd, h])
                    t = V.do(lambda e: e.tensor_scalar(r_, o, vcol(wn), vcol(bn), ALU.mult, ALU.add), t)
                    tg = G.do(lambda e: e.tensor_tensor(b2t(o), b2t(r_), table(rc), ALU.mult), t)
                    t = mm(banks[b][:, :], [(rot[:, :], r_)], t, *m.freed(f"set{b}"))
                    if pend:
                        turned(*pend)
                    pend = (n, t, tg)
                    step(background, 1)
                turned(*pend)
                m.release("rs", q_ready[hd, h])
                m.release("wgv", PE.here())
                for b in range(8):
                    m.release(f"bank{b}", *m.freed(f"set{b}"))
                units = [(b, hd) for b in range(NB) for hd in range(R)]

                def scores(n):
                    b, hd = units[n]
                    t0 = b * T
                    bk, s, c = n % 3, pp[n % NP], 2 * (n % 4)
                    kk = q[:, R, t0:t0 + T]
                    rdy = (q_ready[hd, b // 2], q_ready[R, b // 2])
                    PE.quiet(lambda e: e.matmul(banks[bk][:, 0:P], q[:, hd, t0:t0 + P], kk[:, 0:P], start=True, stop=True,
                                                skip_group_check=True), *rdy, *m.freed(f"bank{bk}"))
                    t = PE.do(lambda e: e.matmul(banks[bk][:, P:P + T], q[:, hd, t0 + P:t0 + T], kk, start=False, stop=True,
                                                 skip_group_check=True))
                    V.do(lambda e: e.memset(gate[:, n % 2:n % 2 + 1], 0.0), t, *m.freed(f"p{n % NP}"))
                    for i, cols in enumerate((slice(0, P), slice(P, P + T))):
                        t = V.do(lambda e: e.tensor_tensor_reduce(s[:, cols], banks[bk][:, cols], msk[:, cols], 1.0, -BIG,
                                                                  ALU.add, ALU.max, st[:, 0, c + i:c + i + 1]))
                    m.release(f"bank{bk}", t)
                    t = V.do(lambda e: e.tensor_scalar(st[:, 0, c:c + 2], st[:, 0, c:c + 2], -SC, None, ALU.mult), t)
                    for i, cols in enumerate((slice(0, P), slice(P, P + T))):
                        ta = A.do(lambda e: e.activation(s[:, cols], s[:, cols], ACT.Exp, bias=st[:, 0, c + i:c + i + 1], scale=SC,
                                                         accum_out=st[:, 1, c + i:c + i + 1]), t)
                    return ta

                def normalise(n, ta):
                    c, s = 2 * (n % 4), pp[n % NP]
                    t = V.do(lambda e: e.reciprocal(st[:, 2, c:c + 2], st[:, 1, c:c + 2]), ta)
                    for i, cols in enumerate((slice(0, P), slice(P, P + T))):
                        t1 = V.do(lambda e: e.tensor_scalar(s[:, cols], s[:, cols], st[:, 2, c + i:c + i + 1], None, ALU.mult), t)
                    return t1

                def turn(n, t1):
                    s, p_, bk = pp[n % NP], pt[n % 2], 3 + n % 2
                    for i in range(3):
                        t = (PE.do if i == 2 else PE.quiet)(
                            lambda e: e.transpose(banks[bk][:, i * P:(i + 1) * P], s[:, i * P:(i + 1) * P], ident[:, :]), t1,
                            *m.freed(f"bank{bk}"))
                    m.release(f"p{n % NP}", t)
                    t = A.do(lambda e: e.copy(p_[:, :], banks[bk][:, 0:384]), t, *m.freed(f"pt{n % 2}"))
                    m.release(f"bank{bk}", t)
                    return t

                def mix(n, t):
                    b, hd = units[n]
                    p_, bk = pt[n % 2], 5 + n % 3
                    v0, v1 = v[:, 2 * b, :], v[:, 2 * b + 1, :]
                    PE.quiet(lambda e: e.matmul(banks[bk][:, 0:P], v0, p_[:, 0:P], start=True, stop=True, skip_group_check=True),
                             t, t_v, *m.freed(f"bank{bk}"))
                    PE.quiet(lambda e: e.matmul(banks[bk][:, P:T], v0, p_[:, P:2 * P], start=False, stop=False, skip_group_check=True))
                    t = PE.do(lambda e: e.matmul(banks[bk][:, P:T], v1, p_[:, 2 * P:3 * P], start=False, stop=True, skip_group_check=True))
                    m.release(f"pt{n % 2}", t)
                    return t

                def gated(n, t):
                    b, hd = units[n]
                    bk = 5 + n % 3
                    o = th[:, hd, b * T:(b + 1) * T]
                    t = V.do(lambda e: e.scalar_tensor_tensor(o, o, 1.0, banks[bk][:, 0:T], ALU.add, ALU.mult), t, t_th)
                    m.release(f"bank{bk}", t)
                    return t

                exps, norms, turns, mixes = {}, {}, {}, {}
                last = len(units)
                for n in range(last + 5):
                    if 0 <= n - 2 < last:
                        norms[n - 2] = normalise(n - 2, exps[n - 2])
                    if 0 <= n - 3 < last:
                        turns[n - 3] = turn(n - 3, norms[n - 3])
                    if 0 <= n - 5 < last:
                        t = gated(n - 5, mixes[n - 5])
                    if n < last:
                        exps[n] = scores(n)
                        step(background, 3)
                    if 0 <= n - 4 < last:
                        mixes[n - 4] = mix(n - 4, turns[n - 4])
                m.release("q", PE.here())
                m.release("v", PE.here())
                for _ in background:
                    pass
                for ct in range(CT):
                    for h in range(NH):
                        b = ct * NH + h
                        t2 = mm(banks[b][:, :], [(wo[:, hd, ct * P:(ct + 1) * P], th[:, hd, half(h)]) for hd in range(R)],
                                t, t_wo, *m.freed(f"bank{b}"))
                        o = XT[:, ct, half(h)]
                        t3 = V.do(lambda e: e.scalar_tensor_tensor(o, banks[b][:, :], 0.5, o, ALU.mult, ALU.add), t2)
                        m.release(f"bank{b}", t3)
                m.release("wo", t2)
                m.release("th", t2)
                for b in range(8):
                    m.release(f"set{b}", *m.freed(f"bank{b}"))

            m.run_loop(KV, body)

    def quantised_ffn():
        I = 704
        OT = 2 * I // P
        IT = 6
        CH = [(0, 512), (512, 192)]
        with Phase() as buf:
            w1t = buf("q_w1t", [P, CT, 2 * I], BF16)
            w2t = buf("q_w2t", [P, IT, C], BF16)
            s1b = buf("q_s1b", [P, 2 * I])
            s2b = buf("q_s2b", [P, C])
            st = buf("q_st", [P, 4, 16])

            def quantise(src, dst, tmp, c, t, *more):
                t = V.do(lambda e: e.tensor_reduce(st[:, 0, c:c + 1], src, AX, ALU.max, apply_absolute_value=True), t)
                t = V.do(lambda e: e.tensor_scalar(st[:, 0, c:c + 1], st[:, 0, c:c + 1], 1.0 / 127.0, 1e-8, ALU.mult, ALU.max), t)
                t = V.do(lambda e: e.reciprocal(st[:, 1, c:c + 1], st[:, 0, c:c + 1]), t)
                t = V.do(lambda e: e.tensor_scalar(tmp, src, st[:, 1, c:c + 1], ROUND, ALU.mult, ALU.add), t)
                t = V.do(lambda e: e.tensor_scalar(tmp, tmp, -ROUND, 127.0, ALU.add, ALU.min), t)
                return V.do(lambda e: e.tensor_scalar(dst, tmp, -127.0, None, ALU.max), t, *more)

            with Phase() as b2:
                w1 = b2("q_w1", [P, OT, C])
                w2 = b2("q_w2", [P, CT, I])
                wb = [b2(f"q_wb{i}", [P, I], BF16) for i in range(2)]
                tmp = b2("q_tmp", [P, I])
                diag = b2("q_diag", [P, P])
                pb = [banks[6][:, :].bitcast(BF16), banks[7][:, :].bitcast(BF16)]
                load(ctr("q"), w1[:, :, :], d["q_w1"])
                t_w = load(ctr("q"), w2[:, :, :], d["q_w2"])
                n = 0
                for o in range(OT + CT):
                    first = o < OT
                    src = w1[:, o, :] if first else w2[:, o - OT, :]
                    ncol = C if first else I
                    i = n % 2
                    t = quantise(src, wb[i][:, 0:ncol], tmp[:, 0:ncol], o, t_w, *m.freed(f"wb{i}"))
                    td = V.do(lambda e: e.tensor_scalar(diag[:, :], ident[:, :], st[:, 0, o:o + 1], None, ALU.mult), t, *m.freed("diag"))
                    t2 = mm(banks[0][:, 0:P], [(ones[:, :], diag[:, :])], td, *m.freed("bank0"))
                    m.release("diag", t2)
                    ds = s1b[:, o * P:(o + 1) * P] if first else s2b[:, (o - OT) * P:(o - OT + 1) * P]
                    t2 = A.do(lambda e: e.copy(ds, banks[0][:, 0:P]), t2)
                    m.release("bank0", t2)
                    blocks = [(c, min(P, ncol - c * P)) for c in range((ncol + P - 1) // P)]
                    for c, w_ in blocks:
                        t3 = PE.do(lambda e: e.transpose(pb[i][0:w_, c * P:(c + 1) * P], wb[i][:, c * P:c * P + w_], identb[:, :]),
                                   t, *m.freed(f"pb{i}"))
                    m.release(f"wb{i}", t3)
                    for c, w_ in blocks:
                        dt = w1t[:, c, o * P:(o + 1) * P] if first else w2t[0:w_, c, (o - OT) * P:(o - OT + 1) * P]
                        t4 = A.do(lambda e: e.copy(dt, pb[i][0:w_, c * P:(c + 1) * P]), t3)
                    m.release(f"pb{i}", t4)
                    n += 1
            ready = condition(5)
            with Phase() as b2:
                xt = [b2(f"q_x{i}", [P, C]) for i in range(2)]
                xb = [b2(f"q_xb{i}", [P, C], BF16) for i in range(2)]
                xqt = [b2(f"q_xqt{i}", [P, CT, P], BF16) for i in range(2)]
                tmp = [b2(f"q_t{i}", [P, I]) for i in range(2)]
                g = [b2(f"q_g{i}", [P, 2 * I]) for i in range(2)]
                hb = [b2(f"q_hb{i}", [P, I], BF16) for i in range(2)]
                hqt = [b2(f"q_hqt{i}", [P, IT, P], BF16) for i in range(2)]
                ob = [b2(f"q_ob{i}", [P, C]) for i in range(2)]
                pb = [banks[5][:, :].bitcast(BF16), banks[6][:, :].bitcast(BF16)]

                def stage1(tt):
                    i = tt % 2
                    for ct in range(CT):
                        t = PE.do(lambda e: e.transpose(banks[4][:, ct * P:(ct + 1) * P], XC[:, ct, tt * P:(tt + 1) * P], ident[:, :]),
                                  *ready, *m.freed("bank4"))
                    t = A.do(lambda e: e.copy(xt[i][:, :], banks[4][:, 0:C]), t, *m.freed(f"xt{i}"))
                    m.release("bank4", t)
                    t = quantise(xt[i][:, :], xb[i][:, :], xt[i][:, :], i, t, *m.freed(f"xb{i}"))
                    m.release(f"xt{i}", t)
                    for ct in range(CT):
                        t = PE.do(lambda e: e.transpose(pb[0][:, ct * P:(ct + 1) * P], xb[i][:, ct * P:(ct + 1) * P], identb[:, :]),
                                  t, *m.freed("pb0"))
                    m.release(f"xb{i}", t)
                    t = A.do(lambda e: e.copy(xqt[i][:, :, :].rearrange("p c t -> p (c t)"), pb[0][:, 0:C]), t, *m.freed(f"xqt{i}"))
                    m.release("pb0", t)
                    for j in range(2):
                        for n, (c0_, w_) in enumerate(CH):
                            b = 2 * j + n
                            t2 = mm(banks[b][:, 0:w_], [(xqt[i][:, k, :], w1t[:, k, j * I + c0_:j * I + c0_ + w_]) for k in range(CT)],
                                    t, *m.freed(f"bank{b}"))
                            gs = g[i][:, j * I + c0_:j * I + c0_ + w_]
                            t3 = V.do(lambda e: e.scalar_tensor_tensor(gs, banks[b][:, 0:w_], st[:, 0, i:i + 1],
                                                                       s1b[:, j * I + c0_:j * I + c0_ + w_], ALU.mult, ALU.mult),
                                      t2, *m.freed(f"g{i}"))
                            m.release(f"bank{b}", t3)
                            if j == 0 and n == 1:
                                m.release(f"xqt{i}", t2)
                                ta = A.do(lambda e: e.activation(tmp[i][:, :], g[i][:, 0:I], ACT.Silu), t3, *m.freed(f"tmp{i}"))
                    m.release(f"xqt{i}", t2)
                    t = V.do(lambda e: e.tensor_tensor(tmp[i][:, :], tmp[i][:, :], g[i][:, I:2 * I], ALU.mult), ta, t3)
                    m.release(f"g{i}", t)
                    return t

                def stage2(tt, t):
                    i = tt % 2
                    t = quantise(tmp[i][:, :], hb[i][:, :], tmp[i][:, :], 2 + i, t, *m.freed(f"hb{i}"))
                    m.release(f"tmp{i}", t)
                    for c in range(IT):
                        w_ = min(P, I - c * P)
                        t2 = PE.do(lambda e: e.transpose(pb[1][0:w_, c * P:(c + 1) * P], hb[i][:, c * P:c * P + w_], identb[:, :]),
                                   t, *m.freed("pb1"))
                    m.release(f"hb{i}", t2)
                    t3 = A.do(lambda e: e.copy(hqt[i][:, 0:IT - 1, :].rearrange("p c t -> p (c t)"), pb[1][:, 0:(IT - 1) * P]), t2,
                              *m.freed(f"hqt{i}"))
                    t3 = A.do(lambda e: e.copy(hqt[i][0:64, IT - 1, :], pb[1][0:64, (IT - 1) * P:IT * P]), t2)
                    m.release("pb1", t3)
                    pairs = [(hqt[i][0:min(P, I - c * P), c, :], w2t[0:min(P, I - c * P), c, :]) for c in range(IT)]
                    t3 = mm(banks[7][:, 0:C], pairs, t3, *m.freed("bank7"))
                    m.release(f"hqt{i}", t3)
                    t3 = V.do(lambda e: e.scalar_tensor_tensor(ob[i][:, :], banks[7][:, 0:C], st[:, 0, 2 + i:3 + i], s2b[:, :],
                                                               ALU.mult, ALU.mult), t3, *m.freed(f"ob{i}"))
                    for ct in range(CT):
                        t4 = PE.do(lambda e: e.transpose(banks[7][:, C + ct * P:C + (ct + 1) * P], ob[i][:, ct * P:(ct + 1) * P],
                                                         ident[:, :]), t3)
                    m.release(f"ob{i}", t4)
                    o = XT[:, :, tt * P:(tt + 1) * P]
                    t4 = V.do(lambda e: e.tensor_tensor(o, o, banks[7][:, C:2 * C].rearrange("p (c t) -> p c t", c=CT), ALU.add), t4)
                    m.release("bank7", t4)

                pend = None
                for tt in range(TT):
                    t = stage1(tt)
                    if pend:
                        stage2(*pend)
                    pend = (tt, t)
                stage2(*pend)

    def selective_scan():
        EI, N, ET = 512, 16, 4
        GN = 4
        HB = NB // 2
        NG = N // GN
        ready = condition(6)
        side.__exit__()
        with Phase() as buf:
            u = buf("s_u", [P, ET, TOK])
            dl = buf("s_dl", [P, ET, TOK])
            y = buf("s_y", [P, ET, TOK])
            wsk = buf("s_wsk", [P, CT, EI])
            wout = buf("s_wout", [P, ET, C])
            an = buf("s_an", [P, ET, N])
            bc3 = buf("s_bc3", [6 * N, TOK], BF16)
            pick3 = buf("s_pick3", [6 * N, 2 * N], BF16)
            xn = XC
            with Phase() as b2:
                sq = b2("s_sq", [P, CT, TOK])
                rs = b2("s_rs", [P, TOK])
                win = b2("s_win", [P, CT, EI])
                wd1 = b2("s_wd1", [P, ET, P])
                wd2 = b2("s_wd2", [P, 1, EI])
                wbc = b2("s_wbc", [P, ET, 2 * N])
                up = [b2(f"s_up{i}", [P, NB, T + 3]) for i in range(2)]
                r1 = b2("s_r1", [P, TOK])
                rest = [b2(f"s_rest{i}", [2 * N, HALF]) for i in range(2)]
                middle = [b2(f"s_middle{i}", [2 * N, HALF], BF16) for i in range(2)]
                t_in = load(ctr("s"), win[:, :, :], d["s_win"])
                load(ctr("s4"), wd1[:, :, :], d["s_wd1"])
                load(ctr("s4"), wd2[:, :, :], d["s_wd2"])
                load(ctr("s4"), an[:, :, :], d["s_alog"])
                t_w = load(ctr("s4"), wbc[:, :, :], d["s_wbc"])
                load(ctr("s3"), wsk[:, :, :], d["s_wskip"])
                t_wo = load(ctr("s3"), wout[:, :, :], d["s_wout"])
                t = inverse_root(XC, ready, sq, rs, 1e-5)
                rdy = scale_rows(XC, rs, "s_norm", xn, t)
                for i in range(2):
                    t_z = V.do(lambda e: e.memset(up[i][:, :, 0:3], 0.0))
                for k in range(3):
                    V.do(lambda e: e.tensor_copy(pick3[2 * N * k:2 * N * (k + 1), :], ident[0:2 * N, 0:2 * N]))
                convs = []
                for et in range(ET):
                    i = et % 2
                    for h in range(NH):
                        b = (2 * et + h) % 4
                        t = mm(banks[b][:, :], [(win[:, k, et * P:(et + 1) * P], xn[:, k, half(h)]) for k in range(CT)],
                               *rdy, t_in, *m.freed(f"bank{b}"))
                        t = A.do(lambda e: e.copy(up[i][:, 2 * h:2 * h + 2, 3:T + 3],
                                                  banks[b][:, :].rearrange("p (b t) -> p b t", b=2)), t, t_z, *m.freed(f"up{i}"))
                        m.release(f"bank{b}", t)
                    uo = u[:, et, :].rearrange("p (b t) -> p b t", b=NB)
                    t = V.do(lambda e: e.tensor_scalar(uo, up[i][:, :, 0:T], vcol("s_conv", et * 4), vcol("s_conv_b", et),
                                                       ALU.mult, ALU.add), t)
                    for j in range(1, 4):
                        t = V.do(lambda e: e.scalar_tensor_tensor(uo, up[i][:, :, j:j + T], vcol("s_conv", et * 4 + j), uo,
                                                                  ALU.mult, ALU.add), t)
                    m.release(f"up{i}", t)
                    convs.append(t)
                    if et:
                        t_u = A.do(lambda e: e.activation(u[:, et - 1, :], u[:, et - 1, :], ACT.Silu), convs[et - 1])
                t_u = A.do(lambda e: e.activation(u[:, ET - 1, :], u[:, ET - 1, :], ACT.Silu), convs[ET - 1])
                for h in range(NH):
                    b = 4 + h
                    t = mm(banks[b][:, :], [(wd1[:, k, :], u[:, k, half(h)]) for k in range(ET)], t_u, t_w)
                    t_r = A.do(lambda e: e.copy(r1[:, half(h)], banks[b][:, :]), t)
                    t = mm(banks[b + 2][0:2 * N, :], [(wbc[:, k, :], u[:, k, half(h)]) for k in range(ET)])
                    part = lambda k: bc3[2 * N * k:2 * N * (k + 1), half(h)]
                    r_, m_ = rest[h][:, :], middle[h][:, :]
                    t0 = V.do(lambda e: e.tensor_copy(part(0), banks[b + 2][0:2 * N, :]), t)
                    t0 = V.do(lambda e: e.tensor_tensor(r_, banks[b + 2][0:2 * N, :], part(0), ALU.subtract), t0)
                    t0 = V.do(lambda e: e.tensor_copy(m_, r_), t0)
                    t1 = V.do(lambda e: e.tensor_tensor(r_, r_, m_, ALU.subtract), t0)
                    V.do(lambda e: e.tensor_copy(part(1), m_), t0)
                    V.do(lambda e: e.tensor_copy(part(2), r_), t1)
                for et in range(ET):
                    for h in range(NH):
                        b = (2 * et + h) % 4
                        t = mm(banks[b][:, :], [(wd2[:, 0, et * P:(et + 1) * P], r1[:, half(h)])], t_r, *m.freed(f"bank{b}"))
                        t_y = A.do(lambda e: e.activation(y[:, et, half(h)], banks[b][:, :], ACT.Abs, bias=vcol("s_bd2", et)), t)
                        t_dl = V.do(lambda e: e.tensor_scalar(dl[:, et, half(h)], banks[b][:, :], vcol("s_bd2", et), 0.0,
                                                              ALU.add, ALU.max), t_y)
                        m.release(f"bank{b}", t_dl)
                t = A.do(lambda e: e.activation(y[:, :, :], y[:, :, :], ACT.Exp, scale=-1.0), t_y)
                t_an = A.do(lambda e: e.activation(an[:, :, :], an[:, :, :], ACT.Exp))
                V.do(lambda e: e.tensor_scalar(an[:, :, :], an[:, :, :], -1.0, None, ALU.mult), t_an)
                for h in range(NH):
                    t2 = A.do(lambda e: e.activation(y[:, :, half(h)], y[:, :, half(h)], ACT.Ln, bias=eps_col(1.0)), t)
                    V.do(lambda e: e.tensor_tensor(dl[:, :, half(h)], dl[:, :, half(h)], y[:, :, half(h)], ALU.add), t2, t_dl)
            with Phase() as b2:
                NBU, NDA = 4, 3
                rep = [[b2(f"s_rep{kind}{i}", [P, GN, HALF]) for i in range(2)] for kind in range(2)]
                du = b2("s_du", [P, ET, HALF])
                da = [b2(f"s_da{i}", [P, GN, HALF]) for i in range(NDA)]
                bu = [b2(f"s_bu{i}", [P, GN, HALF]) for i in range(NBU)]
                groups = [(h, gn) for h in range(NH) for gn in range(NG)]

                def replicate(kind, j, n):
                    if j >= len(groups):
                        return
                    h, gn = groups[j]
                    row, b = kind * N + gn * GN + n, 2 * kind + n % 2
                    t = mm(banks[b][:, :], [(pick3[:, row:row + 1].to_broadcast([6 * N, P]), bc3[:, half(h)])],
                           *m.freed(f"bank{b}"))
                    t = A.do(lambda e: e.copy(rep[kind][j % 2][:, n, :], banks[b][:, :]), t, *m.freed(f"rep{kind}{j % 2}"))
                    m.release(f"bank{b}", t)
                    t_rep[kind, j] = t

                fl = lambda a: a[:, :, :].rearrange("p n t -> p (n t)")
                jobs = [(j, et) for j in range(len(groups)) for et in range(ET)]
                t_rep, t_da, t_bu, t_sum, t_du = {}, {}, {}, {}, None
                for kind in range(2):
                    for n in range(GN):
                        replicate(kind, 0, n)

                def inputs(k):
                    nonlocal t_du
                    j, et = jobs[k]
                    h, gn = groups[j]
                    a_, b_ = da[k % NDA], bu[k % NBU]
                    if et == 0 and gn == 0:
                        t_du = V.do(lambda e: e.tensor_tensor(du[:, :, :], dl[:, :, half(h)], u[:, :, half(h)], ALU.mult),
                                    *m.freed("du"))
                    for n in range(GN):
                        t_da[k] = A.do(lambda e: e.activation(a_[:, n, :], dl[:, et, half(h)], ACT.Exp,
                                                              scale=an[:, et, gn * GN + n:gn * GN + n + 1]), *m.freed(f"da{k % NDA}"))
                    t_bu[k] = G.do(lambda e: e.tensor_tensor(b_[:, :, :], rep[0][j % 2][:, :, :],
                                                             du[:, et, :].unsqueeze(1).to_broadcast([P, GN, HALF]), ALU.mult),
                                   t_du, t_rep[0, j], *m.freed(f"bu{k % NBU}"))
                    m.release("du", t_bu[k])
                    m.release(f"rep0{j % 2}", t_bu[k])
                    replicate(0, j + 1, et)

                def states(k):
                    j, et = jobs[k]
                    h, gn = groups[j]
                    a_, b_, bk = da[k % NDA], bu[k % NBU], 4 + et
                    dz = a_[:, :, :].rearrange("p n (b t) -> p (n b) t", b=HB)[:, :, 0:1]
                    t = V.do(lambda e: e.memset(dz, 0.0), t_da[k])
                    t = V.do(lambda e: e.tensor_tensor_scan(fl(b_), fl(a_), fl(b_), 0.0, ALU.mult, ALU.add), t, t_bu[k])
                    m.release(f"da{k % NDA}", t)
                    t = V.do(lambda e: e.tensor_tensor(b_[:, :, :], b_[:, :, :], rep[1][j % 2][:, :, :], ALU.mult), t, t_rep[1, j])
                    m.release(f"rep1{j % 2}", t)
                    replicate(1, j + 1, et)
                    for n in range(GN):
                        f = lambda e: e.matmul(banks[bk][:, :], ident[:, :], b_[:, n, :], start=(gn == 0 and n == 0),
                                               stop=(gn == NG - 1 and n == GN - 1), skip_group_check=True)
                        tp = (PE.do if n == GN - 1 else PE.quiet)(f, t, *m.freed(f"bank{bk}"))
                    m.release(f"bu{k % NBU}", tp)
                    t_sum[h, et] = tp
                    if gn == NG - 1 and et == ET - 1:
                        for et in range(ET):
                            t = V.do(lambda e: e.scalar_tensor_tensor(y[:, et, half(h)], u[:, et, half(h)], vcol("s_wd", et),
                                                                      banks[4 + et][:, :], ALU.mult, ALU.add), t_sum[h, et])
                            m.release(f"bank{4 + et}", t)

                for k in range(len(jobs) + 2):
                    if k < len(jobs):
                        inputs(k)
                    if k >= 2:
                        states(k - 2)
            with Phase() as b2:
                sk = [b2(f"s_sk{i}", [P, HALF]) for i in range(2)]
                n = 0
                for et in range(ET):
                    for h in range(NH):
                        i, b = n % 2, n % 4
                        n += 1
                        t = mm(banks[b][:, :], [(wsk[:, k, et * P:(et + 1) * P], xn[:, k, half(h)]) for k in range(CT)],
                               t_wo, *m.freed(f"bank{b}"))
                        t = A.do(lambda e: e.activation(sk[i][:, :], banks[b][:, :], ACT.Silu), t, *m.freed(f"sk{i}"))
                        m.release(f"bank{b}", t)
                        o = y[:, et, half(h)]
                        t = V.do(lambda e: e.tensor_tensor(o, o, sk[i][:, :], ALU.mult), t)
                        m.release(f"sk{i}", t)
                project_residual(wout, ET, y, [t], bank0=4)

    def moe_top4():
        E, I, K = 16, 176, 4
        UT = E * I // P
        PER = 2
        SI = 2 * I
        with Phase() as buf:
            wr = buf("e_wr", [P, CT, 2 * E])
            srow = buf("e_row", [P, 2, E])
            revi = buf("e_revi", [P, TT, E])
            sg = buf("e_sg", [P, CT, 2 * SI])
            sd = buf("e_sd", [P, 3, C])
            load(ctr("e"), wr[:, :, :], d["e_router"])
            load(ctr("e"), srow[:, :, :], d["e_extra"].partition_broadcast(P))
            load(ctr("e"), sg[:, :, :], d["e_shared_gu"])
            load(ctr("e"), sd[:, :, :], d["e_shared_down"])
            t_w = load(ctr("e"), revi[:, :, :], d["revi16"])
            ready = condition(7)
            rows = buf("e_rows", [E, TOK])
            with Phase() as b2:
                lg = b2("e_lg", [P, TT, 2 * E])
                pr = b2("e_pr", [P, TT, E])
                bi = b2("e_bi", [P, TT, E])
                hot = b2("e_hot", [P, TT, E])
                tk = b2("e_tk", [P, TT, E])
                tmp = b2("e_tmp", [P, 2, TT, 16])
                st = b2("e_st", [P, TT])

                def bc(a):
                    return a.unsqueeze(2).to_broadcast([P, TT, E])

                def rowb(n):
                    return srow[:, n, :].unsqueeze(1).to_broadcast([P, TT, E])
                t = token_logits(wr, 2 * E, ready + [t_w])
                t = V.do(lambda e: e.tensor_copy(lg[:, :, :].rearrange("p t e -> p (t e)"), banks[0][:, 0:TT * 2 * E]), t)
                m.release("bank0", t)
                t = A.do(lambda e: e.activation(pr[:, :, :], lg[:, :, 0:E], ACT.Silu), t)
                t = V.do(lambda e: e.tensor_tensor(pr[:, :, :], pr[:, :, :], lg[:, :, E:2 * E], ALU.mult), t)
                t = A.do(lambda e: e.activation(pr[:, :, :], pr[:, :, :], ACT.Abs), t)
                t = V.do(lambda e: e.tensor_reduce(st[:, :], pr[:, :, :], AX, ALU.max), t)
                t = V.do(lambda e: e.tensor_tensor(pr[:, :, :], pr[:, :, :], bc(st[:, :]), ALU.subtract), t)
                t = A.do(lambda e: e.activation(pr[:, :, :], pr[:, :, :], ACT.Exp), t)
                t = V.do(lambda e: e.tensor_reduce(st[:, :], pr[:, :, :], AX, ALU.add), t)
                t = V.do(lambda e: e.reciprocal(st[:, :], st[:, :]), t)
                t = V.do(lambda e: e.tensor_tensor(pr[:, :, :], pr[:, :, :], bc(st[:, :]), ALU.mult), t)
                t = V.do(lambda e: e.tensor_tensor(bi[:, :, :], pr[:, :, :], rowb(1), ALU.add), t)
                t = pick_top(bi[:, :, :], None, tk[:, :, :], revi[:, :, :], tmp, E, t)
                for k in range(1, K):
                    t = pick_top(bi[:, :, :], tk[:, :, :], hot[:, :, :], revi[:, :, :], tmp, E, t)
                    t = V.do(lambda e: e.tensor_tensor(tk[:, :, :], tk[:, :, :], hot[:, :, :], ALU.add), t)
                t = V.do(lambda e: e.tensor_tensor(pr[:, :, :], pr[:, :, :], rowb(0), ALU.mult), t)
                t = V.do(lambda e: e.scalar_tensor_tensor(pr[:, :, :], pr[:, :, :], 1.0, tk[:, :, :], ALU.add, ALU.mult), t)
                t = rows_from_tokens(pr, E, rows, t)
            wgu = [buf(f"e_wgu{j}", [P, CT, 2, P]) for j in range(PER)]
            wd = [buf(f"e_wd{j}", [P, C]) for j in range(PER)]
            sel = [buf(f"e_sel{j}", [E, P]) for j in range(PER)]
            cf = [[buf(f"e_cf{j}{h}", [P, HALF]) for h in range(NH)] for j in range(PER)]
            hbuf = [buf(f"e_h{i}", [P, HALF]) for i in range(3)]
            sbuf = [buf(f"e_s{i}", [P, HALF]) for i in range(2)]
            units = []
            for ft in range(3):
                rws = min(P, SI - ft * P)
                for h in range(NH):
                    units.append(dict(src=XC, wg=[sg[:, k, ft * P:ft * P + rws] for k in range(CT)],
                                      wu=[sg[:, k, SI + ft * P:SI + ft * P + rws] for k in range(CT)],
                                      wd=sd[:, ft, :], rows=rws, h=h, coef=None, first=ft == 0, last=False, waits=[t_w]))
            run_units(units, hbuf, sbuf)

            def body(i):
                toks = []
                for j in range(PER):
                    load(ctr(f"e{j}"), wgu[j][:, :, :, :], lambda: d["e_gu"][i, j], *m.freed(f"w{j}"))
                    load(ctr(f"e{j}"), sel[j][:, :], lambda: d["e_sel"][i, j], *m.freed(f"w{j}"))
                    toks.append(load(ctr(f"e{j}"), wd[j][:, :], lambda: d["e_down"][i, j], *m.freed(f"w{j}")))
                units = []
                for ft in range(PER):
                    for h in range(NH):
                        u = dict(src=XC, wg=[wgu[ft][:, k, 0, :] for k in range(CT)],
                                 wu=[wgu[ft][:, k, 1, :] for k in range(CT)], wd=wd[ft], rows=P, h=h,
                                 first=False, last=True, waits=[toks[ft]])

                        def before(ft=ft, h=h, u=u):
                            nn = ft * NH + h
                            b = 4 + 2 * (nn % 2)
                            t = mm(banks[b][:, :], [(sel[ft][:, :], rows[:, half(h)])], toks[ft], *m.freed(f"pair{nn % 2}"))
                            t = A.do(lambda e: e.copy(cf[ft][h][:, :], banks[b][:, :]), t, *m.freed(f"cf{ft}{h}"))
                            u["coef"] = ((lambda: cf[ft][h][:, :]), t)
                            m.release(f"pair{nn % 2}", t)
                        u["before"] = before
                        u["after"] = (lambda ft=ft, h=h: (m.release(f"w{ft}", PE.here()) if h == 1 else None,
                                                          m.release(f"cf{ft}{h}", V.here())))
                        units.append(u)
                run_units(units, hbuf, sbuf)

            m.run_loop(UT // PER, body)
            add_out_banks()

    stages = [linear_attention, moe_top1, banded_attention, lora_ffn, grouped_attention, quantised_ffn,
              selective_scan, moe_top4]
    for n, stage in enumerate(stages):
        if n >= STOP:
            break
        stage()
    m.fence()
    t = SP.issue(lambda e: e.dma_start(out, XT[:, :, :]), count=16, counter=ctr("out"))
    SP.wait(t)


def _constants(np):
    c = {}
    c["ident"] = np.eye(128, dtype=np.float32)
    dist = (np.arange(256)[None, :] - np.arange(128)[:, None]).astype(np.float32)
    c["dist"] = np.concatenate([dist, dist[:, 0:128]], 1)
    for n in (8, 16):
        c[f"revi{n}"] = np.broadcast_to((n - np.arange(n)).astype(np.float32), (128, 8, n)).copy()
    c["sel16"] = np.broadcast_to(np.eye(16, dtype=np.float32)[:, :, None], (16, 16, 128)).copy()
    i, j = np.arange(128)[:, None], np.arange(128)[None, :]
    own = (j <= i) & (j >= i - 31)
    prev = (np.arange(32)[None, :] - 32) >= i - 31
    mask = np.full((128, 2, 176), -1e30, np.float32)
    for t in range(2):
        mask[:, t, 0:128][own] = 0.0
        if t:
            mask[:, t, 128:160][prev] = 0.0
        mask[:, t, 160:176] = 0.0
    c["b_mask"] = mask
    diag = np.where(j <= i, 0.0, -1e30).astype(np.float32)
    c["causal"] = np.concatenate([diag, np.zeros((128, 128), np.float32), diag], 1)
    sel = np.zeros((18, 2, 128), np.float32)
    sel[16, 0], sel[17, 1] = 1.0, 1.0
    c["r_sel"] = sel
    selx = np.zeros((18, 2, 2, 128), np.float32)
    for k in range(2):
        for ct in range(2):
            for p in range(128):
                selx[8 * k + ct * 4 + p // 32, k, ct, p] = 1.0
    c["r_selx"] = selx
    inv = 1.0 / 1000000.0 ** (np.arange(0, 128, 2, dtype=np.float32) / 128)
    fr = np.outer(inv, np.arange(256, dtype=np.float32)).astype(np.float32)
    c["rope_cos"] = np.concatenate([np.cos(fr), np.cos(fr)], 0).astype(np.float32)
    c["rope_sin"] = np.concatenate([np.sin(fr), np.sin(fr)], 0).astype(np.float32)
    rot = np.zeros((128, 128), np.float32)
    for p in range(64):
        rot[p + 64, p], rot[p, p + 64] = -1.0, 1.0
    c["rope_rot"] = rot
    es = np.zeros((11, 2, 16, 128), np.float32)
    for f in range(16 * 176):
        es[f // 256, (f // 128) % 2, f // 176, f % 128] = 1.0
    c["e_sel"] = es
    return c


def _layout(inputs, np):
    a = {k: np.asarray(v) for k, v in inputs.items()}

    def km(wt):
        k, o = wt.shape
        return np.ascontiguousarray(wt.reshape(k // 128, 128, o).transpose(1, 0, 2))

    def cols(v, n):
        return v.reshape(n, 128).T

    def acts(x):
        return km(x.transpose(2, 0, 1).reshape(256, 1024))
    r = dict(_constants(np))
    r["x"] = acts(a["x"])
    r["side"] = acts(a["fside_BxSxS_0"])
    r["cond"] = a["cond_512"]
    blocks = [f"L{l}_{c}" for l in range(4) for c in ("cond", "cond2")]

    def pad32(v):
        w = v.reshape(16, 16, *v.shape[1:])
        return np.concatenate([w, np.zeros_like(w)], 1).reshape(512, *v.shape[1:])
    vec = {"cond_w": np.concatenate([cols(a[f"{b}_w"], 2) for b in blocks], 1),
           "cond_u": np.concatenate([cols(a[f"{b}_u"], 2) for b in blocks], 1),
           "l0_qkv_norm": cols(a["L0_attn_qkv_norm_w"], 2), "l0_norm": cols(pad32(a["L0_attn_norm_w"]), 4),
           "l0_proj_norm": cols(pad32(a["L0_attn_proj_norm_w"]), 4),
           "b_ln_scale": cols(a["L1_attn_ln_scale"], 2), "b_ln_bias": cols(a["L1_attn_ln_bias"], 2),
           "s_norm": cols(a["L3_attn_norm_w"], 2), "s_bd2": cols(a["L3_attn_bd2"], 4), "s_wd": cols(a["L3_attn_W_D"], 4),
           "s_conv_b": cols(a["L3_attn_conv_b"], 4),
           "s_conv": a["L3_attn_conv_w"].reshape(4, 128, 4).transpose(1, 0, 2).reshape(128, 16)}
    order = np.concatenate([np.arange(0, 128, 2), np.arange(1, 128, 2)])
    for n, s in (("g_qn_w", "q_norm_w"), ("g_qn_b", "q_norm_b"), ("g_kn_w", "k_norm_w"), ("g_kn_b", "k_norm_b")):
        vec[n] = a["L2_attn_" + s][order][:, None]
    ofs, at = {}, 0
    for n, v in vec.items():
        ofs[n] = at
        at += v.shape[1]
    r["vecs"] = np.ascontiguousarray(np.concatenate(list(vec.values()), 1))

    def heads32(wt):
        return pad32(wt.T).T
    w = a["L0_attn_qkv_w"].T
    r["l0_qkv"] = km(np.concatenate([heads32(w[:, 0:256]), heads32(w[:, 256:512]), w[:, 512:768]], 1))
    r["l0_proj"] = km(pad32(a["L0_attn_proj_w"].T))
    r["l0_s"] = a["L0_attn_s"]
    r["m0_router"] = km(a["L0_ffn_router_w"].T)
    gu = a["L0_ffn_w_gate_up"].reshape(8, 2, 128, 2, 4, 128)
    r["m0_gu"] = np.ascontiguousarray(gu.transpose(0, 4, 2, 1, 3, 5))
    r["m0_down"] = np.ascontiguousarray(a["L0_ffn_w_down"].reshape(8, 4, 128, 256))
    r["m0_shared_gu"] = km(a["L0_ffn_shared_gate_up"])
    r["m0_shared_down"] = km(a["L0_ffn_shared_down"])
    for n, s in (("b_wq", "Wq"), ("b_wk", "Wk"), ("b_wv", "Wv"), ("b_wo", "Wo")):
        w = a["L1_attn_" + s].T
        r[n] = km(heads32(w) if s in ("Wq", "Wk") else pad32(w) if s == "Wo" else w)
    r["b_global"] = km(a["L1_attn_global_tokens"][0].T)
    r["r_router"] = km(a["L1_ffn_Wg"].T)
    r["r_w1"], r["r_w3"], r["r_w2"] = km(a["L1_ffn_W1"].T), km(a["L1_ffn_W3"].T), km(a["L1_ffn_W2"].T)
    r["r_a1"], r["r_a3"] = km(a["L1_ffn_A1"].reshape(256, 256).T), km(a["L1_ffn_A3"].reshape(256, 256).T)
    r["r_a2"] = km(a["L1_ffn_A2"].reshape(256, 896).T)
    for n, s in (("r_b1", "B1"), ("r_b3", "B3"), ("r_b2", "B2")):
        w = a["L1_ffn_" + s]
        r[n] = km(w.transpose(0, 2, 1).reshape(256, w.shape[1]))
    wqkv = a["L2_attn_w_qkv"]
    wq, wg, wk, wv = wqkv[0:2048], wqkv[2048:4096], wqkv[4096:4608], wqkv[4608:5120]
    wq, wk = wq.reshape(16, 128, 256)[:, order], wk.reshape(4, 128, 256)[:, order]
    wg, wv = wg.reshape(16, 128, 256), wv.reshape(4, 128, 256)
    r["g_qk"] = np.stack([km(np.concatenate([wq[4 * g:4 * g + 4].reshape(512, 256), wk[g]], 0).T) for g in range(4)])
    r["g_gv"] = np.stack([km(np.concatenate([wg[4 * g:4 * g + 4].reshape(512, 256), wv[g]], 0).T) for g in range(4)])
    r["g_wo"] = np.ascontiguousarray(a["L2_attn_w_o"].T.reshape(4, 4, 128, 256).transpose(0, 2, 1, 3))
    r["q_w1"] = km(a["L2_ffn_w_gate_up"])
    r["q_w2"] = km(a["L2_ffn_w_down"])
    r["s_win"], r["s_wskip"] = km(a["L3_attn_W_in"].T), km(a["L3_attn_W_skip"].T)
    r["s_wd1"], r["s_wd2"] = km(a["L3_attn_Wd1"].T), km(a["L3_attn_Wd2"].T)
    r["s_wbc"] = km(np.concatenate([a["L3_attn_WB"], a["L3_attn_WC"]], 0).T)
    r["s_alog"] = km(a["L3_attn_A_log"])
    r["s_wout"] = km(a["L3_attn_W_out"].T)
    r["e_router"] = km(np.concatenate([a["L3_ffn_rg_w"], a["L3_ffn_ru_w"]], 0).T)
    r["e_extra"] = np.stack([a["L3_ffn_extra_scale"], a["L3_ffn_extra_bias"]])
    eg = np.stack([a["L3_ffn_Wg"].reshape(2816, 256), a["L3_ffn_Wu"].reshape(2816, 256)])
    eg = eg.reshape(2, 11, 2, 128, 2, 128)
    r["e_gu"] = np.ascontiguousarray(eg.transpose(1, 2, 5, 4, 0, 3))
    r["e_down"] = np.ascontiguousarray(a["L3_ffn_Wd"].transpose(0, 2, 1).reshape(11, 2, 128, 256))
    r["e_shared_gu"] = km(np.concatenate([a["L3_ffn_Sg"], a["L3_ffn_Su"]], 0).T)
    sd = a["L3_ffn_Sd"].T
    r["e_shared_down"] = km(np.concatenate([sd, np.zeros((32, 256), np.float32)], 0))
    return r, ofs


def kernel(**inputs):
    import numpy as np
    import concourse.bacc as bacc
    from concourse.bass_utils import run_bass_kernel_spmd as run
    arrays, offsets = _layout(inputs, np)
    nc = bacc.Bacc("TRN2", target_bir_lowering=False, num_devices=1)
    arrays = {k: np.ascontiguousarray(v) for k, v in arrays.items()}
    d = {k: nc.dram_tensor("in_" + k, v.shape, mybir.dt.from_np(v.dtype), kind="ExternalInput").ap()
         for k, v in arrays.items()}
    d["vec_offsets"] = offsets
    out = nc.dram_tensor("out_x", [128, 2, 1024], F32, kind="ExternalOutput").ap()
    build_program(nc, d, out)
    r = run(nc, [{"in_" + k: v for k, v in arrays.items()}], core_ids=[0])
    y = np.asarray(r.results[0]["out_x"])
    return np.ascontiguousarray(y.transpose(2, 1, 0).reshape(4, 256, 256))
```

```python
import concourse.bass as bass
from concourse import mybir

F32 = mybir.dt.float32
BF16 = mybir.dt.bfloat16
F32R = mybir.dt.float32r
ALU = mybir.AluOpType
ACT = mybir.ActivationFunctionType
AX = mybir.AxisListType.X

P = 128
C = 256
CT = C // P
NB, T = 4, 256
TOK = NB * T
TT = TOK // P
HALF = 512
NH = TOK // HALF
NCOND = 8
ROUND = 1.5 * 2.0 ** 23
BIG = 1e30


class Counter:

    def __init__(self, nc, name):
        self.sem, self.n, self.name = nc.alloc_semaphore(name), 0, name
        self.base, self.per = 0, 0


class Token:

    def __init__(self, counter, n, loop, back=0):
        self.counter, self.n, self.loop, self.back = counter, n, loop, back


class Loop:
    def __init__(self, count):
        self.count, self.var, self.dry, self.done = count, None, True, False
        self.base, self.per = {}, {}


class Machine:
    def __init__(self, nc):
        self.nc, self.loop, self.counters, self.free = nc, None, [], {}
        self.pe, self.act, self.dve = Lane(self, nc.tensor, "pe"), Lane(self, nc.scalar, "act"), Lane(self, nc.vector, "dve")
        self.pool, self.sp = Lane(self, nc.gpsimd, "pool"), Lane(self, nc.sync, "sp")
        self.lanes = [self.pe, self.act, self.dve, self.pool]

    def counter(self, name):
        c = Counter(self.nc, name)
        self.counters.append(c)
        if self.loop is not None:
            self.loop.base[c] = 0
        return c

    def release(self, name, *tokens):
        self.free[name] = tokens

    def freed(self, name):
        return self.free.get(name, ())

    def fence(self, sp=True):
        for lane in self.lanes + ([self.sp] if sp else []):
            for other in self.lanes:
                lane.wait(Token(other.counter, other.counter.n, None))
        self.free = {}

    def run_loop(self, count, body, prefetch=None):
        assert self.loop is None
        self.fence(sp=False)
        loop = Loop(count)
        for c in self.counters:
            loop.base[c] = c.n
            c.n = 0
        self.loop = loop
        for lane in self.lanes + [self.sp]:
            lane.local = {}
        body(0)
        last = {k: tuple(Token(t.counter, t.n, loop, 1) for t in v) for k, v in self.free.items()}
        for c in self.counters:
            loop.per[c] = c.n
            c.n = 0
        for lane in self.lanes:
            c = lane.counter
            short = loop.per[c] + 1 - loop.base[c]
            if short > 0:
                lane.eng.sem_inc(c.sem, short)
                loop.base[c] += short
        for lane in self.lanes + [self.sp]:
            lane.local = {}
        self.free, loop.dry = last, False
        with self.nc.Fori(0, count) as i:
            loop.var = i
            body(i)
        for c in self.counters:
            assert c.n == loop.per[c], c.name
            c.n = loop.base[c] + count * loop.per[c]
        self.loop, loop.done = None, True
        if prefetch:
            prefetch()
        self.fence()


class Lane:

    def __init__(self, m, eng, name):
        self.m, self.eng, self.counter = m, eng, m.counter("done_" + name)
        self.known, self.local = {}, {}

    def wait(self, t):
        if t is None:
            return
        c, loop = t.counter, t.loop
        if loop is not None and not loop.done:
            assert loop is self.m.loop
            v = t.n - t.back * 10 ** 6
            if self.local.get(c, -10 ** 9) >= v:
                return
            self.local[c] = v
            if not loop.dry:
                off = loop.base[c] + t.n - t.back * loop.per[c]
                self.eng.wait_ge(c.sem, loop.var * loop.per[c] + off)
            return
        v = t.n if loop is None else loop.base[c] + (loop.count - 1) * loop.per[c] + t.n
        if self.known.get(c, 0) >= v or v == 0:
            return
        if self.m.loop is not None:
            assert v <= self.m.loop.base[c]
            if self.m.loop.dry:
                return
        else:
            self.known[c] = v
        self.eng.wait_ge(c.sem, v)

    def issue(self, build, *waits, count=1, counter=None):
        for t in waits:
            self.wait(t)
        loop = self.m.loop
        if loop is None or not loop.dry:
            ins = build(self.eng)
            if count:
                ins.then_inc((counter or self.counter).sem, count)
        c = counter or self.counter
        c.n += count
        return Token(c, c.n, loop)

    def do(self, build, *waits):
        return self.issue(build, *waits)

    def quiet(self, build, *waits):
        return self.issue(build, *waits, count=0)

    def here(self):
        return Token(self.counter, self.counter.n, self.m.loop)


def build_program(nc, d, out):
    m = Machine(nc)
    PE, A, V, G, SP = m.pe, m.act, m.dve, m.pool, m.sp

    def sb(name, shape, dt=F32):
        return nc.alloc_sbuf_tensor(name, shape, dt)

    banks = [nc.alloc_psum_tensor(f"bank{i}", [P, 512], F32) for i in range(8)]

    class Phase:

        def __init__(self):
            self.open = []

        def __enter__(self):
            return self

        def __call__(self, name, shape, dt=F32):
            g = nc.sbuf_tensor(name, shape, dt)
            self.open.append(g)
            return g.__enter__()

        def __exit__(self, *e):
            for g in reversed(self.open):
                g.__exit__(None, None, None)
            m.fence()

    def load(counter, dst, src, *waits):
        return SP.issue(lambda e: e.dma_start(dst() if callable(dst) else dst, src() if callable(src) else src),
                        *waits, count=16, counter=counter)

    ld = {}

    def ctr(name):
        if name not in ld:
            ld[name] = m.counter("load_" + name)
        return ld[name]

    def mm(out_ap, pairs, *waits, start=True, stop=True):
        for n, (lhs, rhs) in enumerate(pairs):
            last = n == len(pairs) - 1
            f = lambda e, l=lhs, r=rhs, s=(start and n == 0), z=(stop and last): e.matmul(
                out_ap, l, r, start=s, stop=z, skip_group_check=True)
            tok = (PE.do if last else PE.quiet)(f, *(waits if n == 0 else ()))
        return tok

    def half(h):
        return slice(h * HALF, (h + 1) * HALF)

    XT = sb("residual", [P, CT, TOK])
    XC = sb("conditioned", [P, CT, TOK])
    ident = sb("ident", [P, P])
    identb = sb("identb", [P, P], BF16)
    ones = sb("ones", [P, P])
    vecs = sb("vecs", [P, d["vecs"].shape[1]])
    eps = sb("eps", [P, 4])
    cond = sb("cond", [P, NB, 64])
    tf = sb("tf", [P, NB])
    decay = sb("decay", [P, NCOND, CT, NB])
    gain = sb("gain", [P, NB])
    factors = [sb(f"factor{i}", [P, CT, TOK]) for i in range(3)]
    SLOT = (0, 1, 0, 1, 0, 1, 2, 0)
    gain8 = sb("gain8", [P, CT * NB])
    side = Phase()
    kv = side("side", [P, CT, TOK])
    ek = side("ek", [P, CT, TOK])
    ekv = side("ekv", [P, CT, TOK])
    wkt = side("wkv_temps", [P, 8, T])
    vofs = d["vec_offsets"]

    def vcol(name, n=0):
        return vecs[:, vofs[name] + n:vofs[name] + n + 1]

    c0 = ctr("start")
    load(c0, vecs[:, :], d["vecs"])
    load(c0, cond[:, :, :], d["cond"].partition_broadcast(P))
    t_start = load(c0, kv[:, :, :], d["side"])
    load(ctr("x"), ident[:, :], d["ident"])
    t_x = load(ctr("x"), XT[:, :, :], d["x"])
    V.do(lambda e: e.memset(ones[:, :], 1.0))
    EPS = {2.0 ** -23: 0, 1e-6: 1, 1e-5: 2, 1.0: 3}
    for v, n in EPS.items():
        t_eps = V.do(lambda e, v=v, n=n: e.memset(eps[:, n:n + 1], v))

    def eps_col(v):
        return eps[:, EPS[v]:EPS[v] + 1]

    t = V.do(lambda e: e.reduce_sum(tf[:, :], cond[:, :, :], AX), t_start)
    t = A.do(lambda e: e.activation(tf[:, :], tf[:, :], ACT.Sigmoid), t)
    t_gain = V.do(lambda e: e.tensor_scalar(gain[:, :], tf[:, :], 0.2, 0.8, ALU.mult, ALU.add), t)
    t = V.do(lambda e: e.tensor_scalar(tf[:, :], tf[:, :], 0.5, 0.5, ALU.mult, ALU.add), t_gain)
    wv = vecs[:, vofs["cond_w"]:vofs["cond_w"] + NCOND * CT]
    ta = A.do(lambda e: e.activation(wv, wv, ACT.Exp), t_start)
    ta = A.do(lambda e: e.activation(wv, wv, ACT.Exp, scale=-1.0), ta)
    for b in range(NB):
        t_decay = V.do(lambda e, b=b: e.tensor_scalar(
            decay[:, :, :, b], wv.rearrange("p (l c) -> p l c", c=CT), tf[:, b:b + 1], None, ALU.mult), ta, t)
    for ct in range(CT):
        t = V.do(lambda e, ct=ct: e.tensor_scalar(ek[:, ct, :], kv[:, ct, :], 30.0, None, ALU.min), t_start)
        t = A.do(lambda e, ct=ct: e.activation(ek[:, ct, :], ek[:, ct, :], ACT.Exp), t)
        t = V.do(lambda e, ct=ct: e.tensor_tensor(ekv[:, ct, :], ek[:, ct, :], kv[:, ct, :], ALU.mult), t)
    V.wait(t)
    V.wait(t_decay)

    def by_unit(a):
        return a[:, :, :].rearrange("p c (b t) -> p (c b) t", t=T)

    for ct in range(CT):
        V.do(lambda e: e.tensor_copy(gain8[:, ct * NB:(ct + 1) * NB], gain[:, :]))

    def wkv_start(l, euk):
        for ct in range(CT):
            t = V.do(lambda e: e.tensor_scalar(euk[:, ct, :], kv[:, ct, :], vcol("cond_u", l * CT + ct), 30.0, ALU.add, ALU.min))
            t = A.do(lambda e: e.activation(euk[:, ct, :], euk[:, ct, :], ACT.Exp), t)
        V.wait(t)

    def wkv_unit(l, u, euk):
        dst = by_unit(factors[SLOT[l]])
        at = lambda a: by_unit(a)[:, bass.ts(u, 1), :].rearrange("p a t -> p (a t)")
        col = lambda a: a[:, bass.ts(u, 1)]
        dec = lambda: decay[:, l, :, :].rearrange("p c b -> p (c b)")[:, bass.ts(u, 1)].to_broadcast([P, T])
        w = [wkt[:, n, :] for n in range(8)]
        t6 = V.do(lambda e: e.tensor_scalar(w[6], at(ekv), 1.0, None, ALU.mult), *m.freed("wkt"))
        t7 = V.do(lambda e: e.tensor_scalar(w[7], at(ek), 1.0, None, ALU.mult))
        yield
        scans = {}
        for n, src, t in ((0, ekv, None), (2, ek, None), (1, w[6], t6), (3, w[7], t7)):
            if t is None:
                scans[n] = V.do(lambda e: e.tensor_tensor_scan(w[n], dec(), at(src), 0.0, ALU.mult, ALU.add), *m.freed("wkt"))
            else:
                scans[n] = V.do(lambda e: e.tensor_tensor_scan(w[n][:, ::-1], dec(), src[:, ::-1], 0.0, ALU.mult, ALU.add), t)
            yield
        te = V.do(lambda e: e.tensor_tensor(w[4], at(euk), at(ek), ALU.subtract))
        yield
        t1 = G.do(lambda e: e.tensor_tensor(w[0], w[0], w[1], ALU.add), scans[0], scans[1], te)
        t3 = V.do(lambda e: e.tensor_tensor(w[2], w[2], w[3], ALU.add), scans[2], scans[3])
        t5 = V.do(lambda e: e.tensor_tensor(w[5], w[4], at(kv), ALU.mult), te)
        yield
        t3 = V.do(lambda e: e.tensor_tensor(w[2], w[2], w[4], ALU.add), t3)
        t1 = G.do(lambda e: e.tensor_tensor(w[0], w[0], w[5], ALU.add), t5, t1)
        yield
        t3 = V.do(lambda e: e.tensor_scalar(w[2], w[2], 1e-8, None, ALU.max), t3)
        yield
        t3 = V.do(lambda e: e.reciprocal(w[2], w[2]), t3)
        yield
        t = V.do(lambda e: e.scalar_tensor_tensor(at(factors[SLOT[l]]), w[0], col(gain8), w[2], ALU.mult, ALU.mult), t1, t3)
        m.release("wkt", t)
        yield

    def wkv_units(jobs):
        for l, u, euk in jobs:
            yield from wkv_unit(l, u, euk)

    def step(background, n):
        for _ in range(n):
            next(background, None)

    def condition(l):
        factor = factors[SLOT[l]]
        toks = []
        for ct in range(CT):
            t = A.do(lambda e: e.activation(XC[:, ct, :], XT[:, ct, :], ACT.Sigmoid))
            toks.append(V.do(lambda e: e.tensor_tensor(XC[:, ct, :], XC[:, ct, :], factor[:, ct, :], ALU.mult), t))
        return toks

    def inverse_root(src, ready, sq, dst, e_value, width=C, bank0=0, tiles=CT):
        for ct in range(tiles):
            t = A.do(lambda e: e.activation(sq[:, ct, :], src[:, ct, :], ACT.Square), ready[ct])
        for h in range(NH):
            bk = f"bank{bank0 + h}"
            t2 = mm(banks[bank0 + h][:, :], [(ones[:, :], sq[:, ct, half(h)]) for ct in range(tiles)], t, *m.freed(bk))
            t2 = A.do(lambda e: e.activation(dst[:, half(h)], banks[bank0 + h][:, :], ACT.Ln, scale=1.0 / width,
                                             bias=eps_col(e_value)), t2)
            m.release(bk, t2)
            t3 = A.do(lambda e: e.activation(dst[:, half(h)], dst[:, half(h)], ACT.Exp, scale=-0.5), t2)
        return t3

    def scale_rows(src, rs, wname, dst, t, tiles=CT):
        return [V.do(lambda e: e.scalar_tensor_tensor(dst[:, ct, :], src[:, ct, :], vcol(wname, ct), rs[:, :],
                                                      ALU.mult, ALU.mult), t) for ct in range(tiles)]

    def project_residual(w, kt, src, ready, add=None, bank0=0):
        for ct in range(CT):
            for h in range(NH):
                b = bank0 + ct * NH + h
                t = mm(banks[b][:, :], [(w[:, k, ct * P:(ct + 1) * P], src[:, k, half(h)]) for k in range(kt)],
                       *ready, *m.freed(f"bank{b}"))
                o = XT[:, ct, half(h)]
                t = V.do(lambda e: e.tensor_tensor(o, o, banks[b][:, :], ALU.add), t)
                m.release(f"bank{b}", t)
                if add is not None:
                    V.do(lambda e: e.tensor_tensor(o, o, add[:, ct, half(h)], ALU.add), t)

    def ternary(w, n, total, buf, name, t_w):
        part = buf(name + "_part", [P, 2])
        wf = w[:, :, :].rearrange("p c n -> p (c n)")
        t = V.do(lambda e: e.tensor_reduce(part[:, 0:1], wf, AX, ALU.add, apply_absolute_value=True), t_w)
        t = mm(banks[7][:, 0:1], [(ones[:, :], part[:, 0:1])], t, *m.freed("bank7"))
        t = V.do(lambda e: e.tensor_scalar(part[:, 0:1], banks[7][:, 0:1], 1.0 / total, 1e-5, ALU.mult, ALU.max), t)
        m.release("bank7", t)
        t = V.do(lambda e: e.reciprocal(part[:, 1:2], part[:, 0:1]), t)
        t = V.do(lambda e: e.tensor_scalar(wf, wf, part[:, 1:2], ROUND, ALU.mult, ALU.add), t)
        t = V.do(lambda e: e.tensor_scalar(wf, wf, -ROUND, -1.0, ALU.add, ALU.max), t)
        return V.do(lambda e: e.tensor_scalar(wf, wf, 1.0, part[:, 0:1], ALU.min, ALU.mult), t)

    def linear_attention():
        with Phase() as buf:
            wqkv = buf("l0_wqkv", [P, CT, d["l0_qkv"].shape[2]])
            wp = buf("l0_wp", [P, 4, C])
            srow = buf("l0_s", [P, 16])
            dist = buf("l0_dist", [P, T + P])
            decm = buf("l0_decm", [P, 16, T + P])
            t_s = load(ctr("l0s"), srow[:, :], d["l0_s"].partition_broadcast(P))
            t_w = load(ctr("l0"), wqkv[:, :, :], d["l0_qkv"])
            t_p = load(ctr("l0p"), wp[:, :, :], d["l0_proj"])
            t_d = load(ctr("l0d"), dist[:, :], d["dist"])
            q4 = buf("l0_q4", [P, 4, TOK])
            k4 = buf("l0_k4", [P, 4, TOK])
            v = buf("l0_v", [P, TT, 2 * C])
            heads = lambda a: a.rearrange("p (h d) -> p h d", d=32)[:, :, 0:16]
            t_v0 = G.do(lambda e: e.memset(v[:, :, :], 0.0))
            euk = buf("l0_euk", [P, CT, TOK])
            wkv_start(0, euk)
            for _ in wkv_units([(0, u_, euk) for u_ in range(CT * NB)]):
                pass
            ts = V.do(lambda e: e.tensor_scalar(srow[:, :], srow[:, :], -1.0, None, ALU.mult), t_s)
            for h in range(16):
                t = A.do(lambda e: e.activation(decm[:, h, :], dist[:, :], ACT.Exp, scale=srow[:, h:h + 1]), ts, t_d)
                for c_, w_ in ((0, T), (T, P)):
                    t_m = G.do(lambda e: e.affine_select(out=decm[:, h, c_:c_ + w_], in_=decm[:, h, c_:c_ + w_], compare_op=ALU.is_ge,
                                                         fill=0.0, base=0, pattern=[[1, w_]], channel_multiplier=-1), t)
            tq = ternary(wqkv, 768, 768 * C, buf, "l0q", t_w)
            tp = ternary(wp, C, C * C, buf, "l0p", t_p)
            for lane in (A, V):
                lane.wait(t_x)
            V.do(lambda e: e.tensor_copy(identb[:, :], ident[:, :]))
            ready = condition(0)
            V.wait(m.freed("wkt")[0])
            wkv_start(1, euk)
            with Phase() as b2:
                sq = b2("l0_sq", [P, CT, TOK])
                rs = b2("l0_rs", [P, TOK])
                t = inverse_root(XC, ready, sq, rs, 2.0 ** -23)
                rdy = scale_rows(XC, rs, "l0_qkv_norm", sq, t)
                wq = wqkv
                n = 0
                for dst, base in ((q4, 0), (k4, 2 * C)):
                    for tile in range(4):
                        for h in range(NH):
                            b = n % 4
                            n += 1
                            t = mm(banks[b][:, :], [(wq[:, k, base + tile * P:base + (tile + 1) * P], sq[:, k, half(h)])
                                                    for k in range(CT)], *rdy, tq, *m.freed(f"bank{b}"))
                            o = dst[:, tile, half(h)]
                            t = A.do(lambda e: e.copy(o, banks[b][:, :]), t) if h else V.do(lambda e: e.tensor_copy(o, banks[b][:, :]), t)
                            m.release(f"bank{b}", t)
                for tt in range(TT):
                    b = 4 + tt % 4
                    t = mm(banks[b][:, 0:C], [(sq[:, k, tt * P:(tt + 1) * P], wq[:, k, 4 * C:5 * C]) for k in range(CT)],
                           *rdy, tq, *m.freed(f"bank{b}"))
                    t = V.do(lambda e: e.tensor_copy(heads(v[:, tt, :]), banks[b][:, 0:C].rearrange("p (h d) -> p h d", d=16)), t, t_v0)
                    m.release(f"bank{b}", t)
            with Phase() as b2:
                NPR = 3
                sm = [b2(f"l0_sm{i}", [P, T + P]) for i in range(2 * NPR)]
                o = b2("l0_o", [P, 4, TOK])
                pairs = [(b, tile, jj) for b in range(NB) for tile in range(4) for jj in range(2)]

                def scores(n):
                    b, tile, jj = pairs[n]
                    t0 = b * T
                    for part in range(2):
                        for k in range(2):
                            j, bk = 32 * (2 * jj + k), 2 * (n % NPR) + k
                            ks = slice(t0 + part * P, t0 + (part + 1) * P)
                            cols = slice(T, T + P) if part else slice(0, T)
                            t = PE.do(lambda e: e.matmul(banks[bk][:, cols], k4[j:j + 16, tile, ks],
                                                         q4[j:j + 16, tile, t0 + part * P:t0 + T], start=part == 0, stop=True,
                                                         skip_group_check=True), *m.freed(f"bank{bk}"))
                    for k in range(2):
                        i = 2 * (n % NPR) + k
                        tv = V.do(lambda e: e.tensor_tensor(sm[i][:, :], banks[i][:, 0:T + P], decm[:, 4 * tile + 2 * jj + k, :],
                                                            ALU.mult), t, t_m, *m.freed(f"sm{i}"))
                        m.release(f"bank{i}", tv)
                    return tv

                def mix(n, t):
                    b, tile, jj = pairs[n]
                    bk = 6 + (n // 2) % 2
                    for part in range(2):
                        for k in range(2):
                            j, i, h = 32 * (2 * jj + k), 2 * (n % NPR) + k, 4 * tile + 2 * jj + k
                            cols, src = (slice(P, T), slice(T, T + P)) if part else (slice(0, T), slice(0, T))
                            tp = PE.do(lambda e: e.matmul(banks[bk][j:j + 32, cols], v[:, 2 * b + part, 32 * h:32 * h + 32],
                                                          sm[i][:, src], start=part == 0, stop=True, skip_group_check=True),
                                       t, *(m.freed(f"bank{bk}") if jj == 0 else ()))
                            m.release(f"sm{i}", tp)
                    if jj:
                        t2 = A.do(lambda e: e.mul(o[:, tile, b * T:(b + 1) * T], banks[bk][:, 0:T], 0.25), tp)
                        m.release(f"bank{bk}", t2)

                background = wkv_units([(1, u_, euk) for u_ in range(CT * NB)])
                done = {}
                for n in range(len(pairs) + 2):
                    if n < len(pairs):
                        done[n] = scores(n)
                        step(background, 3)
                    if n >= 2:
                        mix(n - 2, done[n - 2])
                for _ in background:
                    pass
                m.fence()
                sq = q4
                rs = b2("l0_rs2", [P, TOK])
                t = inverse_root(o, [None] * 4, sq, rs, 1e-6, tiles=4)
                rdy = scale_rows(o, rs, "l0_norm", o, t, tiles=4)
                t = inverse_root(o, rdy, sq, rs, 2.0 ** -23, tiles=4)
                rdy = scale_rows(o, rs, "l0_proj_norm", o, t, tiles=4)
                project_residual(wp, 4, o, rdy + [tp])

    def pick_top(scores, taken, hot, revi, tmp, E, t):
        def bc(a):
            return a.unsqueeze(2).to_broadcast([P, TT, E])
        mx = tmp[:, 0, :, 0]
        w = tmp[:, 1, :, 0:E]
        if taken is not None:
            t = V.do(lambda e: e.scalar_tensor_tensor(w, taken, -BIG, scores, ALU.mult, ALU.add), t)
            src = w
        else:
            src = scores
        t = V.do(lambda e: e.tensor_reduce(mx, src, AX, ALU.max), t)
        t = V.do(lambda e: e.tensor_tensor(hot, src, bc(mx), ALU.is_equal), t)
        t = V.do(lambda e: e.tensor_tensor(hot, hot, revi, ALU.mult), t)
        t = V.do(lambda e: e.tensor_reduce(mx, hot, AX, ALU.max), t)
        return V.do(lambda e: e.tensor_tensor(hot, revi, bc(mx), ALU.is_equal), t)

    def token_logits(w, n, ready, bank=0):
        for tt in range(TT):
            for k in range(CT):
                f = lambda e: e.matmul(banks[bank][:, tt * n:(tt + 1) * n], XC[:, k, tt * P:(tt + 1) * P], w[:, k, :],
                                       start=(tt == 0 and k == 0), stop=(k == CT - 1), skip_group_check=True)
                wt = (*ready, *m.freed(f"bank{bank}")) if tt == 0 and k == 0 else ()
                t = (PE.do if (tt == TT - 1 and k == CT - 1) else PE.quiet)(f, *wt)
        return t

    def rows_from_tokens(src, n, dst, t):
        for tt in range(TT):
            b = 6 + tt // 4
            t2 = PE.do(lambda e: e.transpose(banks[b][0:n, (tt % 4) * P:(tt % 4 + 1) * P], src[:, tt, :], ident[:, :]), t,
                       *m.freed(f"bank{b}"))
            if tt % 4 == 3:
                h = tt // 4
                t2 = V.do(lambda e: e.tensor_copy(dst[0:n, half(h)], banks[b][0:n, :]), t2)
                m.release(f"bank{b}", t2)
        return t2

    def split(x, hi, lo, *waits, lane=V):
        t = A.do(lambda e: e.copy(hi, x), *waits)
        return lane.do(lambda e: e.tensor_tensor(lo, x, hi, ALU.subtract), t)

    def split_pairs(w, x):
        return [(a, b) for wk, xk in zip(w, x) for a, b in ((wk[0], xk[0]), (wk[0], xk[1]), (wk[1], xk[0]))]

    def gated_unit(u, n, sbuf):
        src, wg, wu, rows, h, coef = (u[key] for key in ("src", "wg", "wu", "rows", "h", "coef"))
        b, bk, i = 4 + 2 * (n % 2), f"pair{n % 2}", n % len(sbuf)
        if isinstance(src, tuple):
            x = [tuple(part[:, k, half(h)] for part in src) for k in range(CT)]
            mm(banks[b][:, :], split_pairs(wg, x), *u["waits"], *m.freed(bk))
            t = mm(banks[b + 1][:, :], split_pairs(wu, x))
        else:
            mm(banks[b][0:rows, :], [(wg[k], src[:, k, half(h)]) for k in range(CT)], *u["waits"], *m.freed(bk))
            t = mm(banks[b + 1][0:rows, :], [(wu[k], src[:, k, half(h)]) for k in range(CT)])
        s = sbuf[i][0:rows, :]
        t = A.do(lambda e: e.activation(s, banks[b][0:rows, :], ACT.Silu), t, *m.freed(f"s{i}"))
        t = V.do(lambda e: e.tensor_tensor(s, s, banks[b + 1][0:rows, :], ALU.mult), t)
        m.release(bk, t)
        if coef is not None:
            cf, tc = coef
            t = V.do(lambda e: e.tensor_tensor(s, s, cf(), ALU.mult), t, tc)
        return t

    def split_hidden(n, sbuf, hbuf, *t):
        i, k = n % len(sbuf), n % len(hbuf)
        hi, lo = hbuf[k]
        t = split(sbuf[i][:, :], hi[:, :], lo[:, :], *t, *m.freed(f"h{k}"))
        m.release(f"s{i}", t)
        return t

    def down_unit(wd, rows, h, n, sbuf, hbuf, first, last, waits):
        for ct in range(CT):
            cs = slice(ct * P, (ct + 1) * P)
            if isinstance(wd, tuple):
                name, pairs = f"h{n % len(hbuf)}", split_pairs([[part[:, cs] for part in wd]],
                                                               [[part[:, :] for part in hbuf[n % len(hbuf)]]])
            else:
                name, pairs = f"s{n % len(sbuf)}", [(wd[0:rows, cs], sbuf[n % len(sbuf)][0:rows, :])]
            t = mm(banks[ct * NH + h][:, :], pairs, *(waits if ct == 0 else ()), start=first, stop=last)
        m.release(name, t)
        return t

    def run_units(units, sbuf, hbuf, background=iter(()), pace=0, left=None):
        if units[0].get("before"):
            units[0]["before"]()
        downs, toks, last = {}, {}, len(units) - 1
        if left:
            down_unit(*left[0], m.freed("left0"))
            downs[-1] = (*left[1], [split_hidden(last, sbuf, hbuf, *m.freed("left1")), *m.freed("left1")])

        def finish(n):
            u = units[n]
            t = split_hidden(n, sbuf, hbuf, toks[n]) if isinstance(u["wd"], tuple) and not (left and n == last) else toks[n]
            downs[n] = (u["wd"], u["rows"], u["h"], n, sbuf, hbuf, u["first"], u["last"], [t] + u.get("down_waits", []))
            if u.get("after"):
                u["after"]()

        def down(n):
            if n in downs:
                down_unit(*downs[n])
                if n >= 0 and units[n].get("downed"):
                    units[n]["downed"]()
        for n, u in enumerate(units):
            if n:
                finish(n - 1)
            toks[n] = gated_unit(u, n, sbuf)
            for hook in ("done", "start"):
                if u.get(hook):
                    u[hook]()
            step(background, pace)
            if n + 1 < len(units) and units[n + 1].get("before"):
                units[n + 1]["before"]()
            down(n - 2)
        finish(last)
        for n in (last - 1, last):
            if left:
                m.release(f"left{n - last + 1}", *downs[n][-1])
            else:
                down(n)

    def leave(wd, count, sbuf, hbuf):
        for part in hbuf[(count - 2) % len(hbuf)]:
            V.do(lambda e: e.memset(part[:, :].bitcast(F32), 0.0))
        V.do(lambda e: e.memset(sbuf[(count - 1) % len(sbuf)][:, :], 0.0), V.here(), PE.here())
        for part in wd:
            V.do(lambda e: e.memset(part[:, :].bitcast(F32), 0.0))
        m.fence(sp=False)
        return [(wd, P, h, count - 2 + h, sbuf, hbuf, False, True) for h in range(NH)]

    def take_left(left):
        down_unit(*left[0], m.freed("left0"))
        n, sbuf, hbuf = left[1][3:6]
        down_unit(*left[1], [split_hidden(n, sbuf, hbuf, *m.freed("left1"))])

    def add_out_banks():
        t0 = PE.here()
        for ct in range(CT):
            for h in range(NH):
                o = XT[:, ct, half(h)]
                V.do(lambda e: e.tensor_tensor(o, o, banks[ct * NH + h][:, :], ALU.add), t0)

    def moe_top1():
        E, F = 8, 512
        FT = F // P
        with Phase() as buf:
            wr = buf("m0_wr", [P, CT, E])
            sg = buf("m0_sg", [P, CT, 2 * F])
            sd = buf("m0_sd", [P, FT, C])
            revi = buf("m0_revi", [P, TT, E])
            selm = buf("m0_sel", [16, 9, P])
            t_w = load(ctr("m0"), wr[:, :, :], d["m0_router"])
            load(ctr("m0"), revi[:, :, :], d["revi8"])
            t_w = load(ctr("m0"), selm[:, :, :], d["sel16"][:, 0:9, :])
            load(ctr("m0s"), sg[:, :, :], d["m0_shared_gu"])
            t_s = load(ctr("m0s"), sd[:, :, :], d["m0_shared_down"])
            euk2 = [buf(f"m0_euk{i}", [P, CT, TOK]) for i in range(2)]
            wkv_start(2, euk2[0])
            wkv_start(3, euk2[1])
            ready = condition(1)
            xs = tuple(buf(f"m0_xs{i}", [P, CT, TOK], F32R) for i in range(2))
            maskb = buf("m0_mask", [P, E, TOK], BF16)
            rows = buf("m0_rows", [16, TOK])
            rowsb = buf("m0_rowsb", [8, TOK], BF16)
            selb = buf("m0_selb", [8, 8, P], BF16)
            with Phase() as b2:
                lg = b2("m0_lg", [P, TT, E])
                hot = b2("m0_hot", [P, TT, 9])
                tmp = b2("m0_tmp", [P, 2, TT, 16])
                t = token_logits(wr, E, ready + [t_w])
                t = V.do(lambda e: e.tensor_copy(lg[:, :, :].rearrange("p t e -> p (t e)"), banks[0][:, 0:TT * E]), t)
                m.release("bank0", t)
                tm = V.do(lambda e: e.tensor_reduce(hot[:, :, 8], lg[:, :, :], AX, ALU.max), t)
                ta = A.do(lambda e: e.activation(hot[:, :, 8], hot[:, :, 8], ACT.Sigmoid), tm)
                t = pick_top(lg[:, :, :], None, hot[:, :, 0:8], revi[:, :, :], tmp, E, tm)
                PE.wait(ta)
                t = rows_from_tokens(hot, 9, rows, t)
                t_hot = V.do(lambda e: e.tensor_copy(rowsb[:, :], rows[0:8, :]), t)
                t_hot = V.do(lambda e: e.tensor_copy(selb[:, :, :], selm[0:8, 0:8, :]), t_hot)
            xt_ = [buf(f"m0_xt{i}", [P, HALF]) for i in range(2)]
            for e_ in range(9):
                for h in range(NH):
                    b = (e_ * NH + h) % 4
                    t = mm(banks[b][:, :], [(selb[:, e_, :], rowsb[:, half(h)]) if e_ < 8 else (selm[0:9, e_, :], rows[0:9, half(h)])],
                           t_hot, *m.freed(f"bank{b}"))
                    if e_ < 8:
                        t = A.do(lambda e: e.copy(maskb[:, e_, half(h)], banks[b][:, :]), t)
                    else:
                        for ct in range(CT):
                            x_ = xt_[ct]
                            tx = V.do(lambda e: e.tensor_tensor(x_[:, :], XC[:, ct, half(h)], banks[b][:, :], ALU.mult), t,
                                      *m.freed(f"xt{ct}"))
                            m.release(f"xt{ct}", split(x_[:, :], xs[0][:, ct, half(h)], xs[1][:, ct, half(h)], tx))
                        t = tx
                    m.release(f"bank{b}", t)
            m.fence()
            wgu = [buf(f"m0_wgu{j}", [P, CT, 2, P]) for j in range(FT)]
            wd = [buf(f"m0_wd{j}", [P, C]) for j in range(FT)]
            wsp = [tuple(buf(f"m0_wsp{j}{i}", [P, CT, 2, P], F32R) for i in range(2)) for j in range(2)]
            sbuf = [buf(f"m0_s{i}", [P, HALF]) for i in range(4)]
            hbuf = [tuple(buf(f"m0_h{i}{k}", [P, HALF], F32R) for k in range(2)) for i in range(4)]
            wdsp = [tuple(buf(f"m0_wdsp{j}{k}", [P, C], F32R) for k in range(2)) for j in range(FT)]
            units = []
            for ft in range(FT):
                for h in range(NH):
                    units.append(dict(src=XC, wg=[sg[:, k, ft * P:(ft + 1) * P] for k in range(CT)],
                                      wu=[sg[:, k, F + ft * P:F + (ft + 1) * P] for k in range(CT)],
                                      wd=sd[:, ft, :], rows=P, h=h, coef=None, first=ft == 0, last=False, waits=[t_s]))
            run_units(units, sbuf, hbuf)
            left = leave(wdsp[FT - 1], FT * NH, sbuf, hbuf)

            def body(i):
                toks = []
                for j in range(FT):
                    load(ctr(f"m0w{j}"), wgu[j][:, :, :, :], lambda: d["m0_gu"][i, j], *m.freed(f"wgu{j}"))
                    toks.append(load(ctr(f"m0w{j}"), wd[j][:, :], lambda: d["m0_down"][i, j], *m.freed(f"wd{j}")))
                units, t_split, t_down = [], [[] for _ in range(FT)], [[] for _ in range(FT)]

                def split_weights(j):
                    hi, lo = wsp[j % 2]
                    t = split(wgu[j][:, :, :, :], hi[:, :, :, :], lo[:, :, :, :], toks[j], *m.freed(f"wsp{j % 2}"), lane=G)
                    m.release(f"wgu{j}", t)
                    t_split[j].append(t)
                    hi, lo = wdsp[j]
                    t = split(wd[j][:, :], hi[:, :], lo[:, :], toks[j], *((PE.here(),) if j == FT - 1 else m.freed(f"wdsp{j}")), lane=G)
                    m.release(f"wd{j}", t)
                    t_down[j].append(t)
                split_weights(0)
                for ft in range(FT):
                    for h in range(NH):
                        cf = (lambda h=h: maskb[:, i, half(h)])

                        start = (lambda ft=ft: split_weights(ft + 1)) if h == 0 and ft + 1 < FT else None
                        w_ = wsp[ft % 2]
                        units.append(dict(src=xs, wg=[tuple(p[:, k, 0, :] for p in w_) for k in range(CT)],
                                          wu=[tuple(p[:, k, 1, :] for p in w_) for k in range(CT)], wd=wdsp[ft], rows=P, h=h,
                                          coef=(cf, None), first=False, last=True, waits=t_split[ft], down_waits=t_down[ft],
                                          start=start,
                                          downed=(lambda ft=ft: m.release(f"wdsp{ft}", PE.here())) if h == 1 else None,
                                          done=(lambda ft=ft: m.release(f"wsp{ft % 2}", PE.here())) if h == 1 else None))
                background = wkv_units([(2, i, euk2[0]), (3, i, euk2[1])])
                run_units(units, sbuf, hbuf, background, 4, left)
                for _ in background:
                    pass

            m.run_loop(E, body)
            take_left(left)
            add_out_banks()

    def banded_attention():
        NG, W = 16, 32
        KS = P + W + NG
        with Phase() as buf:
            wq = buf("b_wq", [P, CT, 2 * C])
            wk = buf("b_wk", [P, CT, 2 * C])
            wv = buf("b_wv", [P, CT, C])
            wo = buf("b_wo", [P, 4, C])
            msk = buf("b_msk", [P, 2, KS])
            small = buf("b_small", [P, CT, NB, W + NG])
            load(ctr("b"), wq[:, :, :], d["b_wq"])
            load(ctr("b"), wk[:, :, :], d["b_wk"])
            load(ctr("b"), wv[:, :, :], d["b_wv"])
            for b in range(NB):
                load(ctr("b"), small[:, :, b, W:W + NG], d["b_global"])
            load(ctr("b"), msk[:, :, :], d["b_mask"])
            t_w = load(ctr("b"), wo[:, :, :], d["b_wo"])
            ready = condition(2)
            q4 = buf("b_q4", [P, 4, TOK])
            k4 = buf("b_k4", [P, 4, TOK])
            ks4 = buf("b_ks4", [P, 4, NB * (W + NG)])
            v = buf("b_v", [P, TT, 2 * C])
            vs = buf("b_vs", [W + NG, NB, 2 * C])
            heads = lambda a: a.rearrange("p (h d) -> p h d", d=32)[:, :, 0:16]
            G.do(lambda e: e.memset(v[:, :, :], 0.0))
            t_v0 = G.do(lambda e: e.memset(vs[:, :, :], 0.0))
            with Phase() as b2:
                xn = b2("b_xn", [P, CT, TOK])
                sq = b2("b_sq", [P, CT, TOK])
                rs = b2("b_rs", [P, TOK])
                for h in range(NH):
                    t = mm(banks[h][:, :], [(ones[:, :], XC[:, k, half(h)]) for k in range(CT)], *ready, *m.freed(f"bank{h}"))
                    t = A.do(lambda e: e.mul(rs[:, half(h)], banks[h][:, :], 1.0 / C), t)
                    m.release(f"bank{h}", t)
                rdy = [V.do(lambda e: e.tensor_tensor(xn[:, ct, :], XC[:, ct, :], rs[:, :], ALU.subtract), t) for ct in range(CT)]
                A.wait(rdy[-1])
                t = inverse_root(xn, rdy, sq, rs, 1e-5)
                rdy = scale_rows(xn, rs, "b_ln_scale", xn, t)
                rdy = [A.do(lambda e: e.activation(xn[:, ct, :], xn[:, ct, :], ACT.Identity, bias=vcol("b_ln_bias", ct)), rdy[ct])
                       for ct in range(CT)]
                t_sm = V.do(lambda e: e.tensor_copy(
                    small[:, :, :, 0:W], xn[:, :, :].rearrange("p c (b t) -> p c b t", b=NB)[:, :, :, P - W:P]), *rdy, t_w)
                n = 0
                jobs = [(q4, wq, xn, half(h), tile) for tile in range(4) for h in range(NH)]
                jobs += [(k4, wk, xn, half(h), tile) for tile in range(4) for h in range(NH)]
                smf = small[:, :, :, :].rearrange("p c b t -> p c (b t)")
                jobs += [(ks4, wk, smf, slice(0, NB * (W + NG)), tile) for tile in range(4)]
                for dst, w, src, cols, tile in jobs:
                    b = n % 4
                    n += 1
                    nn = cols.stop - cols.start
                    t = mm(banks[b][:, 0:nn], [(w[:, k, tile * P:(tile + 1) * P], src[:, k, cols]) for k in range(CT)],
                           *rdy, t_w, t_sm, *m.freed(f"bank{b}"))
                    o = dst[:, tile, cols]
                    t = A.do(lambda e: e.copy(o, banks[b][:, 0:nn]), t) if n % 2 else V.do(lambda e: e.tensor_copy(o, banks[b][:, 0:nn]), t)
                    m.release(f"bank{b}", t)
                for tt in range(TT):
                    b = 4 + tt % 4
                    t = mm(banks[b][:, 0:C], [(xn[:, k, tt * P:(tt + 1) * P], wv[:, k, :]) for k in range(CT)], *m.freed(f"bank{b}"))
                    t = V.do(lambda e: e.tensor_copy(heads(v[:, tt, :]), banks[b][:, 0:C].rearrange("p (h d) -> p h d", d=16)), t, t_v0)
                    m.release(f"bank{b}", t)
                for b_ in range(NB):
                    b = 4 + b_
                    t = mm(banks[b][0:W + NG, 0:C], [(small[:, k, b_, :], wv[:, k, :]) for k in range(CT)], *m.freed(f"bank{b}"))
                    t = V.do(lambda e: e.tensor_copy(heads(vs[:, b_, :]),
                                                     banks[b][0:W + NG, 0:C].rearrange("p (h d) -> p h d", d=16)), t, t_v0)
                    m.release(f"bank{b}", t)
            with Phase() as b2:
                NS = 5
                s_ = [b2(f"b_s{i}", [P, 2, KS]) for i in range(NS)]
                st = b2("b_st", [P, 3, 8])
                pt = [b2(f"b_pt{i}", [P, 4 * P]) for i in range(3)]
                o = b2("b_o", [P, 4, TOK])
                pairs = [(tt, tile, jj) for tt in range(TT) for tile in range(4) for jj in range(2)]

                def scores(n):
                    tt, tile, jj = pairs[n]
                    b, s, c = tt // 2, s_[n % NS], 2 * (n % 4)
                    for part in range(2):
                        for k in range(2):
                            j, bk = 32 * (2 * jj + k), 2 * (n % 2) + k
                            ql = q4[j:j + 16, tile, tt * P:(tt + 1) * P]
                            kk = k4[j:j + 16, tile, tt * P:(tt + 1) * P] if part == 0 else \
                                ks4[j:j + 16, tile, b * (W + NG):(b + 1) * (W + NG)]
                            cols = slice(P, KS) if part else slice(0, P)
                            t = PE.do(lambda e: e.matmul(banks[bk][:, cols], ql, kk, start=part == 0, stop=True,
                                                         skip_group_check=True), *m.freed(f"bank{bk}"))
                    for k in range(2):
                        bk = 2 * (n % 2) + k
                        tv = V.do(lambda e: e.tensor_tensor_reduce(s[:, k, :], banks[bk][:, 0:KS], msk[:, tt % 2, :], 1.0, -BIG,
                                                                   ALU.add, ALU.max, st[:, 0, c + k:c + k + 1]), t,
                                  *m.freed(f"s{n % NS}"))
                        m.release(f"bank{bk}", tv)
                    t = V.do(lambda e: e.tensor_scalar(st[:, 0, c:c + 2], st[:, 0, c:c + 2], -0.25, None, ALU.mult), tv)
                    for k in range(2):
                        ta = A.do(lambda e: e.activation(s[:, k, :], s[:, k, :], ACT.Exp, bias=st[:, 0, c + k:c + k + 1], scale=0.25,
                                                         accum_out=st[:, 1, c + k:c + k + 1]), t)
                    return ta

                def normalise(n, t):
                    s, c = s_[n % NS], 2 * (n % 4)
                    t = V.do(lambda e: e.reciprocal(st[:, 2, c:c + 2], st[:, 1, c:c + 2]), t)
                    return V.do(lambda e: e.tensor_tensor(s[:, :, :], s[:, :, :], st[:, 2, c:c + 2].unsqueeze(2).to_broadcast([P, 2, KS]),
                                                          ALU.mult), t)

                def turn(n, t):
                    bk, s, p_ = 4 + n % 2, s_[n % NS], pt[n % 3]
                    for k in range(2):
                        PE.quiet(lambda e: e.transpose(banks[bk][:, k * P:(k + 1) * P], s[:, k, 0:P], ident[:, :]), t,
                                 *m.freed(f"bank{bk}"))
                        tp = PE.do(lambda e: e.transpose(banks[bk][0:W + NG, (2 + k) * P:(3 + k) * P], s[:, k, P:KS], ident[:, :]))
                    m.release(f"s{n % NS}", tp)
                    A.do(lambda e: e.copy(p_[:, 0:2 * P], banks[bk][:, 0:2 * P]), tp, *m.freed(f"pt{n % 3}"))
                    t = A.do(lambda e: e.copy(p_[0:W + NG, 2 * P:4 * P], banks[bk][0:W + NG, 2 * P:4 * P]))
                    m.release(f"bank{bk}", t)
                    return t

                def mix(n, t):
                    tt, tile, jj = pairs[n]
                    bk, p_ = 6 + (n // 2) % 2, pt[n % 3]
                    for part in range(2):
                        for k in range(2):
                            j, h = 32 * (2 * jj + k), 4 * tile + 2 * jj + k
                            hs = slice(32 * h, 32 * h + 32)
                            lhs = vs[:, tt // 2, hs] if part else v[:, tt, hs]
                            rhs = p_[0:W + NG, (2 + k) * P:(3 + k) * P] if part else p_[:, k * P:(k + 1) * P]
                            tp = PE.do(lambda e: e.matmul(banks[bk][j:j + 32, 0:P], lhs, rhs, start=part == 0, stop=part == 1,
                                                          skip_group_check=True), t, *(m.freed(f"bank{bk}") if jj == 0 else ()))
                    m.release(f"pt{n % 3}", tp)
                    if jj:
                        t2 = V.do(lambda e: e.tensor_copy(o[:, tile, tt * P:(tt + 1) * P], banks[bk][:, 0:P]), tp)
                        m.release(f"bank{bk}", t2)
                    return tp

                exps, norms, turns, last = {}, {}, {}, len(pairs)
                for n in range(last + 4):
                    if 0 <= n - 2 < last:
                        norms[n - 2] = normalise(n - 2, exps[n - 2])
                    if 0 <= n - 3 < last:
                        turns[n - 3] = turn(n - 3, norms[n - 3])
                    if n < last:
                        exps[n] = scores(n)
                    if 0 <= n - 4 < last:
                        mix(n - 4, turns[n - 4])
                m.fence()
                project_residual(wo, 4, o, [], add=XC)

    def lora_ffn():
        E, F = 8, 896
        FT = F // P
        with Phase() as buf:
            wr = buf("r_wr", [P, CT, E])
            w1 = buf("r_w1", [P, CT, F])
            w3 = buf("r_w3", [P, CT, F])
            w2 = buf("r_w2", [P, FT, C])
            b1 = buf("r_b1", [P, CT, F])
            b3 = buf("r_b3", [P, CT, F])
            a2 = buf("r_a2", [P, FT, C])
            b2w = buf("r_b2", [P, CT, C])
            t_wr = load(ctr("rr"), wr[:, :, :], d["r_router"])
            ready = condition(3)
            rows = buf("r_rows", [18, TOK])
            a1 = buf("r_a1", [P, CT, C])
            a3 = buf("r_a3", [P, CT, C])
            sel = buf("r_sel", [18, 2, P])
            selx = buf("r_selx", [18, 2, CT, P])
            load(ctr("r2"), a1[:, :, :], d["r_a1"])
            load(ctr("r2"), a3[:, :, :], d["r_a3"])
            load(ctr("r2"), sel[:, :, :], d["r_sel"])
            load(ctr("r2"), selx[:, :, :, :], d["r_selx"])
            with Phase() as bb:
                revi = bb("r_revi", [P, TT, E])
                t_w2 = load(ctr("r2"), revi[:, :, :], d["revi8"])
                for dst, name in ((w1, "r_w1"), (w3, "r_w3"), (b1, "r_b1"), (b3, "r_b3"), (a2, "r_a2"), (b2w, "r_b2"), (w2, "r_w2")):
                    t_w = load(ctr("r"), dst[:, :, :], d[name])
                pr = bb("r_pr", [P, TT, E])
                hot = bb("r_hot", [P, TT, 18])
                tmp = bb("r_tmp", [P, 2, TT, 16])
                st = bb("r_st", [P, 4, TT])

                def bc(a, n=E):
                    return a.unsqueeze(2).to_broadcast([P, TT, n])
                t = token_logits(wr, E, ready + [t_wr])
                t = V.do(lambda e: e.tensor_copy(pr[:, :, :].rearrange("p t e -> p (t e)"), banks[0][:, 0:TT * E]), t)
                m.release("bank0", t)
                t = V.do(lambda e: e.tensor_reduce(st[:, 0, :], pr[:, :, :], AX, ALU.max), t)
                t = V.do(lambda e: e.tensor_tensor(pr[:, :, :], pr[:, :, :], bc(st[:, 0, :]), ALU.subtract), t)
                t = A.do(lambda e: e.activation(pr[:, :, :], pr[:, :, :], ACT.Exp), t)
                t = V.do(lambda e: e.tensor_reduce(st[:, 0, :], pr[:, :, :], AX, ALU.add), t)
                t = V.do(lambda e: e.reciprocal(st[:, 0, :], st[:, 0, :]), t)
                t = V.do(lambda e: e.tensor_tensor(pr[:, :, :], pr[:, :, :], bc(st[:, 0, :]), ALU.mult), t)
                V.wait(t_w2)
                t = pick_top(pr[:, :, :], None, hot[:, :, 0:8], revi[:, :, :], tmp, E, t)
                t = pick_top(pr[:, :, :], hot[:, :, 0:8], hot[:, :, 8:16], revi[:, :, :], tmp, E, t)
                for k in range(2):
                    t = V.do(lambda e: e.tensor_tensor(tmp[:, 1, :, 0:8], pr[:, :, :], hot[:, :, 8 * k:8 * k + 8], ALU.mult), t)
                    t = V.do(lambda e: e.tensor_reduce(st[:, k, :], tmp[:, 1, :, 0:8], AX, ALU.add), t)
                t = V.do(lambda e: e.tensor_tensor(st[:, 2, :], st[:, 0, :], st[:, 1, :], ALU.add), t)
                t = V.do(lambda e: e.reciprocal(st[:, 2, :], st[:, 2, :]), t)
                for k in range(2):
                    t = V.do(lambda e: e.tensor_tensor(hot[:, :, 16 + k], st[:, k, :], st[:, 2, :], ALU.mult), t)
                t_rows = rows_from_tokens(hot, 18, rows, t)
            maskx = buf("r_maskx", [P, 2, CT, HALF])
            rwb = buf("r_rwb", [P, 2, HALF])
            md = buf("r_md", [P, HALF])
            am = [[buf(f"r_am{k}{j}", [P, CT, HALF]) for j in range(2)] for k in range(2)]
            euk = buf("r_euk", [P, CT, TOK])

            def prepare(h):
                for k in range(2):
                    t2 = mm(banks[k][:, :], [(sel[:, k, :], rows[:, half(h)])], *m.freed(f"bank{k}"), *m.freed("pair0"))
                    t2 = A.do(lambda e: e.copy(rwb[:, k, :], banks[k][:, :]), t2, *m.freed("rwb"))
                    m.release(f"bank{k}", t2)
                for ct in range(CT):
                    for k in range(2):
                        t2 = mm(banks[2 + k][:, :], [(selx[:, k, ct, :], rows[:, half(h)])], *m.freed(f"bank{2 + k}"), *m.freed("pair1"))
                        t2 = A.do(lambda e: e.copy(maskx[:, k, ct, :], banks[2 + k][:, :]), t2, *m.freed("maskx"))
                        m.release(f"bank{2 + k}", t2)
                    td = V.do(lambda e: e.tensor_tensor(md[:, :], maskx[:, 1, ct, :], maskx[:, 0, ct, :], ALU.subtract), t2,
                              *m.freed("md"))
                    for j, w in enumerate((a1, a3)):
                        b = 4 + j
                        t3 = mm(banks[b][:, :], [(w[:, k2, ct * P:(ct + 1) * P], XC[:, k2, half(h)]) for k2 in range(CT)],
                                *m.freed(f"bank{b}"))
                        for k in range(2):
                            src = maskx[:, 0, ct, :] if k == 0 else md[:, :]
                            t3 = V.do(lambda e: e.tensor_tensor(am[k][j][:, ct, :], src, banks[b][:, :], ALU.mult), t3, td,
                                      *m.freed("am"))
                        m.release(f"bank{b}", t3)
                    m.release("md", t3)
                for b in range(2):
                    m.release(f"pair{b}", *m.freed(f"bank{2 * b}"), *m.freed(f"bank{2 * b + 1}"))
                PE.wait(t3)
                PE.wait(t_w)

            with Phase() as bb:
                ys = bb("r_ys", [P, FT, HALF])
                y = [[bb(f"r_y{k}{i}", [P, HALF]) for i in range(3)] for k in range(2)]
                sl = [bb(f"r_sl{i}", [P, HALF]) for i in range(2)]
                u2 = bb("r_u2", [P, CT, HALF])
                u3 = bb("r_u3", [P, HALF])
                wkv_start(4, euk)
                background = wkv_units([(4, u_, euk) for u_ in range(CT * NB)])
                for h in range(NH):
                    if h == 1:
                        wkv_start(5, euk)
                        background = wkv_units([(5, u_, euk) for u_ in range(CT * NB)])
                    prepare(h)

                    def up(ft, k):
                        pr_ = ft % 2
                        b = 2 * pr_
                        fs = slice(ft * P, (ft + 1) * P)
                        first = [(w1, b1), (w3, b3)]
                        for j, (w, lw) in enumerate(first):
                            pairs = [(lw[:, c, fs], am[k][j][:, c, :]) for c in range(CT)]
                            if k == 0:
                                pairs = [(w[:, c, fs], XC[:, c, half(h)]) for c in range(CT)] + pairs
                            t = mm(banks[b + j][:, :], pairs, *m.freed(f"pair{pr_}"), start=(k == 0))
                        s, yy = sl[k], y[k][ft % 3]
                        t1 = A.do(lambda e: e.activation(s[:, :], banks[b][:, :], ACT.Silu), t, *m.freed(f"sl{k}"))
                        t1 = V.do(lambda e: e.tensor_tensor(s[:, :], s[:, :], banks[b + 1][:, :], ALU.mult), t1)
                        m.release(f"pair{pr_}", t1)
                        t2 = V.do(lambda e: e.tensor_tensor(yy[:, :], s[:, :], rwb[:, k, :], ALU.mult), t1, *m.freed(f"y{k}{ft % 3}"))
                        m.release(f"sl{k}", t2)
                        return t2

                    def low(ft, k, t, t0):
                        pr_ = ft % 3
                        rel = ()
                        if k == 1:
                            rel = (G.do(lambda e: e.tensor_tensor(ys[:, ft, :], y[0][pr_][:, :], y[1][pr_][:, :], ALU.add), t, t0,
                                        *m.freed("ys")),)
                        for ct in range(CT):
                            f = lambda e: e.matmul(banks[4 + 2 * k + ct][:, :], a2[:, ft, ct * P:(ct + 1) * P], y[k][pr_][:, :],
                                                   start=(ft == 0), stop=(ft == FT - 1), skip_group_check=True)
                            tt_ = (PE.do if ct else PE.quiet)(f, t, *m.freed(f"bank{4 + 2 * k + ct}"))
                        if k == 1:
                            m.release(f"y1{pr_}", tt_, *rel)
                            m.release(f"y0{pr_}", tt_, *rel)
                        return rel[0] if rel else None

                    t0 = {}
                    tg = None
                    order = []
                    for ft in range(FT + 1):
                        if ft < FT:
                            order.append((ft, 0))
                        if ft > 0:
                            order.append((ft - 1, 1))
                    for ft, k in order:
                        t0[ft, k] = up(ft, k)
                        step(background, 6)
                        if (ft, k) == (0, 0):
                            continue
                        if k == 1:
                            low(ft, 0, t0[ft, 0], None)
                            if ft > 0:
                                tg = low(ft - 1, 1, t0[ft - 1, 1], t0[ft - 1, 0])
                    tg = low(FT - 1, 1, t0[FT - 1, 1], t0[FT - 1, 0])
                    t = PE.here()
                    for ct in range(CT):
                        ta = V.do(lambda e: e.tensor_tensor(u2[:, ct, :], maskx[:, 0, ct, :], banks[4 + ct][:, :], ALU.mult),
                                  t, *m.freed("u2"))
                        tb = V.do(lambda e: e.tensor_tensor(u3[:, :], maskx[:, 1, ct, :], banks[6 + ct][:, :], ALU.mult), ta)
                        ta = V.do(lambda e: e.tensor_tensor(u2[:, ct, :], u2[:, ct, :], u3[:, :], ALU.add), ta, tb)
                    for b in range(4, 8):
                        m.release(f"bank{b}", ta)
                    for ct in range(CT):
                        cs = slice(ct * P, (ct + 1) * P)
                        t = mm(banks[4 + ct][:, :], [(w2[:, ft, cs], ys[:, ft, :]) for ft in range(FT)] +
                               [(b2w[:, c, cs], u2[:, c, :]) for c in range(CT)], tg, ta)
                        o = XT[:, ct, half(h)]
                        t4 = V.do(lambda e: e.tensor_tensor(o, o, banks[4 + ct][:, :], ALU.add), t)
                        m.release(f"bank{4 + ct}", t4)
                    m.release("u2", t)
                    m.release("ys", t)
                    for name in ("maskx", "rwb", "am"):
                        m.release(name, V.here(), PE.here())
                    for _ in background:
                        pass

    staging = Phase()
    staged = {}

    def grouped_attention():
        staged["w1"] = staging("q_w1", [P, 11, C])
        staged["w2"] = staging("q_w2", [P, CT, 704])

        def prefetch():
            staged["t1"] = load(ctr("q"), staged["w1"][:, :, :], d["q_w1"])
            staged["t2"] = load(ctr("qw2"), staged["w2"][:, :, :], d["q_w2"])
        D, KV, R = 128, 4, 4
        SC = float(D) ** -0.5
        with Phase() as buf:
            wqk = buf("g_wqk", [P, CT, (R + 1) * D])
            wgv = buf("g_wgv", [P, CT, (R + 1) * D])
            wo = buf("g_wo", [P, R, C])
            rc = buf("g_rc", [P, T])
            rsn = buf("g_rsn", [P, T])
            rot = buf("g_rot", [P, P])
            msk = buf("g_msk", [P, P + T])
            load(ctr("g"), rc[:, :], d["rope_cos"])
            load(ctr("g"), rsn[:, :], d["rope_sin"])
            load(ctr("g"), rot[:, :], d["rope_rot"])
            t_msk = load(ctr("g"), msk[:, :], d["causal"])
            ready = condition(4)
            q = buf("g_q", [P, R + 1, TOK])
            v = buf("g_v", [P, TT, D])
            th = buf("g_th", [P, R, TOK])
            rs = buf("g_rs", [P, R + 1, TOK])
            sq = [buf(f"g_sq{i}", [P, HALF]) for i in range(2)]
            mean = buf("g_mean", [P, CT * (R + 1)])
            euk2 = [buf(f"g_euk{i}", [P, CT, TOK]) for i in range(2)]
            wkv_start(6, euk2[0])
            wkv_start(7, euk2[1])
            NP = 5
            pp = [buf(f"g_p{i}", [P, 384]) for i in range(NP)]
            pt = [buf(f"g_pt{i}", [P, 384]) for i in range(2)]
            st = buf("g_st", [P, 3, 8])
            gate = buf("g_gate", [P, 2])
            m.fence(sp=False)
            for lane in (PE, V, G, A):
                lane.wait(t_msk)

            def body(g):
                t_qk = load(ctr("gqk"), wqk[:, :, :], lambda: d["g_qk"][g], *m.freed("wqk"))
                t_gv = load(ctr("ggv"), wgv[:, :, :], lambda: d["g_gv"][g], *m.freed("wgv"))
                t_wo = load(ctr("gwo"), wo[:, :, :], lambda: d["g_wo"][g], *m.freed("wo"))
                background = wkv_units([(6, i_, euk2[0]) for i_ in (g * 2, g * 2 + 1)] + [(7, i_, euk2[1]) for i_ in (g * 2, g * 2 + 1)])
                heads = wqk[:, :, :].rearrange("p c (h d) -> p (c h) d", d=D)
                t = V.do(lambda e: e.reduce_sum(mean[:, :], heads, AX), t_qk)
                t = V.do(lambda e: e.tensor_scalar(mean[:, :], mean[:, :], 1.0 / D, None, ALU.mult), t)
                t_c = V.do(lambda e: e.tensor_tensor(heads, heads, mean[:, :].unsqueeze(2).to_broadcast([P, CT * (R + 1), D]),
                                                     ALU.subtract), t)
                jobs = [(hd, h) for hd in [R] + list(range(R)) for h in range(NH)]
                t_ln = {}

                def squares(n, t):
                    (hd, h), b, s_ = jobs[n], n % 2, sq[n % 2]
                    t = mm(banks[2 + b][:, :], [(ones[:, :], s_[:, :])], t, *m.freed(f"set{2 + b}"))
                    m.release(f"sq{b}", t)
                    t_ln[hd, h] = A.do(lambda e: e.activation(rs[:, hd, half(h)], banks[2 + b][:, :], ACT.Ln, scale=1.0 / D,
                                                              bias=eps_col(1e-6)), t, *m.freed("rs"))
                    m.release(f"set{2 + b}", t_ln[hd, h])

                pend = None
                for n, (hd, h) in enumerate(jobs):
                    b = n % 2
                    o, s_ = q[:, hd, half(h)], sq[n % 2]
                    t = mm(banks[b][:, :], [(wqk[:, k, hd * D:(hd + 1) * D], XC[:, k, half(h)]) for k in range(CT)], t_c,
                           *m.freed(f"set{b}"))
                    t = V.do(lambda e: e.tensor_copy(o, banks[b][:, :]), t, *m.freed("q"))
                    m.release(f"set{b}", t)
                    t = A.do(lambda e: e.activation(s_[:, :], o, ACT.Square), t, *m.freed(f"sq{b}"))
                    step(background, 4)
                    if pend:
                        squares(*pend)
                    pend = (n, t)
                m.release("wqk", PE.here())
                squares(*pend)
                t_rs = {}
                for hd in [R] + list(range(R)):
                    t = A.do(lambda e: e.activation(rs[:, hd, :], rs[:, hd, :], ACT.Exp, scale=-0.5), t_ln[hd, 0], t_ln[hd, 1])
                    t_rs[hd, 0] = t_rs[hd, 1] = t
                q_ready = {}
                b2t = lambda a: a.rearrange("p (b t) -> p b t", b=2)
                table = lambda a: a[:, :].unsqueeze(1).to_broadcast([P, 2, T])

                def turned(n, t, tg):
                    (hd, h), b = jobs[n], 4 + n % 2
                    o, r_ = q[:, hd, half(h)], rs[:, hd, half(h)]
                    t = V.do(lambda e: e.tensor_tensor(b2t(r_), b2t(banks[b][:, :]), table(rsn), ALU.mult), t, tg)
                    m.release(f"set{b}", t)
                    q_ready[hd, h] = V.do(lambda e: e.tensor_tensor(o, o, r_, ALU.add), t)

                pend = None
                for n, (hd, h) in enumerate(jobs):
                    if n < R * NH:
                        hg, b = n // NH, n % 2
                        t = mm(banks[b][:, :], [(wgv[:, k, hg * D:(hg + 1) * D], XC[:, k, half(h)]) for k in range(CT)], t_gv,
                               *m.freed(f"set{b}"))
                        t_th = A.do(lambda e: e.activation(th[:, hg, half(h)], banks[b][:, :], ACT.Tanh, scale=0.5), t, *m.freed("th"))
                        m.release(f"set{b}", t_th)
                        tt, b = n, 6 + n % 2
                        t = mm(banks[b][:, 0:D], [(XC[:, k, tt * P:(tt + 1) * P], wgv[:, k, R * D:(R + 1) * D]) for k in range(CT)],
                               *m.freed(f"set{b}"))
                        t_v = A.do(lambda e: e.copy(v[:, tt, :], banks[b][:, 0:D]), t, *m.freed("v"))
                        m.release(f"set{b}", t_v)
                    b = 4 + n % 2
                    wn, bn = ("g_kn_w", "g_kn_b") if hd == R else ("g_qn_w", "g_qn_b")
                    o, r_ = q[:, hd, half(h)], rs[:, hd, half(h)]
                    t = V.do(lambda e: e.tensor_tensor(o, o, r_, ALU.mult), t_rs[hd, h])
                    t = V.do(lambda e: e.tensor_scalar(r_, o, vcol(wn), vcol(bn), ALU.mult, ALU.add), t)
                    tg = G.do(lambda e: e.tensor_tensor(b2t(o), b2t(r_), table(rc), ALU.mult), t)
                    t = mm(banks[b][:, :], [(rot[:, :], r_)], t, *m.freed(f"set{b}"))
                    if pend:
                        turned(*pend)
                    pend = (n, t, tg)
                turned(*pend)
                m.release("rs", q_ready[hd, h])
                m.release("wgv", PE.here())
                for b in range(8):
                    m.release(f"bank{b}", *m.freed(f"set{b}"))
                units = [(b, hd) for b in range(NB) for hd in range(R)]

                def scores(n):
                    b, hd = units[n]
                    t0 = b * T
                    bk, s, c = n % 3, pp[n % NP], 2 * (n % 4)
                    kk = q[:, R, t0:t0 + T]
                    rdy = (q_ready[hd, b // 2], q_ready[R, b // 2])
                    PE.quiet(lambda e: e.matmul(banks[bk][:, 0:P], q[:, hd, t0:t0 + P], kk[:, 0:P], start=True, stop=True,
                                                skip_group_check=True), *rdy, *m.freed(f"bank{bk}"))
                    t = PE.do(lambda e: e.matmul(banks[bk][:, P:P + T], q[:, hd, t0 + P:t0 + T], kk, start=False, stop=True,
                                                 skip_group_check=True))
                    V.do(lambda e: e.memset(gate[:, n % 2:n % 2 + 1], 0.0), t, *m.freed(f"p{n % NP}"))
                    for i, cols in enumerate((slice(0, P), slice(P, P + T))):
                        t = V.do(lambda e: e.tensor_tensor_reduce(s[:, cols], banks[bk][:, cols], msk[:, cols], 1.0, -BIG,
                                                                  ALU.add, ALU.max, st[:, 0, c + i:c + i + 1]))
                    m.release(f"bank{bk}", t)
                    t = V.do(lambda e: e.tensor_scalar(st[:, 0, c:c + 2], st[:, 0, c:c + 2], -SC, None, ALU.mult), t)
                    for i, cols in enumerate((slice(0, P), slice(P, P + T))):
                        ta = A.do(lambda e: e.activation(s[:, cols], s[:, cols], ACT.Exp, bias=st[:, 0, c + i:c + i + 1], scale=SC,
                                                         accum_out=st[:, 1, c + i:c + i + 1]), t)
                    return ta

                def normalise(n, ta):
                    c, s = 2 * (n % 4), pp[n % NP]
                    t = V.do(lambda e: e.reciprocal(st[:, 2, c:c + 2], st[:, 1, c:c + 2]), ta)
                    for i, cols in enumerate((slice(0, P), slice(P, P + T))):
                        t1 = V.do(lambda e: e.tensor_scalar(s[:, cols], s[:, cols], st[:, 2, c + i:c + i + 1], None, ALU.mult), t)
                    return t1

                def turn(n, t1):
                    s, p_, bk = pp[n % NP], pt[n % 2], 3 + n % 2
                    for i in range(3):
                        t = (PE.do if i == 2 else PE.quiet)(
                            lambda e: e.transpose(banks[bk][:, i * P:(i + 1) * P], s[:, i * P:(i + 1) * P], ident[:, :]), t1,
                            *m.freed(f"bank{bk}"))
                    m.release(f"p{n % NP}", t)
                    t = A.do(lambda e: e.copy(p_[:, :], banks[bk][:, 0:384]), t, *m.freed(f"pt{n % 2}"))
                    m.release(f"bank{bk}", t)
                    return t

                def mix(n, t):
                    b, hd = units[n]
                    p_, bk = pt[n % 2], 5 + n % 3
                    v0, v1 = v[:, 2 * b, :], v[:, 2 * b + 1, :]
                    PE.quiet(lambda e: e.matmul(banks[bk][:, 0:P], v0, p_[:, 0:P], start=True, stop=True, skip_group_check=True),
                             t, t_v, *m.freed(f"bank{bk}"))
                    PE.quiet(lambda e: e.matmul(banks[bk][:, P:T], v0, p_[:, P:2 * P], start=False, stop=False, skip_group_check=True))
                    t = PE.do(lambda e: e.matmul(banks[bk][:, P:T], v1, p_[:, 2 * P:3 * P], start=False, stop=True, skip_group_check=True))
                    m.release(f"pt{n % 2}", t)
                    return t

                def gated(n, t):
                    b, hd = units[n]
                    bk = 5 + n % 3
                    o = th[:, hd, b * T:(b + 1) * T]
                    t = V.do(lambda e: e.scalar_tensor_tensor(o, o, 1.0, banks[bk][:, 0:T], ALU.add, ALU.mult), t, t_th)
                    m.release(f"bank{bk}", t)
                    return t

                exps, norms, turns, mixes = {}, {}, {}, {}
                last = len(units)
                for n in range(last + 5):
                    if 0 <= n - 2 < last:
                        norms[n - 2] = normalise(n - 2, exps[n - 2])
                    if 0 <= n - 3 < last:
                        turns[n - 3] = turn(n - 3, norms[n - 3])
                    if 0 <= n - 5 < last:
                        t = gated(n - 5, mixes[n - 5])
                    if n < last:
                        exps[n] = scores(n)
                        step(background, 2)
                    if 0 <= n - 4 < last:
                        mixes[n - 4] = mix(n - 4, turns[n - 4])
                m.release("q", PE.here())
                m.release("v", PE.here())
                for _ in background:
                    pass
                for ct in range(CT):
                    for h in range(NH):
                        b = ct * NH + h
                        t2 = mm(banks[b][:, :], [(wo[:, hd, ct * P:(ct + 1) * P], th[:, hd, half(h)]) for hd in range(R)],
                                t, t_wo, *m.freed(f"bank{b}"))
                        o = XT[:, ct, half(h)]
                        t3 = V.do(lambda e: e.scalar_tensor_tensor(o, banks[b][:, :], 0.5, o, ALU.mult, ALU.add), t2)
                        m.release(f"bank{b}", t3)
                m.release("wo", t2)
                m.release("th", t2)
                for b in range(8):
                    m.release(f"set{b}", *m.freed(f"bank{b}"))

            m.run_loop(KV, body, prefetch)

    def quantised_ffn():
        I = 704
        OT = 2 * I // P
        IT = 6
        CH = [(0, 512), (512, 192)]
        with Phase() as buf:
            w1t = buf("q_w1t", [P, CT, 2 * I], BF16)
            w2t = buf("q_w2t", [P, IT, C], BF16)
            s1b = buf("q_s1b", [P, 2 * I])
            s2b = buf("q_s2b", [P, C])
            st = buf("q_st", [P, 4, 16])

            def quantise(src, dst, tmp, c, t, *more):
                t = V.do(lambda e: e.tensor_reduce(st[:, 0, c:c + 1], src, AX, ALU.max, apply_absolute_value=True), t)
                t = V.do(lambda e: e.tensor_scalar(st[:, 0, c:c + 1], st[:, 0, c:c + 1], 1.0 / 127.0, 1e-8, ALU.mult, ALU.max), t)
                t = V.do(lambda e: e.reciprocal(st[:, 1, c:c + 1], st[:, 0, c:c + 1]), t)
                t = V.do(lambda e: e.tensor_scalar(tmp, src, st[:, 1, c:c + 1], ROUND, ALU.mult, ALU.add), t)
                t = V.do(lambda e: e.tensor_scalar(tmp, tmp, -ROUND, 127.0, ALU.add, ALU.min), t)
                return V.do(lambda e: e.tensor_scalar(dst, tmp, -127.0, None, ALU.max), t, *more)

            with Phase() as b2:
                w1, w2, t_w1, t_w2 = staged["w1"], staged["w2"], staged["t1"], staged["t2"]
                wb = [b2(f"q_wb{i}", [P, I], BF16) for i in range(2)]
                tmp = b2("q_tmp", [P, I])
                diag = b2("q_diag", [P, P])
                pb = [banks[6][:, :].bitcast(BF16), banks[7][:, :].bitcast(BF16)]
                n = 0
                for o in range(OT + CT):
                    first = o < OT
                    src = w1[:, o, :] if first else w2[:, o - OT, :]
                    ncol = C if first else I
                    i = n % 2
                    t = quantise(src, wb[i][:, 0:ncol], tmp[:, 0:ncol], o, t_w1 if first else t_w2, *m.freed(f"wb{i}"))
                    td = V.do(lambda e: e.tensor_scalar(diag[:, :], ident[:, :], st[:, 0, o:o + 1], None, ALU.mult), t, *m.freed("diag"))
                    t2 = mm(banks[0][:, 0:P], [(ones[:, :], diag[:, :])], td, *m.freed("bank0"))
                    m.release("diag", t2)
                    ds = s1b[:, o * P:(o + 1) * P] if first else s2b[:, (o - OT) * P:(o - OT + 1) * P]
                    t2 = A.do(lambda e: e.copy(ds, banks[0][:, 0:P]), t2)
                    m.release("bank0", t2)
                    blocks = [(c, min(P, ncol - c * P)) for c in range((ncol + P - 1) // P)]
                    for c, w_ in blocks:
                        t3 = PE.do(lambda e: e.transpose(pb[i][0:w_, c * P:(c + 1) * P], wb[i][:, c * P:c * P + w_], identb[:, :]),
                                   t, *m.freed(f"pb{i}"))
                    m.release(f"wb{i}", t3)
                    for c, w_ in blocks:
                        dt = w1t[:, c, o * P:(o + 1) * P] if first else w2t[0:w_, c, (o - OT) * P:(o - OT + 1) * P]
                        t4 = A.do(lambda e: e.copy(dt, pb[i][0:w_, c * P:(c + 1) * P]), t3)
                    m.release(f"pb{i}", t4)
                    n += 1
            ready = condition(5)
            with Phase() as b2:
                xt = [b2(f"q_x{i}", [P, C]) for i in range(2)]
                xb = [b2(f"q_xb{i}", [P, C], BF16) for i in range(2)]
                xqt = [b2(f"q_xqt{i}", [P, CT, P], BF16) for i in range(2)]
                tmp = [b2(f"q_t{i}", [P, I]) for i in range(2)]
                g = [b2(f"q_g{i}", [P, 2 * I]) for i in range(2)]
                hb = [b2(f"q_hb{i}", [P, I], BF16) for i in range(2)]
                hqt = [b2(f"q_hqt{i}", [P, IT, P], BF16) for i in range(2)]
                ob = [b2(f"q_ob{i}", [P, C]) for i in range(2)]
                pb = [banks[5][:, :].bitcast(BF16), banks[6][:, :].bitcast(BF16)]
                chunks = [(0, 512), (512, 512), (1024, 2 * I - 1024)]

                def rows(tt, _):
                    i = tt % 2
                    for ct in range(CT):
                        t = PE.do(lambda e: e.transpose(banks[4][:, ct * P:(ct + 1) * P], XC[:, ct, tt * P:(tt + 1) * P], ident[:, :]),
                                  *ready, *m.freed("bank4"))
                    t = A.do(lambda e: e.copy(xt[i][:, :], banks[4][:, 0:C]), t, *m.freed(f"xt{i}"))
                    m.release("bank4", t)
                    return t

                def quantise_rows(tt, t):
                    i = tt % 2
                    t = quantise(xt[i][:, :], xb[i][:, :], xt[i][:, :], tt % 4, t, *m.freed(f"xb{i}"))
                    m.release(f"xt{i}", t)
                    return t

                def gate_up(tt, t):
                    i, toks = tt % 2, []
                    for ct in range(CT):
                        t = PE.do(lambda e: e.transpose(pb[0][:, ct * P:(ct + 1) * P], xb[i][:, ct * P:(ct + 1) * P], identb[:, :]),
                                  t, *m.freed("pb0"))
                    m.release(f"xb{i}", t)
                    t = A.do(lambda e: e.copy(xqt[i][:, :, :].rearrange("p c t -> p (c t)"), pb[0][:, 0:C]), t, *m.freed(f"xqt{i}"))
                    m.release("pb0", t)
                    for b, (c_, w_) in enumerate(chunks):
                        toks.append(mm(banks[b][:, 0:w_], [(xqt[i][:, k, :], w1t[:, k, c_:c_ + w_]) for k in range(CT)],
                                       t, *m.freed(f"bank{b}")))
                    m.release(f"xqt{i}", toks[-1])
                    return toks

                def rescale(tt, toks):
                    i = tt % 2
                    for b, (c_, w_) in enumerate(chunks):
                        t = V.do(lambda e: e.scalar_tensor_tensor(g[i][:, c_:c_ + w_], banks[b][:, 0:w_], st[:, 0, tt % 4:tt % 4 + 1],
                                                                  s1b[:, c_:c_ + w_], ALU.mult, ALU.mult), toks[b], *m.freed(f"g{i}"))
                        m.release(f"bank{b}", t)
                        if c_ < I <= c_ + w_:
                            ta = A.do(lambda e: e.activation(tmp[i][:, :], g[i][:, 0:I], ACT.Silu), t, *m.freed(f"tmp{i}"))
                    return ta, t

                def quantise_hidden(tt, toks):
                    i = tt % 2
                    t = V.do(lambda e: e.tensor_tensor(tmp[i][:, :], tmp[i][:, :], g[i][:, I:2 * I], ALU.mult), *toks)
                    m.release(f"g{i}", t)
                    t = quantise(tmp[i][:, :], hb[i][:, :], tmp[i][:, :], 4 + tt % 4, t, *m.freed(f"hb{i}"))
                    m.release(f"tmp{i}", t)
                    return t

                def down(tt, t):
                    i = tt % 2
                    for c in range(IT):
                        w_ = min(P, I - c * P)
                        t2 = PE.do(lambda e: e.transpose(pb[1][0:w_, c * P:(c + 1) * P], hb[i][:, c * P:c * P + w_], identb[:, :]),
                                   t, *m.freed("pb1"))
                    m.release(f"hb{i}", t2)
                    A.do(lambda e: e.copy(hqt[i][:, 0:IT - 1, :].rearrange("p c t -> p (c t)"), pb[1][:, 0:(IT - 1) * P]), t2,
                         *m.freed(f"hqt{i}"))
                    t3 = A.do(lambda e: e.copy(hqt[i][0:64, IT - 1, :], pb[1][0:64, (IT - 1) * P:IT * P]), t2)
                    m.release("pb1", t3)
                    return t3

                def down_product(tt, t):
                    i = tt % 2
                    wd_ = [(hqt[i][0:min(P, I - c * P), c, :], w2t[0:min(P, I - c * P), c, :]) for c in range(IT)]
                    t = mm(banks[7][:, 0:C], wd_, t, *m.freed("bank7"))
                    m.release(f"hqt{i}", t)
                    t = V.do(lambda e: e.scalar_tensor_tensor(ob[i][:, :], banks[7][:, 0:C], st[:, 0, 4 + tt % 4:5 + tt % 4], s2b[:, :],
                                                              ALU.mult, ALU.mult), t, *m.freed(f"ob{i}"))
                    m.release("bank7", t)
                    return t

                def add(tt, t):
                    i = tt % 2
                    for ct in range(CT):
                        t4 = PE.do(lambda e: e.transpose(banks[3][:, ct * P:(ct + 1) * P], ob[i][:, ct * P:(ct + 1) * P],
                                                         ident[:, :]), t, *m.freed("bank3"))
                    m.release(f"ob{i}", t4)
                    o = XT[:, :, tt * P:(tt + 1) * P]
                    t4 = V.do(lambda e: e.tensor_tensor(o, o, banks[3][:, 0:C].rearrange("p (c t) -> p c t", c=CT), ALU.add), t4)
                    m.release("bank3", t4)

                order = [(add, 5), (quantise_rows, 1), (quantise_hidden, 3), (rows, 0), (gate_up, 2), (rescale, 2),
                         (down, 4), (down_product, 4)]
                state = {}
                for n in range(TT + 5):
                    for stage, behind in order:
                        tt = n - behind
                        if 0 <= tt < TT:
                            state[tt] = stage(tt, state.get(tt))
        staging.__exit__()

    def selective_scan():
        EI, N, ET = 512, 16, 4
        GN = 4
        HB = NB // 2
        NG = N // GN
        ready = condition(6)
        side.__exit__()
        with Phase() as buf:
            u = buf("s_u", [P, ET, TOK])
            dl = buf("s_dl", [P, ET, TOK])
            y = buf("s_y", [P, ET, TOK])
            wsk = buf("s_wsk", [P, CT, EI])
            wout = buf("s_wout", [P, ET, C])
            an = buf("s_an", [P, ET, N])
            bc3 = buf("s_bc3", [6 * N, TOK], BF16)
            pick3 = buf("s_pick3", [6 * N, 2 * N], BF16)
            xn = XC
            with Phase() as b2:
                sq = b2("s_sq", [P, CT, TOK])
                rs = b2("s_rs", [P, TOK])
                win = b2("s_win", [P, CT, EI])
                wd1 = b2("s_wd1", [P, ET, P])
                wd2 = b2("s_wd2", [P, 1, EI])
                wbc = b2("s_wbc", [P, ET, 2 * N])
                up = [b2(f"s_up{i}", [P, NB, T + 3]) for i in range(2)]
                r1 = b2("s_r1", [P, TOK])
                rest = [b2(f"s_rest{i}", [2 * N, HALF]) for i in range(2)]
                middle = [b2(f"s_middle{i}", [2 * N, HALF], BF16) for i in range(2)]
                t_in = load(ctr("s"), win[:, :, :], d["s_win"])
                load(ctr("s4"), wd1[:, :, :], d["s_wd1"])
                load(ctr("s4"), wd2[:, :, :], d["s_wd2"])
                load(ctr("s4"), an[:, :, :], d["s_alog"])
                t_w = load(ctr("s4"), wbc[:, :, :], d["s_wbc"])
                load(ctr("s3"), wsk[:, :, :], d["s_wskip"])
                t_wo = load(ctr("s3"), wout[:, :, :], d["s_wout"])
                t = inverse_root(XC, ready, sq, rs, 1e-5)
                rdy = scale_rows(XC, rs, "s_norm", xn, t)
                for i in range(2):
                    t_z = V.do(lambda e: e.memset(up[i][:, :, 0:3], 0.0))
                for k in range(3):
                    V.do(lambda e: e.tensor_copy(pick3[2 * N * k:2 * N * (k + 1), :], ident[0:2 * N, 0:2 * N]))
                convs = []
                for et in range(ET):
                    i = et % 2
                    for h in range(NH):
                        b = (2 * et + h) % 4
                        t = mm(banks[b][:, :], [(win[:, k, et * P:(et + 1) * P], xn[:, k, half(h)]) for k in range(CT)],
                               *rdy, t_in, *m.freed(f"bank{b}"))
                        t = A.do(lambda e: e.copy(up[i][:, 2 * h:2 * h + 2, 3:T + 3],
                                                  banks[b][:, :].rearrange("p (b t) -> p b t", b=2)), t, t_z, *m.freed(f"up{i}"))
                        m.release(f"bank{b}", t)
                    uo = u[:, et, :].rearrange("p (b t) -> p b t", b=NB)
                    t = V.do(lambda e: e.tensor_scalar(uo, up[i][:, :, 0:T], vcol("s_conv", et * 4), vcol("s_conv_b", et),
                                                       ALU.mult, ALU.add), t)
                    for j in range(1, 4):
                        t = V.do(lambda e: e.scalar_tensor_tensor(uo, up[i][:, :, j:j + T], vcol("s_conv", et * 4 + j), uo,
                                                                  ALU.mult, ALU.add), t)
                    m.release(f"up{i}", t)
                    convs.append(t)
                    if et:
                        t_u = A.do(lambda e: e.activation(u[:, et - 1, :], u[:, et - 1, :], ACT.Silu), convs[et - 1])
                t_u = A.do(lambda e: e.activation(u[:, ET - 1, :], u[:, ET - 1, :], ACT.Silu), convs[ET - 1])
                for h in range(NH):
                    b = 4 + h
                    t = mm(banks[b][:, :], [(wd1[:, k, :], u[:, k, half(h)]) for k in range(ET)], t_u, t_w)
                    t_r = A.do(lambda e: e.copy(r1[:, half(h)], banks[b][:, :]), t)
                    t = mm(banks[b + 2][0:2 * N, :], [(wbc[:, k, :], u[:, k, half(h)]) for k in range(ET)])
                    part = lambda k: bc3[2 * N * k:2 * N * (k + 1), half(h)]
                    r_, m_ = rest[h][:, :], middle[h][:, :]
                    t0 = V.do(lambda e: e.tensor_copy(part(0), banks[b + 2][0:2 * N, :]), t)
                    t0 = V.do(lambda e: e.tensor_tensor(r_, banks[b + 2][0:2 * N, :], part(0), ALU.subtract), t0)
                    t0 = V.do(lambda e: e.tensor_copy(m_, r_), t0)
                    t1 = V.do(lambda e: e.tensor_tensor(r_, r_, m_, ALU.subtract), t0)
                    V.do(lambda e: e.tensor_copy(part(1), m_), t0)
                    V.do(lambda e: e.tensor_copy(part(2), r_), t1)
                for et in range(ET):
                    for h in range(NH):
                        b = (2 * et + h) % 4
                        t = mm(banks[b][:, :], [(wd2[:, 0, et * P:(et + 1) * P], r1[:, half(h)])], t_r, *m.freed(f"bank{b}"))
                        t_y = A.do(lambda e: e.activation(y[:, et, half(h)], banks[b][:, :], ACT.Abs, bias=vcol("s_bd2", et)), t)
                        t_dl = V.do(lambda e: e.tensor_scalar(dl[:, et, half(h)], banks[b][:, :], vcol("s_bd2", et), 0.0,
                                                              ALU.add, ALU.max), t_y)
                        m.release(f"bank{b}", t_dl)
                t = A.do(lambda e: e.activation(y[:, :, :], y[:, :, :], ACT.Exp, scale=-1.0), t_y)
                t_an = A.do(lambda e: e.activation(an[:, :, :], an[:, :, :], ACT.Exp))
                V.do(lambda e: e.tensor_scalar(an[:, :, :], an[:, :, :], -1.0, None, ALU.mult), t_an)
                for h in range(NH):
                    t2 = A.do(lambda e: e.activation(y[:, :, half(h)], y[:, :, half(h)], ACT.Ln, bias=eps_col(1.0)), t)
                    V.do(lambda e: e.tensor_tensor(dl[:, :, half(h)], dl[:, :, half(h)], y[:, :, half(h)], ALU.add), t2, t_dl)
            with Phase() as b2:
                NBU, NDA = 4, 3
                rep = [[b2(f"s_rep{kind}{i}", [P, GN, HALF]) for i in range(2)] for kind in range(2)]
                du = b2("s_du", [P, ET, HALF])
                da = [b2(f"s_da{i}", [P, GN, HALF]) for i in range(NDA)]
                bu = [b2(f"s_bu{i}", [P, GN, HALF]) for i in range(NBU)]
                groups = [(h, gn) for h in range(NH) for gn in range(NG)]

                def replicate(kind, j, n):
                    if j >= len(groups):
                        return
                    h, gn = groups[j]
                    row, b = kind * N + gn * GN + n, 2 * kind + n % 2
                    t = mm(banks[b][:, :], [(pick3[:, row:row + 1].to_broadcast([6 * N, P]), bc3[:, half(h)])],
                           *m.freed(f"bank{b}"))
                    t = A.do(lambda e: e.copy(rep[kind][j % 2][:, n, :], banks[b][:, :]), t, *m.freed(f"rep{kind}{j % 2}"))
                    m.release(f"bank{b}", t)
                    t_rep[kind, j] = t

                fl = lambda a: a[:, :, :].rearrange("p n t -> p (n t)")
                jobs = [(j, et) for j in range(len(groups)) for et in range(ET)]
                t_rep, t_da, t_bu, t_sum, t_du = {}, {}, {}, {}, None
                for kind in range(2):
                    for n in range(GN):
                        replicate(kind, 0, n)

                def inputs(k):
                    nonlocal t_du
                    j, et = jobs[k]
                    h, gn = groups[j]
                    a_, b_ = da[k % NDA], bu[k % NBU]
                    if et == 0 and gn == 0:
                        t_du = V.do(lambda e: e.tensor_tensor(du[:, :, :], dl[:, :, half(h)], u[:, :, half(h)], ALU.mult),
                                    *m.freed("du"))
                    for n in range(GN):
                        t_da[k] = A.do(lambda e: e.activation(a_[:, n, :], dl[:, et, half(h)], ACT.Exp,
                                                              scale=an[:, et, gn * GN + n:gn * GN + n + 1]), *m.freed(f"da{k % NDA}"))
                    t_bu[k] = G.do(lambda e: e.tensor_tensor(b_[:, :, :], rep[0][j % 2][:, :, :],
                                                             du[:, et, :].unsqueeze(1).to_broadcast([P, GN, HALF]), ALU.mult),
                                   t_du, t_rep[0, j], *m.freed(f"bu{k % NBU}"))
                    m.release("du", t_bu[k])
                    m.release(f"rep0{j % 2}", t_bu[k])
                    replicate(0, j + 1, et)

                def states(k):
                    j, et = jobs[k]
                    h, gn = groups[j]
                    a_, b_, bk = da[k % NDA], bu[k % NBU], 4 + et
                    dz = a_[:, :, :].rearrange("p n (b t) -> p (n b) t", b=HB)[:, :, 0:1]
                    t = V.do(lambda e: e.memset(dz, 0.0), t_da[k])
                    t = V.do(lambda e: e.tensor_tensor_scan(fl(b_), fl(a_), fl(b_), 0.0, ALU.mult, ALU.add), t, t_bu[k])
                    m.release(f"da{k % NDA}", t)
                    t = V.do(lambda e: e.tensor_tensor(b_[:, :, :], b_[:, :, :], rep[1][j % 2][:, :, :], ALU.mult), t, t_rep[1, j])
                    m.release(f"rep1{j % 2}", t)
                    replicate(1, j + 1, et)
                    for n in range(GN):
                        f = lambda e: e.matmul(banks[bk][:, :], ident[:, :], b_[:, n, :], start=(gn == 0 and n == 0),
                                               stop=(gn == NG - 1 and n == GN - 1), skip_group_check=True)
                        tp = (PE.do if n == GN - 1 else PE.quiet)(f, t, *m.freed(f"bank{bk}"))
                    m.release(f"bu{k % NBU}", tp)
                    t_sum[h, et] = tp
                    if gn == NG - 1 and et == ET - 1:
                        for et in range(ET):
                            t = V.do(lambda e: e.scalar_tensor_tensor(y[:, et, half(h)], u[:, et, half(h)], vcol("s_wd", et),
                                                                      banks[4 + et][:, :], ALU.mult, ALU.add), t_sum[h, et])
                            m.release(f"bank{4 + et}", t)

                for k in range(len(jobs) + 2):
                    if k < len(jobs):
                        inputs(k)
                    if k >= 2:
                        states(k - 2)
            with Phase() as b2:
                sk = [b2(f"s_sk{i}", [P, HALF]) for i in range(2)]
                n = 0
                for et in range(ET):
                    for h in range(NH):
                        i, b = n % 2, n % 4
                        n += 1
                        t = mm(banks[b][:, :], [(wsk[:, k, et * P:(et + 1) * P], xn[:, k, half(h)]) for k in range(CT)],
                               t_wo, *m.freed(f"bank{b}"))
                        t = A.do(lambda e: e.activation(sk[i][:, :], banks[b][:, :], ACT.Silu), t, *m.freed(f"sk{i}"))
                        m.release(f"bank{b}", t)
                        o = y[:, et, half(h)]
                        t = V.do(lambda e: e.tensor_tensor(o, o, sk[i][:, :], ALU.mult), t)
                        m.release(f"sk{i}", t)
                project_residual(wout, ET, y, [t], bank0=4)

    def moe_top4():
        E, I, K = 16, 176, 4
        UT = E * I // P
        PER = 2
        SI = 2 * I
        with Phase() as buf:
            wr = buf("e_wr", [P, CT, 2 * E])
            srow = buf("e_row", [P, 2, E])
            revi = buf("e_revi", [P, TT, E])
            sg = buf("e_sg", [P, CT, 2 * SI])
            sd = buf("e_sd", [P, 3, C])
            load(ctr("e"), wr[:, :, :], d["e_router"])
            load(ctr("e"), srow[:, :, :], d["e_extra"].partition_broadcast(P))
            load(ctr("e"), sg[:, :, :], d["e_shared_gu"])
            load(ctr("e"), sd[:, :, :], d["e_shared_down"])
            t_w = load(ctr("e"), revi[:, :, :], d["revi16"])
            ready = condition(7)
            rows = buf("e_rows", [E, TOK])
            rows3 = buf("e_rows3", [96, TOK], BF16)
            t_r0 = G.do(lambda e: e.memset(rows3[:, :], 0.0))
            with Phase() as b2:
                lg = b2("e_lg", [P, TT, 2 * E])
                pr = b2("e_pr", [P, TT, E])
                bi = b2("e_bi", [P, TT, E])
                hot = b2("e_hot", [P, TT, E])
                tk = b2("e_tk", [P, TT, E])
                tmp = b2("e_tmp", [P, 2, TT, 16])
                st = b2("e_st", [P, TT])

                def bc(a):
                    return a.unsqueeze(2).to_broadcast([P, TT, E])

                def rowb(n):
                    return srow[:, n, :].unsqueeze(1).to_broadcast([P, TT, E])
                t = token_logits(wr, 2 * E, ready + [t_w])
                t = V.do(lambda e: e.tensor_copy(lg[:, :, :].rearrange("p t e -> p (t e)"), banks[0][:, 0:TT * 2 * E]), t)
                m.release("bank0", t)
                t = A.do(lambda e: e.activation(pr[:, :, :], lg[:, :, 0:E], ACT.Silu), t)
                t = V.do(lambda e: e.tensor_tensor(pr[:, :, :], pr[:, :, :], lg[:, :, E:2 * E], ALU.mult), t)
                t = A.do(lambda e: e.activation(pr[:, :, :], pr[:, :, :], ACT.Abs), t)
                t = V.do(lambda e: e.tensor_reduce(st[:, :], pr[:, :, :], AX, ALU.max), t)
                t = V.do(lambda e: e.tensor_tensor(pr[:, :, :], pr[:, :, :], bc(st[:, :]), ALU.subtract), t)
                t = A.do(lambda e: e.activation(pr[:, :, :], pr[:, :, :], ACT.Exp), t)
                t = V.do(lambda e: e.tensor_reduce(st[:, :], pr[:, :, :], AX, ALU.add), t)
                t = V.do(lambda e: e.reciprocal(st[:, :], st[:, :]), t)
                t = V.do(lambda e: e.tensor_tensor(pr[:, :, :], pr[:, :, :], bc(st[:, :]), ALU.mult), t)
                t = V.do(lambda e: e.tensor_tensor(bi[:, :, :], pr[:, :, :], rowb(1), ALU.add), t)
                t = pick_top(bi[:, :, :], None, tk[:, :, :], revi[:, :, :], tmp, E, t)
                for k in range(1, K):
                    t = pick_top(bi[:, :, :], tk[:, :, :], hot[:, :, :], revi[:, :, :], tmp, E, t)
                    t = V.do(lambda e: e.tensor_tensor(tk[:, :, :], tk[:, :, :], hot[:, :, :], ALU.add), t)
                t = V.do(lambda e: e.tensor_tensor(pr[:, :, :], pr[:, :, :], rowb(0), ALU.mult), t)
                t = V.do(lambda e: e.scalar_tensor_tensor(pr[:, :, :], pr[:, :, :], 1.0, tk[:, :, :], ALU.add, ALU.mult), t)
                t = rows_from_tokens(pr, E, rows, t)
                middle = b2("e_middle", [E, TOK], BF16)
                r_ = rows[:, :]
                t = V.do(lambda e: e.tensor_copy(rows3[0:E, :], r_), t, t_r0)
                t = V.do(lambda e: e.tensor_tensor(r_, r_, rows3[0:E, :], ALU.subtract), t)
                t = V.do(lambda e: e.tensor_copy(middle[:, :], r_), t)
                V.do(lambda e: e.tensor_copy(rows3[32:32 + E, :], middle[:, :]), t)
                t = V.do(lambda e: e.tensor_tensor(r_, r_, middle[:, :], ALU.subtract), t)
                V.do(lambda e: e.tensor_copy(rows3[64:64 + E, :], r_), t)
            wgu = [buf(f"e_wgu{j}", [P, CT, 2, P]) for j in range(PER)]
            wd = [buf(f"e_wd{j}", [P, C]) for j in range(PER)]
            wsp = [tuple(buf(f"e_wsp{j}{i}", [P, CT, 2, P], F32R) for i in range(2)) for j in range(PER)]
            xs = tuple(buf(f"e_xs{i}", [P, CT, TOK], F32R) for i in range(2))
            split(XC[:, :, :], xs[0][:, :, :], xs[1][:, :, :], *ready)
            sel = [buf(f"e_sel{j}", [96, P]) for j in range(PER)]
            selb = [buf(f"e_selb{j}", [96, P], BF16) for j in range(PER)]
            cf = [[buf(f"e_cf{j}{h}", [P, HALF]) for h in range(NH)] for j in range(PER)]
            sbuf = [buf(f"e_s{i}", [P, HALF]) for i in range(4)]
            hbuf = [tuple(buf(f"e_h{i}{k}", [P, HALF], F32R) for k in range(2)) for i in range(4)]
            wdsp = [tuple(buf(f"e_wdsp{j}{k}", [P, C], F32R) for k in range(2)) for j in range(PER)]
            units = []
            for ft in range(3):
                rws = min(P, SI - ft * P)
                for h in range(NH):
                    units.append(dict(src=XC, wg=[sg[:, k, ft * P:ft * P + rws] for k in range(CT)],
                                      wu=[sg[:, k, SI + ft * P:SI + ft * P + rws] for k in range(CT)],
                                      wd=sd[:, ft, :], rows=rws, h=h, coef=None, first=ft == 0, last=False, waits=[t_w]))
            run_units(units, sbuf, hbuf)
            left = leave(wdsp[PER - 1], PER * NH, sbuf, hbuf)

            def body(i):
                toks, sels = [], []
                for j in range(PER):
                    t = load(ctr(f"es{j}"), sel[j][:, :], lambda: d["e_sel"][i, j], *m.freed(f"sel{j}"))
                    t = V.do(lambda e: e.tensor_copy(selb[j][:, :], sel[j][:, :]), t, *m.freed(f"selb{j}"))
                    m.release(f"sel{j}", t)
                    sels.append(t)
                    load(ctr(f"e{j}"), wgu[j][:, :, :, :], lambda: d["e_gu"][i, j], *m.freed(f"w{j}"))
                    toks.append(load(ctr(f"e{j}"), wd[j][:, :], lambda: d["e_down"][i, j], *m.freed(f"wd{j}")))
                units = []
                t_split, t_down = [[] for _ in range(PER)], [[] for _ in range(PER)]

                def split_weights(j):
                    hi, lo = wsp[j]
                    t = split(wgu[j][:, :, :, :], hi[:, :, :, :], lo[:, :, :, :], toks[j], *m.freed(f"wsp{j}"))
                    m.release(f"w{j}", t)
                    t_split[j].append(t)

                def split_down(j):
                    hi, lo = wdsp[j]
                    t = split(wd[j][:, :], hi[:, :], lo[:, :], toks[j], *((PE.here(),) if j == PER - 1 else m.freed(f"wdsp{j}")), lane=G)
                    m.release(f"wd{j}", t)
                    t_down[j].append(t)

                def start(ft):
                    if ft + 1 < PER:
                        split_weights(ft + 1)
                    split_down(ft)
                split_weights(0)
                for ft in range(PER):
                    for h in range(NH):
                        w_ = wsp[ft]
                        u = dict(src=xs, wg=[tuple(p[:, k, 0, :] for p in w_) for k in range(CT)],
                                 wu=[tuple(p[:, k, 1, :] for p in w_) for k in range(CT)], wd=wdsp[ft], rows=P, h=h,
                                 first=False, last=True, waits=t_split[ft], down_waits=t_down[ft],
                                 start=(lambda ft=ft: start(ft)) if h == 0 else None,
                                 downed=(lambda ft=ft: m.release(f"wdsp{ft}", PE.here())) if h == 1 else None,
                                 done=(lambda ft=ft: m.release(f"wsp{ft}", PE.here())) if h == 1 else None)

                        def before(ft=ft, h=h, u=u):
                            nn = ft * NH + h
                            b = 4 + 2 * (nn % 2)
                            t = mm(banks[b][:, :], [(selb[ft][:, :], rows3[:, half(h)])], sels[ft], *m.freed(f"pair{nn % 2}"))
                            if h == NH - 1:
                                m.release(f"selb{ft}", t)
                            t = A.do(lambda e: e.copy(cf[ft][h][:, :], banks[b][:, :]), t, *m.freed(f"cf{ft}{h}"))
                            u["coef"] = ((lambda: cf[ft][h][:, :]), t)
                            m.release(f"pair{nn % 2}", t)
                        u["before"] = before
                        u["after"] = lambda ft=ft, h=h: m.release(f"cf{ft}{h}", V.here())
                        units.append(u)
                run_units(units, sbuf, hbuf, left=left)

            m.run_loop(UT // PER, body)
            take_left(left)
            add_out_banks()

    stages = [linear_attention, moe_top1, banded_attention, lora_ffn, grouped_attention, quantised_ffn,
              selective_scan, moe_top4]
    for stage in stages:
        stage()
    m.fence()
    t = SP.issue(lambda e: e.dma_start(out, XT[:, :, :]), count=16, counter=ctr("out"))
    SP.wait(t)


def _constants(np):
    c = {}
    c["ident"] = np.eye(128, dtype=np.float32)
    dist = (np.arange(256)[None, :] - np.arange(128)[:, None]).astype(np.float32)
    c["dist"] = np.concatenate([dist, dist[:, 0:128]], 1)
    for n in (8, 16):
        c[f"revi{n}"] = np.broadcast_to((n - np.arange(n)).astype(np.float32), (128, 8, n)).copy()
    c["sel16"] = np.broadcast_to(np.eye(16, dtype=np.float32)[:, :, None], (16, 16, 128)).copy()
    i, j = np.arange(128)[:, None], np.arange(128)[None, :]
    own = (j <= i) & (j >= i - 31)
    prev = (np.arange(32)[None, :] - 32) >= i - 31
    mask = np.full((128, 2, 176), -1e30, np.float32)
    for t in range(2):
        mask[:, t, 0:128][own] = 0.0
        if t:
            mask[:, t, 128:160][prev] = 0.0
        mask[:, t, 160:176] = 0.0
    c["b_mask"] = mask
    diag = np.where(j <= i, 0.0, -1e30).astype(np.float32)
    c["causal"] = np.concatenate([diag, np.zeros((128, 128), np.float32), diag], 1)
    sel = np.zeros((18, 2, 128), np.float32)
    sel[16, 0], sel[17, 1] = 1.0, 1.0
    c["r_sel"] = sel
    selx = np.zeros((18, 2, 2, 128), np.float32)
    for k in range(2):
        for ct in range(2):
            for p in range(128):
                selx[8 * k + ct * 4 + p // 32, k, ct, p] = 1.0
    c["r_selx"] = selx
    inv = 1.0 / 1000000.0 ** (np.arange(0, 128, 2, dtype=np.float32) / 128)
    fr = np.outer(inv, np.arange(256, dtype=np.float32)).astype(np.float32)
    c["rope_cos"] = np.concatenate([np.cos(fr), np.cos(fr)], 0).astype(np.float32)
    c["rope_sin"] = np.concatenate([np.sin(fr), np.sin(fr)], 0).astype(np.float32)
    rot = np.zeros((128, 128), np.float32)
    for p in range(64):
        rot[p + 64, p], rot[p, p + 64] = -1.0, 1.0
    c["rope_rot"] = rot
    es = np.zeros((11, 2, 96, 128), np.float32)
    for f in range(16 * 176):
        for part in range(3):
            es[f // 256, (f // 128) % 2, 32 * part + f // 176, f % 128] = 1.0
    c["e_sel"] = es
    return c


def _layout(inputs, np):
    a = {k: np.asarray(v) for k, v in inputs.items()}

    def km(wt):
        k, o = wt.shape
        return np.ascontiguousarray(wt.reshape(k // 128, 128, o).transpose(1, 0, 2))

    def cols(v, n):
        return v.reshape(n, 128).T

    def acts(x):
        return km(x.transpose(2, 0, 1).reshape(256, 1024))
    r = dict(_constants(np))
    r["x"] = acts(a["x"])
    r["side"] = acts(a["fside_BxSxS_0"])
    r["cond"] = a["cond_512"]
    blocks = [f"L{l}_{c}" for l in range(4) for c in ("cond", "cond2")]

    def pad32(v):
        w = v.reshape(16, 16, *v.shape[1:])
        return np.concatenate([w, np.zeros_like(w)], 1).reshape(512, *v.shape[1:])
    vec = {"cond_w": np.concatenate([cols(a[f"{b}_w"], 2) for b in blocks], 1),
           "cond_u": np.concatenate([cols(a[f"{b}_u"], 2) for b in blocks], 1),
           "l0_qkv_norm": cols(a["L0_attn_qkv_norm_w"], 2), "l0_norm": cols(pad32(a["L0_attn_norm_w"]), 4),
           "l0_proj_norm": cols(pad32(a["L0_attn_proj_norm_w"]), 4),
           "b_ln_scale": cols(a["L1_attn_ln_scale"], 2), "b_ln_bias": cols(a["L1_attn_ln_bias"], 2),
           "s_norm": cols(a["L3_attn_norm_w"], 2), "s_bd2": cols(a["L3_attn_bd2"], 4), "s_wd": cols(a["L3_attn_W_D"], 4),
           "s_conv_b": cols(a["L3_attn_conv_b"], 4),
           "s_conv": a["L3_attn_conv_w"].reshape(4, 128, 4).transpose(1, 0, 2).reshape(128, 16)}
    order = np.concatenate([np.arange(0, 128, 2), np.arange(1, 128, 2)])
    for n, s in (("g_qn_w", "q_norm_w"), ("g_qn_b", "q_norm_b"), ("g_kn_w", "k_norm_w"), ("g_kn_b", "k_norm_b")):
        vec[n] = a["L2_attn_" + s][order][:, None]
    ofs, at = {}, 0
    for n, v in vec.items():
        ofs[n] = at
        at += v.shape[1]
    r["vecs"] = np.ascontiguousarray(np.concatenate(list(vec.values()), 1))

    def heads32(wt):
        return pad32(wt.T).T
    w = a["L0_attn_qkv_w"].T
    r["l0_qkv"] = km(np.concatenate([heads32(w[:, 0:256]), heads32(w[:, 256:512]), w[:, 512:768]], 1))
    r["l0_proj"] = km(pad32(a["L0_attn_proj_w"].T))
    r["l0_s"] = a["L0_attn_s"]
    r["m0_router"] = km(a["L0_ffn_router_w"].T)
    gu = a["L0_ffn_w_gate_up"].reshape(8, 2, 128, 2, 4, 128)
    r["m0_gu"] = np.ascontiguousarray(gu.transpose(0, 4, 2, 1, 3, 5))
    r["m0_down"] = np.ascontiguousarray(a["L0_ffn_w_down"].reshape(8, 4, 128, 256))
    r["m0_shared_gu"] = km(a["L0_ffn_shared_gate_up"])
    r["m0_shared_down"] = km(a["L0_ffn_shared_down"])
    for n, s in (("b_wq", "Wq"), ("b_wk", "Wk"), ("b_wv", "Wv"), ("b_wo", "Wo")):
        w = a["L1_attn_" + s].T
        r[n] = km(heads32(w) if s in ("Wq", "Wk") else pad32(w) if s == "Wo" else w)
    r["b_global"] = km(a["L1_attn_global_tokens"][0].T)
    r["r_router"] = km(a["L1_ffn_Wg"].T)
    r["r_w1"], r["r_w3"], r["r_w2"] = km(a["L1_ffn_W1"].T), km(a["L1_ffn_W3"].T), km(a["L1_ffn_W2"].T)
    r["r_a1"], r["r_a3"] = km(a["L1_ffn_A1"].reshape(256, 256).T), km(a["L1_ffn_A3"].reshape(256, 256).T)
    r["r_a2"] = km(a["L1_ffn_A2"].reshape(256, 896).T)
    for n, s in (("r_b1", "B1"), ("r_b3", "B3"), ("r_b2", "B2")):
        w = a["L1_ffn_" + s]
        r[n] = km(w.transpose(0, 2, 1).reshape(256, w.shape[1]))
    wqkv = a["L2_attn_w_qkv"]
    wq, wg, wk, wv = wqkv[0:2048], wqkv[2048:4096], wqkv[4096:4608], wqkv[4608:5120]
    wq, wk = wq.reshape(16, 128, 256)[:, order], wk.reshape(4, 128, 256)[:, order]
    wg, wv = wg.reshape(16, 128, 256), wv.reshape(4, 128, 256)
    r["g_qk"] = np.stack([km(np.concatenate([wq[4 * g:4 * g + 4].reshape(512, 256), wk[g]], 0).T) for g in range(4)])
    r["g_gv"] = np.stack([km(np.concatenate([wg[4 * g:4 * g + 4].reshape(512, 256), wv[g]], 0).T) for g in range(4)])
    r["g_wo"] = np.ascontiguousarray(a["L2_attn_w_o"].T.reshape(4, 4, 128, 256).transpose(0, 2, 1, 3))
    r["q_w1"] = km(a["L2_ffn_w_gate_up"])
    r["q_w2"] = km(a["L2_ffn_w_down"])
    r["s_win"], r["s_wskip"] = km(a["L3_attn_W_in"].T), km(a["L3_attn_W_skip"].T)
    r["s_wd1"], r["s_wd2"] = km(a["L3_attn_Wd1"].T), km(a["L3_attn_Wd2"].T)
    r["s_wbc"] = km(np.concatenate([a["L3_attn_WB"], a["L3_attn_WC"]], 0).T)
    r["s_alog"] = km(a["L3_attn_A_log"])
    r["s_wout"] = km(a["L3_attn_W_out"].T)
    r["e_router"] = km(np.concatenate([a["L3_ffn_rg_w"], a["L3_ffn_ru_w"]], 0).T)
    r["e_extra"] = np.stack([a["L3_ffn_extra_scale"], a["L3_ffn_extra_bias"]])
    eg = np.stack([a["L3_ffn_Wg"].reshape(2816, 256), a["L3_ffn_Wu"].reshape(2816, 256)])
    eg = eg.reshape(2, 11, 2, 128, 2, 128)
    r["e_gu"] = np.ascontiguousarray(eg.transpose(1, 2, 5, 4, 0, 3))
    r["e_down"] = np.ascontiguousarray(a["L3_ffn_Wd"].transpose(0, 2, 1).reshape(11, 2, 128, 256))
    r["e_shared_gu"] = km(np.concatenate([a["L3_ffn_Sg"], a["L3_ffn_Su"]], 0).T)
    sd = a["L3_ffn_Sd"].T
    r["e_shared_down"] = km(np.concatenate([sd, np.zeros((32, 256), np.float32)], 0))
    return r, ofs


def kernel(**inputs):
    import numpy as np
    import concourse.bacc as bacc
    from concourse.bass_utils import run_bass_kernel_spmd as run
    arrays, offsets = _layout(inputs, np)
    nc = bacc.Bacc("TRN2", target_bir_lowering=False, num_devices=1)
    arrays = {k: np.ascontiguousarray(v) for k, v in arrays.items()}
    d = {k: nc.dram_tensor("in_" + k, v.shape, mybir.dt.from_np(v.dtype), kind="ExternalInput").ap()
         for k, v in arrays.items()}
    d["vec_offsets"] = offsets
    out = nc.dram_tensor("out_x", [128, 2, 1024], F32, kind="ExternalOutput").ap()
    build_program(nc, d, out)
    r = run(nc, [{"in_" + k: v for k, v in arrays.items()}], core_ids=[0])
    y = np.asarray(r.results[0]["out_x"])
    return np.ascontiguousarray(y.transpose(2, 1, 0).reshape(4, 256, 256))
```
